# Optimizing a Trainium2 kernel written in Bass

```python
import numpy as np
import jax
import jax.numpy as jnp

def _softmax(x, axis=-1):
    return jax.nn.softmax(x, axis=axis)

def _gelu(x):
    return jax.nn.gelu(x, approximate=True)

def _silu(x):
    return jax.nn.silu(x)

def _sigmoid(x):
    return jax.nn.sigmoid(x)

def _layernorm(x, axis=-1, eps=1e-05):
    m = jnp.mean(x, axis=axis, keepdims=True)
    v = jnp.var(x, axis=axis, keepdims=True)
    return (x - m) / jnp.sqrt(v + eps)

def _scatter_add(tgt, idx, src, axis=0):
    return tgt.at[idx].add(src)

def _segment_sum(src, seg, n):
    return jax.ops.segment_sum(src, seg, n)
kernel_name = 'mk_audio_tower_d1_tok_audfeat1024_r4_e1e198'

def setup_inputs(seed: int=0):
    np.random.seed(seed)
    _w = jnp.asarray

    def _rec_inputs():
        import jax
        import jax.numpy as jnp
        _rk = jax.random.key(seed)
        x = -0.000123307 + 1.00004 * jax.random.normal(jax.random.fold_in(_rk, 1), (32, 80, 750), jnp.float32)
        return x
    x = _rec_inputs()

    def _L0_tok_setup():
        import jax, jax.numpy as jnp
        import numpy as np
        N_MELS = 80
        PATCH_FRAMES = 8
        HOP_FRAMES = 4
        D_MODEL = 256
        PATCH_DIM = N_MELS * PATCH_FRAMES

        def _patchify(mel):
            T = mel.shape[2]
            N = (T - PATCH_FRAMES) // HOP_FRAMES + 1
            idx = jnp.arange(N)[:, None] * HOP_FRAMES + jnp.arange(PATCH_FRAMES)[None, :]
            patches = mel[:, :, idx]
            patches = jnp.transpose(patches, (0, 2, 1, 3))
            return patches.reshape(patches.shape[0], N, PATCH_DIM)
        key = jax.random.key(seed)
        k1, k2, k3 = jax.random.split(key, 3)
        B, T = (32, 1024)
        mel = jax.random.normal(k1, (B, N_MELS, T), dtype=jnp.float32)
        bound = 1.0 / np.sqrt(PATCH_DIM)
        W = jax.random.uniform(k2, (PATCH_DIM, D_MODEL), dtype=jnp.float32, minval=-bound, maxval=bound)
        b = jax.random.uniform(k3, (D_MODEL,), dtype=jnp.float32, minval=-bound, maxval=bound)
        gamma = jnp.ones((D_MODEL,), dtype=jnp.float32)
        beta = jnp.zeros((D_MODEL,), dtype=jnp.float32)
        return {'mel': mel, 'W': W, 'b': b, 'gamma': gamma, 'beta': beta}
    _L0_tok_all = _L0_tok_setup()
    _L0_tok_in = {k: v for k, v in _L0_tok_all.items() if k in ('W', 'b', 'gamma', 'beta')}
    del _L0_tok_all

    def _L0_attn_setup():
        import jax, jax.numpy as jnp
        import numpy as np
        B, T, C = (2, 512, 256)
        H = 16
        HS = C // H
        key = jax.random.key(seed)
        k1, k2, k3 = jax.random.split(key, 3)
        x = jax.random.normal(k1, (B, T, C), dtype=jnp.float32)
        w_qkv = jax.random.normal(k2, (3 * C, C), dtype=jnp.float32) * C ** (-0.5)
        w_proj = jax.random.normal(k3, (C, C), dtype=jnp.float32) * C ** (-0.5)
        b_proj = jnp.zeros((C,), dtype=jnp.float32)
        return {'x': x, 'w_qkv': w_qkv, 'w_proj': w_proj, 'b_proj': b_proj}
    _L0_attn_all = _L0_attn_setup()
    _L0_attn_in = {k: v for k, v in _L0_attn_all.items() if k in ('w_qkv', 'w_proj', 'b_proj')}
    del _L0_attn_all

    def _L0_ffn_setup():
        import jax, jax.numpy as jnp
        import numpy as np
        import math
        B, S, H, I, E = (4, 512, 256, 1024, 8)
        TOP_K = 2
        CAPACITY_FACTOR = 1.25
        key = jax.random.key(seed)
        k1, k2, k3, k4, k5 = jax.random.split(key, 5)
        x = jax.random.normal(k1, (B, S, H), dtype=jnp.float32)
        W_router = jax.random.normal(k2, (E, H), dtype=jnp.float32) * (1.0 / math.sqrt(H))
        b_router = jnp.zeros((E,), dtype=jnp.float32)
        experts_inter = jax.random.normal(k3, (E, H, I), dtype=jnp.float32) * 0.02
        experts_out = jax.random.normal(k4, (E, I, H), dtype=jnp.float32) * 0.02
        return {'x': x, 'W_router': W_router, 'b_router': b_router, 'experts_inter': experts_inter, 'experts_out': experts_out}
    _L0_ffn_all = _L0_ffn_setup()
    _L0_ffn_in = {k: v for k, v in _L0_ffn_all.items() if k in ('W_router', 'b_router', 'experts_inter', 'experts_out')}
    del _L0_ffn_all
    return {'x': x, 'L0_tok_W': _L0_tok_in['W'], 'L0_tok_b': _L0_tok_in['b'], 'L0_tok_gamma': _L0_tok_in['gamma'], 'L0_tok_beta': _L0_tok_in['beta'], 'L0_attn_w_qkv': _L0_attn_in['w_qkv'], 'L0_attn_w_proj': _L0_attn_in['w_proj'], 'L0_attn_b_proj': _L0_attn_in['b_proj'], 'L0_ffn_W_router': _L0_ffn_in['W_router'], 'L0_ffn_b_router': _L0_ffn_in['b_router'], 'L0_ffn_experts_inter': _L0_ffn_in['experts_inter'], 'L0_ffn_experts_out': _L0_ffn_in['experts_out']}

def reference(x, L0_tok_W, L0_tok_b, L0_tok_gamma, L0_tok_beta, L0_attn_w_qkv, L0_attn_w_proj, L0_attn_b_proj, L0_ffn_W_router, L0_ffn_b_router, L0_ffn_experts_inter, L0_ffn_experts_out):
    import jax
    import jax.numpy as jnp

    def _L0_tok_ref(mel, W, b, gamma, beta):
        import jax, jax.numpy as jnp
        import numpy as np
        N_MELS = 80
        PATCH_FRAMES = 8
        HOP_FRAMES = 4
        D_MODEL = 256
        PATCH_DIM = N_MELS * PATCH_FRAMES

        def _patchify(mel):
            T = mel.shape[2]
            N = (T - PATCH_FRAMES) // HOP_FRAMES + 1
            idx = jnp.arange(N)[:, None] * HOP_FRAMES + jnp.arange(PATCH_FRAMES)[None, :]
            patches = mel[:, :, idx]
            patches = jnp.transpose(patches, (0, 2, 1, 3))
            return patches.reshape(patches.shape[0], N, PATCH_DIM)
        patches = _patchify(mel)
        x = jnp.einsum('bnp,pd->bnd', patches, W) + b
        mu = jnp.mean(x, axis=-1, keepdims=True)
        var = jnp.mean(jnp.square(x - mu), axis=-1, keepdims=True)
        x_hat = (x - mu) * jax.lax.rsqrt(var + 1e-05)
        return x_hat * gamma + beta

    def _L0_attn_ref(x, w_qkv, w_proj, b_proj):
        import jax, jax.numpy as jnp
        import numpy as np
        B, T, C = (2, 512, 256)
        H = 16
        HS = C // H
        b, t, c = x.shape
        hs = c // H
        qkv = jnp.einsum('btc,fc->btf', x, w_qkv)
        qkv = qkv.reshape(b, t, 3, H, hs)
        q = jnp.transpose(qkv[:, :, 0], (0, 2, 1, 3))
        k = jnp.transpose(qkv[:, :, 1], (0, 2, 1, 3))
        v = jnp.transpose(qkv[:, :, 2], (0, 2, 1, 3))
        scores = jnp.einsum('bhqd,bhkd->bhqk', q, k) * hs ** (-0.5)
        p = jax.nn.softplus(scores)
        p = p * p
        causal = jnp.tril(jnp.ones((t, t), dtype=p.dtype))
        p = p * causal
        attn = p / (jnp.sum(p, axis=-1, keepdims=True) + 1e-09)
        out = jnp.einsum('bhqk,bhkd->bhqd', attn, v)
        out = jnp.transpose(out, (0, 2, 1, 3)).reshape(b, t, c)
        return jnp.einsum('btc,oc->bto', out, w_proj) + b_proj

    def _L0_ffn_ref(x, W_router, b_router, experts_inter, experts_out):
        import jax, jax.numpy as jnp
        import numpy as np
        import math
        B, S, H, I, E = (4, 512, 256, 1024, 8)
        TOP_K = 2
        CAPACITY_FACTOR = 1.25
        b, s, h = x.shape
        e = experts_inter.shape[0]
        T = b * s
        capacity = math.ceil(T / e * CAPACITY_FACTOR)
        x_flat = x.reshape(T, h)
        logits = x_flat @ W_router.T + b_router
        weights_flat = jax.nn.softmax(logits, axis=-1)
        top_vals, top_idx = jax.lax.top_k(weights_flat, TOP_K)
        topk_flat = jnp.zeros_like(weights_flat).at[jnp.arange(T)[:, None], top_idx].set(top_vals)
        routing_mask = (topk_flat > 0).astype(jnp.int32)
        order = jnp.argsort(-routing_mask, axis=0, stable=True)
        sorted_mask = jnp.take_along_axis(routing_mask, order, axis=0)
        sorted_mask = sorted_mask[:capacity]
        sorted_idx = order[:capacity]
        used_tokens = (sorted_idx * sorted_mask).reshape(-1)
        mask_flat = sorted_mask.reshape(-1).astype(x.dtype)
        inputs_tokens = x_flat[used_tokens] * mask_flat[:, None]
        inputs_tokens = inputs_tokens.reshape(capacity, e, h)
        inputs_weights = jnp.take_along_axis(topk_flat, sorted_idx, axis=0)
        hmid = jnp.einsum('ceh,ehi->cei', inputs_tokens, experts_inter)
        hmid = jax.nn.relu(hmid)
        out = jnp.einsum('cei,eih->ceh', hmid, experts_out)
        out = out * inputs_weights[:, :, None]
        combined = jnp.zeros((T, h), dtype=x.dtype).at[used_tokens].add(out.reshape(-1, h))
        return combined.reshape(b, s, h)
    h = _L0_tok_ref(x, L0_tok_W, L0_tok_b, L0_tok_gamma, L0_tok_beta)
    h = h + _L0_attn_ref(_layernorm(h, axis=-1), L0_attn_w_qkv, L0_attn_w_proj, L0_attn_b_proj)
    h = h + _L0_ffn_ref(_layernorm(h, axis=-1), L0_ffn_W_router, L0_ffn_b_router, L0_ffn_experts_inter, L0_ffn_experts_out)
    return h

_drawn_inputs = setup_inputs


def setup_inputs(seed=0):
    import zlib

    import numpy as np

    out = dict(_drawn_inputs(seed))
    spreads = {'L0_tok_gamma': (1.0, 0.2),
     'L0_tok_beta': (0.0, 0.1),
     'L0_attn_b_proj': (0.0, 0.1),
     'L0_ffn_b_router': (0.0, 1.963)}
    factors = {}
    for name, (base, spread) in spreads.items():
        noise = np.random.default_rng([zlib.crc32(name.encode()), seed]).standard_normal(out[name].shape)
        drawn = base * np.exp(spread * noise) if base else spread * noise
        out[name] = jnp.asarray(drawn.astype(out[name].dtype))
    for name, factor in factors.items():
        out[name] = (out[name] * factor).astype(out[name].dtype)
    return out
```

```python
from contextlib import ExitStack

import concourse.bass as bass
from concourse import mybir

ALU = mybir.AluOpType
ACT = mybir.ActivationFunctionType
AX = mybir.AxisListType
F32 = mybir.dt.float32
F32R = mybir.dt.float32r
BF16 = mybir.dt.bfloat16
I32 = mybir.dt.int32
U32 = mybir.dt.uint32

P = 128
EPS = 1e-5
DEN_EPS = 1e-9
LN_MAX = 2.0 ** 60


def words(ap):
    return ap.bitcast(F32)


def need(eng, sem, value):
    if isinstance(value, int) and value <= 0:
        return
    eng.wait_ge(sem, value)


def wait_apart(eng, sem, value, passed):
    if isinstance(value, int):
        return need(eng, sem, value)
    eng.wait_ge(sem, value)
    eng.sem_inc(passed, 1)


def audio_tower(nc, x, tok_w, tok_b, gamma, beta, wqk_t, wv_t, wp_t, b_proj, wr_t, b_router, w_in, w_out,
                out, tokens_dram, table_dram):
    B, MELS, FRAMES = x.shape
    D = tok_w.shape[2]
    TAPS = tok_w.shape[1]
    HOP = TAPS // 2
    N = (FRAMES - TAPS) // HOP + 1
    PAIRS = B // 2
    NP = 2 * N
    T = 124
    TILES = NP // T
    TOKENS = B * N
    CT = D // P
    HEADS, HS = 16, D // 16
    HT = P // HS
    K0 = P
    K1 = N - K0
    E, INNER = w_in.shape[0], w_in.shape[2]
    CAP = -(-(TOKENS * 5) // (E * 4))
    S = 117
    STILES = 8
    SLOTS = S * STILES
    ITILES = INNER // P
    HALF = SLOTS // 2
    BIG = float(1 << 20)
    SCALE = HS ** -0.5
    STACK = MELS + MELS // 2
    BATCH_COLS = N * HOP
    MID = BATCH_COLS + BATCH_COLS + HOP
    MID_HALF = HOP * T // 2
    XCOLS = MID + 2 * MID_HALF
    assert TAPS == 2 * HOP and TILES == 3 and N - T == T // 2
    UNITS = 12
    assert TILES * T == NP and SLOTS >= CAP and HALF <= 512 and CAP * E * 4 >= TOKENS * 5

    out_pairs = out.rearrange("(p k t) d -> p t k d", k=TILES, t=T)
    tokens_pairs = tokens_dram.rearrange("(p k t) d -> p t k d", k=TILES, t=T)
    table_experts = table_dram.rearrange("(e s t) w -> e t s w", e=E, s=STILES)
    w_in_v = w_in.rearrange("e (c p) i -> e p c i", p=P)
    w_out_v = w_out.rearrange("e (t p) d -> e p t d", p=P)

    with ExitStack() as ctx:
        sems = {}

        def sem(name):
            sems[name] = ctx.enter_context(nc.semaphore(name))
            return sems[name]

        with ExitStack() as mem:
            def sb(name, shape, dt=F32):
                return mem.enter_context(nc.sbuf_tensor(name, shape, dt))

            def bank(name):
                return mem.enter_context(nc.psum_tensor(name, [P, 512], F32))

            score = mem.enter_context(nc.psum_tensor("score", [P, 4, 512], F32))
            heads_out = [bank(f"heads_out{i}") for i in range(2)]
            work = [bank(f"work{i}") for i in range(2)]

            ident = sb("ident", [P, P])
            pick = sb("pick", [P, 4, P])
            before_f = sb("before_f", [P, T])
            before = sb("before", [P, T], BF16)
            ones_b = sb("ones_b", [P, T], BF16)
            expert_id = sb("expert_id", [P, E])
            token_id = sb("token_id", [P, TILES])
            mel_wa = sb("mel_wa", [P, TAPS, D], F32R)
            mel_wb = sb("mel_wb", [P, TAPS, D], F32R)
            bias_raw = sb("bias_raw", [1, 2, D])
            qk_wh = sb("qk_wh", [P, CT, 2 * D], F32R)
            qk_wl = sb("qk_wl", [P, CT, 2 * D], F32R)
            v_wh = sb("v_wh", [P, CT, D], F32R)
            v_wl = sb("v_wl", [P, CT, D], F32R)
            p_wh = sb("p_wh", [P, 4, D], F32R)
            p_wl = sb("p_wl", [P, 4, D], F32R)
            p_bias = sb("p_bias", [P, D], F32R)
            one_rows = sb("one_rows", [P, T], F32R)
            wr = sb("wr", [P, CT, E])
            br = sb("br", [P, E])
            gam = sb("gam", [P, D])
            bet = sb("bet", [P, D])

            xraw = sb("xraw", [P, XCOLS])
            xa = sb("xa", [P, XCOLS], F32R)
            xb = sb("xb", [P, XCOLS], F32R)
            h0 = sb("h0", [P, TILES, D])
            h0_next = sb("h0_next", [P, TILES, D])
            h0_kept = sb("h0_kept", [P, TILES, D])
            xn = sb("xn", [P, TILES, D])
            stats = sb("stats", [P, TILES, 6])
            mv = sb("mv", [P, TILES, 2])
            ve = sb("ve", [P, TILES])
            lnv = sb("lnv", [P, TILES])
            ra = sb("ra", [P, TILES])
            rb = sb("rb", [P, TILES])
            rc = sb("rc", [P, TILES])
            rstd = sb("rstd", [P, TILES])
            KPAD = N + K0 + P
            xth = sb("xth", [P, CT, KPAD], F32R)
            xtl = sb("xtl", [P, CT, KPAD], F32R)
            q_hl = sb("q_hl", [P, 2, CT, NP], F32R)
            q_diag = sb("q_diag", [P, HT, 2, CT, NP], F32R)
            kh = sb("kh", [P, CT, KPAD], F32R)
            kl = sb("kl", [P, CT, KPAD], F32R)
            v = sb("v", [P, 2, 2, HEADS, 2 * HS])
            RING = 4
            probs_all = sb("probs_all", [P, RING, 4 * N])
            probs = [probs_all[:, i, :] for i in range(RING)]
            stage = probs_all[:].rearrange("p r q -> p (r q)")[:, 0:TAPS * D]
            flat = q_diag[:].rearrange("p h s c q -> p (h s c q)")
            mel_wl = flat[:, 0:TAPS * D].rearrange("p (f d) -> p f d", f=TAPS)
            one_line = flat[0:1, TAPS * D:TAPS * D + XCOLS]
            bias_at = TAPS * D + XCOLS
            bias_hl = flat[0:1, bias_at:bias_at + 2 * D].rearrange("p (s d) -> p s d", s=2)
            p_bias_hl = flat[0:1, bias_at + 2 * D:bias_at + 4 * D].rearrange("p (s d) -> p s d", s=2)
            u = sb("u", [P, 4, NP])
            den = sb("den", [HEADS, NP])
            rden = sb("rden", [P, NP])
            ah = sb("ah", [P, 4, NP], F32R)
            al = sb("al", [P, 4, NP], F32R)
            h1 = sb("h1", [P, TILES, D])
            xn2 = sb("xn2", [P, TILES, D])
            stats2 = sb("stats2", [P, TILES, 6])
            mv2 = sb("mv2", [P, TILES, 2])
            ve2 = sb("ve2", [P, TILES])
            lnv2 = sb("lnv2", [P, TILES])
            ra2 = sb("ra2", [P, TILES])
            rb2 = sb("rb2", [P, TILES])
            rc2 = sb("rc2", [P, TILES])
            rstd2 = sb("rstd2", [P, TILES])
            x2t = sb("x2t", [P, CT, NP])
            lg = sb("lg", [P, TILES, E])
            top = sb("top", [P, TILES, 8])
            top_at = sb("top_at", [P, TILES, 8], U32)
            topd = sb("topd", [P, TILES, 8])
            tope = sb("tope", [P, TILES, 8])
            tsum = sb("tsum", [P, TILES])
            trec = sb("trec", [P, TILES])
            at_f = sb("at_f", [P, TILES, 2])
            valid = sb("valid", [P, 2, TILES])
            hot = sb("hot", [P, 2, TILES, E])
            hot_b = sb("hot_b", [P, TILES, E], BF16)
            seen = [sb(f"seen{i}", [P, E]) for i in range(TILES + 1)]
            seen_b = sb("seen_b", [P, E], BF16)
            rank = sb("rank", [P, TILES, E])
            mine = sb("mine", [P, 2, TILES, E])
            place = sb("place", [P, 2, TILES])
            over = sb("over", [P, 2, TILES])
            place2 = sb("place2", [P, 2, TILES])
            place_i = sb("place_i", [P, 2, TILES], U32)
            entry = sb("entry", [P, 2, TILES, 2])
            blank = sb("blank", [96, 2 * E * SLOTS // 96], I32)

            w_loaded = sem("w_loaded")
            w_stage_free = sem("w_stage_free")
            dve_setup = sem("dve_setup")
            pool_setup = sem("pool_setup")
            setup_moved = sem("setup_moved")
            x_loaded = sem("x_loaded")
            xh_made = sem("xh_made")
            xl_made = sem("xl_made")
            x_stacked = sem("x_stacked")
            tok_done = sem("tok_done")
            ln_var = sem("ln_var")
            ln_guess = sem("ln_guess")
            xhat_made = sem("xhat_made")
            h0_made = sem("h0_made")
            xn_made = sem("xn_made")
            xt_done = sem("xt_done")
            xth_made = sem("xth_made")
            xtl_made = sem("xtl_made")
            qkv_done = sem("qkv_done")
            qk_hi = sem("qk_hi")
            qk_lo = sem("qk_lo")
            v_made = sem("v_made")
            q_spread = sem("q_spread")
            scores_done = sem("scores_done")
            exp_done = sem("exp_done")
            clamp_done = sem("clamp_done")
            ln_done = sem("ln_done")
            max_done = sem("max_done")
            square_done = sem("square_done")
            causal_done = sem("causal_done")
            pv_done = sem("pv_done")
            u_made = sem("u_made")
            den_moved = sem("den_moved")
            rden_made = sem("rden_made")
            spread_done = sem("spread_done")
            attn_made = sem("attn_made")
            ah_made = sem("ah_made")
            al_made = sem("al_made")
            proj_done = sem("proj_done")
            h1_made = sem("h1_made")
            ln2_var = sem("ln2_var")
            ln2_guess = sem("ln2_guess")
            xn2_made = sem("xn2_made")
            stored = sem("stored")
            x2t_done = sem("x2t_done")
            x2t_made = sem("x2t_made")
            logits_done = sem("logits_done")
            top_ready = sem("top_ready")
            top_exp = sem("top_exp")
            hot_made = sem("hot_made")
            rank_done = sem("rank_done")
            rank_read = sem("rank_read")
            place_made = sem("place_made")
            listed = sem("listed")
            own = sem("own")
            front_own = sem("front_own")
            finish_own = sem("finish_own")
            table_blank = sem("table_blank")
            pool_passed = sem("pool_passed")
            dve_passed = sem("dve_passed")
            pe_passed = sem("pe_passed")
            sp_passed = sem("sp_passed")
            rest_split = sem("rest_split")
            q_cleared = sem("q_cleared")
            raw_made = sem("raw_made")
            h0_scaled = sem("h0_scaled")
            h0_next_moved = sem("h0_next_moved")
            h0_kept_moved = sem("h0_kept_moved")

            def keys(b, kt):
                return b * N + kt * K0

            def unit(w):
                return w // 6, w // 3 % 2, w % 3

            def patches(t, k, f):
                rows = STACK + 1 if f == 0 else STACK
                at = MID + f - HOP if k == 1 and f >= HOP else HOP * T * k + f
                return t[:rows, at:at + HOP * (T - 1) + 1:HOP]

            def frames(n):
                if isinstance(n, int):
                    src = x[2 * n], x[2 * n + 1]
                else:
                    src = [x[bass.ds(2 * n + b, 1)].rearrange("b m t -> (b m) t") for b in range(2)]
                return [(xraw[:MELS, 0:BATCH_COLS], src[0][:, 0:BATCH_COLS]),
                        (xraw[:MELS, BATCH_COLS:MID], src[1][:, 0:BATCH_COLS + HOP]),
                        (xraw[:MELS, MID:MID + MID_HALF], src[0][:, HOP * (T + 1):HOP * (T + 1) + MID_HALF]),
                        (xraw[:MELS, MID + MID_HALF:XCOLS], src[1][:, HOP:HOP + MID_HALF])]

            block = mem.enter_context(nc.Block())

            @block.sync
            def _(sp):
                sp.dma_start(stage[:MELS, :], tok_w.rearrange("m f d -> m (f d)")).then_inc(w_loaded, 16)
                sp.dma_start(bias_raw[:, 0, :], tok_b).then_inc(w_loaded, 16)
                sp.dma_start(bias_raw[:, 1, :], b_proj).then_inc(w_loaded, 16)
                sp.dma_start(wr[:], wr_t.rearrange("(c p) e -> p c e", p=P)).then_inc(w_loaded, 16)
                sp.dma_start(br[:], b_router.partition_broadcast(P)).then_inc(w_loaded, 16)
                sp.dma_start(gam[:], gamma.partition_broadcast(P)).then_inc(w_loaded, 16)
                sp.dma_start(bet[:], beta.partition_broadcast(P)).then_inc(w_loaded, 16)
                for cols, src in frames(0):
                    sp.dma_start(cols, src).then_inc(x_loaded, 16)
                sp.wait_ge(dve_setup, 4)
                sp.dma_start(words(mel_wa[MELS:STACK, :, :]), words(mel_wl[0:STACK - MELS, :, :])).then_inc(setup_moved, 16)
                sp.dma_start(words(mel_wb[MELS:STACK, :, :]), words(mel_wl[STACK - MELS:MELS, :, :])).then_inc(setup_moved, 16)
                sp.dma_start(words(mel_wa[STACK:STACK + 1, 0, :]), words(bias_hl[:, 0])).then_inc(setup_moved, 16)
                sp.dma_start(words(mel_wb[STACK:STACK + 1, 0, :]), words(bias_hl[:, 1])).then_inc(setup_moved, 16)
                sp.dma_start(words(p_bias[0:1, :]), words(p_bias_hl[:, 0])).then_inc(setup_moved, 16)
                sp.dma_start(words(p_bias[1:2, :]), words(p_bias_hl[:, 1])).then_inc(setup_moved, 16)
                sp.dma_start(words(xa[STACK:STACK + 1, :]), words(one_line)).then_inc(setup_moved, 16)
                sp.dma_start(words(xb[STACK:STACK + 1, :]), words(one_line)).then_inc(setup_moved, 16)
                sp.dma_start(words(one_rows[0:1, :]), words(one_line[:, 0:T])).then_inc(setup_moved, 16)
                sp.dma_start(words(one_rows[1:2, :]), words(one_line[:, 0:T])).then_inc(setup_moved, 16)
                sp.dma_start(stage[:, 0:CT * 2 * D].rearrange("p (c n) -> p c n", c=CT),
                             wqk_t.rearrange("(c p) n -> p c n", p=P)).then_inc(w_loaded, 16)
                sp.wait_ge(pool_setup, 9)
                sp.dma_start(table_dram.rearrange("(p n) w -> p (n w)", p=96).bitcast(I32), blank[:]).then_inc(table_blank, 16)

                def stack(n):
                    h = STACK - MELS
                    sp.wait_ge(xh_made, n)
                    sp.dma_start(words(xa[MELS:STACK, :]), words(xa[0:h, :])).then_inc(x_stacked, 16)
                    sp.dma_start(words(xb[MELS:STACK, :]), words(xa[h:MELS, :])).then_inc(x_stacked, 16)

                def load_x(n, parts):
                    sp.wait_ge(xl_made, n)
                    for cols, src in parts:
                        sp.dma_start(cols, src).then_inc(x_loaded, 16)

                def spread_q(lo, free):
                    wait_apart(sp, qk_lo, lo, sp_passed)
                    if free is not None:
                        sp.wait_ge(scores_done, free)
                    for h in range(HT):
                        sp.dma_start(words(q_diag[HS * h:HS * h + HS, h]), words(q_hl[HS * h:HS * h + HS])).then_inc(q_spread, 16)

                def move_den(made, free):
                    sp.wait_ge(u_made, made)
                    if free is not None:
                        sp.wait_ge(rden_made, free)
                    for g in range(4):
                        sp.dma_start(den[4 * g:4 * g + 4, :], u[HS:P:2 * HS, g, :]).then_inc(den_moved, 16)

                def keep_h0(h1_n, next_n, kept_n, h0_n):
                    if h1_n is not None:
                        sp.wait_ge(h1_made, h1_n)
                    sp.wait_ge(h0_next_moved, next_n)
                    sp.dma_start(h0_kept[:T], h0_next[:T]).then_inc(h0_kept_moved, 16)
                    if h0_n is not None:
                        sp.wait_ge(h0_kept_moved, kept_n)
                        sp.wait_ge(h0_made, h0_n)
                        sp.dma_start(h0_next[:T], h0[:T]).then_inc(h0_next_moved, 16)

                def store(n, out_at, tokens_at):
                    sp.wait_ge(h1_made, n)
                    sp.dma_start(out_at, h1[:T]).then_inc(stored, 16)
                    sp.wait_ge(xn2_made, n)
                    sp.dma_start(tokens_at, xn2[:T]).then_inc(stored, 16)

                stack(1)
                load_x(1, frames(1))
                sp.wait_ge(w_stage_free, 1)
                sp.dma_start(stage[:, 0:CT * D].rearrange("p (c n) -> p c n", c=CT),
                             wv_t.rearrange("(c p) n -> p c n", p=P)).then_inc(w_loaded, 16)
                sp.dma_start(stage[:, CT * D:CT * D + 4 * D].rearrange("p (c n) -> p c n", c=4),
                             wp_t.rearrange("(c p) n -> p c n", p=P)).then_inc(w_loaded, 16)
                stack(2)
                sp.wait_ge(h0_made, 1)
                sp.dma_start(h0_next[:T], h0[:T]).then_inc(h0_next_moved, 16)

                def body(i, n, finish, front, load):
                    if load is not None:
                        load_x(n["xl"], load)
                    spread_q(n["lo"], n["scores"])
                    if load is not None:
                        stack(n["xh"])
                    keep_h0(n["i"] if finish else None, n["next"], n["kept"], n["h0"] if front else None)
                    if finish:
                        store(n["i"], n["out"], n["tokens"])
                    move_den(n["u"], n["i"] if finish else None)

                def counts(i):
                    n = dict(xl=i + 2, lo=4 * i + 4, scores=UNITS * i, xh=i + 3, i=i, next=16 * i + 16,
                             kept=16 * i + 16, h0=i + 2, u=4 * i + 4)
                    if isinstance(i, int):
                        n["scores"] = n["scores"] or None
                        if i:
                            n["out"], n["tokens"] = out_pairs[i - 1], tokens_pairs[i - 1]
                    else:
                        n["out"] = out_pairs[bass.ds(i - 1, 1)].rearrange("p t k d -> (p t) k d")
                        n["tokens"] = tokens_pairs[bass.ds(i - 1, 1)].rearrange("p t k d -> (p t) k d")
                        n = {k: (v_ if k in ("out", "tokens") else sp.snap(v_)) for k, v_ in n.items()}
                    return n

                body(0, counts(0), False, True, frames(2))
                body(1, counts(1), True, True, frames(3))
                with sp.Fori(2, PAIRS - 2) as i:
                    body(i, counts(i), True, True, frames(i + 2))
                body(PAIRS - 2, counts(PAIRS - 2), True, True, None)
                body(PAIRS - 1, counts(PAIRS - 1), True, False, None)
                store(PAIRS, out_pairs[PAIRS - 1], tokens_pairs[PAIRS - 1])
                sp.wait_ge(stored, 32 * PAIRS)

            @block.gpsimd
            def _(pool):
                setup = [0]

                def made(ins, wait=False):
                    setup[0] += 1
                    ins.then_inc(pool_setup, 1)
                    if wait:
                        pool.wait_ge(pool_setup, setup[0])

                made(pool.memset(ident[:], 0.0))
                made(pool.memset(pick[:], 0.0))
                made(pool.memset(before_f[:], 1.0))
                made(pool.memset(blank[:], 1 << 20), True)
                made(pool.affine_select(out=ident[:], in_=ident[:], compare_op=ALU.not_equal, fill=1.0, base=0,
                                        pattern=[[-1, P]], channel_multiplier=1))
                made(pool.affine_select(out=pick[:].rearrange("p g (j d) -> p g j d", j=4),
                                        in_=pick[:].rearrange("p g (j d) -> p g j d", j=4),
                                        compare_op=ALU.not_equal, fill=1.0, base=0,
                                        pattern=[[4, 4], [1, 4], [0, 2 * HS]], channel_multiplier=-1))
                made(pool.affine_select(out=before_f[:], in_=before_f[:], compare_op=ALU.is_gt, fill=0.0, base=0,
                                        pattern=[[1, T]], channel_multiplier=-1))
                made(pool.iota(expert_id[:], pattern=[[1, E]], base=0, channel_multiplier=0,
                               allow_small_or_imprecise_dtypes=True))
                made(pool.iota(token_id[:], pattern=[[T, TILES]], base=0, channel_multiplier=1,
                               allow_small_or_imprecise_dtypes=True))

                def x_lo(n):
                    pool.wait_ge(xh_made, n + 1)
                    need(pool, tok_done, 2 * n)
                    pool.tensor_tensor(xb[:MELS, :], xraw[:MELS, :], xa[:MELS, :].bitcast(F32),
                                       ALU.subtract).then_inc(xl_made, 1)

                def affine(n):
                    pool.wait_ge(xhat_made, n + 1)
                    need(pool, h0_next_moved, 16 * n)
                    g = gam[:T].rearrange("p (a d) -> p a d", a=1).broadcast_to([T, TILES, D])
                    b = bet[:T].rearrange("p (a d) -> p a d", a=1).broadcast_to([T, TILES, D])
                    pool.tensor_tensor(h0[:T], xn[:T], g, ALU.mult).then_inc(h0_scaled, 1)
                    pool.wait_ge(h0_scaled, n + 1)
                    pool.tensor_tensor(h0[:T], h0[:T], b, ALU.add).then_inc(h0_made, 1)

                def causal(n, w):
                    ct, b, part = unit(w)
                    buf = probs[w % RING]
                    wait_apart(pool, square_done, n * UNITS + w + 1, pool_passed)
                    if part < 2:
                        a = buf.rearrange("p (h q) -> p h q", h=4)[:, :, 0:K0]
                        pattern = [[0, 4], [1, K0]]
                    else:
                        a = buf[0:K1, 0:HT * K1].rearrange("p (h q) -> p h q", h=HT)
                        pattern = [[0, HT], [1, K1]]
                    pool.affine_select(out=a, in_=a, compare_op=ALU.is_ge, fill=0.0, base=0, pattern=pattern,
                                       channel_multiplier=-1).then_inc(causal_done, 1)

                def attn_lo(n, g):
                    pool.wait_ge(ah_made, n * 4 + g + 1)
                    if g == 0:
                        need(pool, proj_done, 2 * n)
                    pool.tensor_tensor(al[:, g, :], u[:, g, :], ah[:, g, :].bitcast(F32), ALU.subtract).then_inc(al_made, 1)

                def lists(n):
                    wait_apart(pool, place_made, n + 1, pool_passed)
                    for c in range(2):
                        for k in range(TILES):
                            pool.indirect_dma_start(
                                out=table_dram[:, :],
                                out_offset=bass.IndirectOffsetOnAxis(ap=place_i[:T, c, k:k + 1], axis=0),
                                in_=entry[:T, c, k, :], in_offset=None,
                                bounds_check=E * SLOTS - 1, oob_is_err=False).then_inc(listed, 16)

                x_lo(0)
                pool.wait_ge(setup_moved, 160)
                pool.memset(q_diag[:].bitcast(F32), 0.0).then_inc(q_cleared, 1)
                affine(0)
                x_lo(1)
                pool.wait_ge(table_blank, 16)

                def body(i, finish, front, split):
                    for s in range(UNITS + 3):
                        if finish and s in (4, 5):
                            attn_lo(i - 1, 2 * s - 8)
                            attn_lo(i - 1, 2 * s - 7)
                        if front and s == 5:
                            affine(i + 1)
                        if split and s == 7:
                            x_lo(i + 2)
                        if 2 <= s < UNITS + 2:
                            causal(i, s - 2)
                    if finish:
                        lists(i - 1)

                body(0, False, True, True)
                body(1, True, True, True)
                with pool.Fori(2, PAIRS - 2) as i:
                    body(i, True, True, True)
                body(PAIRS - 2, True, True, False)
                body(PAIRS - 1, True, False, False)
                for g in range(4):
                    attn_lo(PAIRS - 1, g)
                lists(PAIRS - 1)
                pool.wait_ge(listed, 16 * 2 * TILES * PAIRS)

            @block.scalar
            def _(act):
                act.preload_act_table_set("natural_log_exp_and_others")

                def x_hi(n):
                    act.wait_ge(x_loaded, n * 64 + 64)
                    need(act, tok_done, 2 * n)
                    act.activation(xa[:MELS, :], xraw[:MELS, :], ACT.Copy).then_inc(xh_made, 1)

                def take_tok(n):
                    for j, cols in ((0, 2), (1, 1)):
                        act.wait_ge(tok_done, n * 2 + j + 1)
                        if j == 0:
                            need(act, xt_done, 2 * n)
                        act.activation(xn[:T, 2 * j:2 * j + cols, :].rearrange("p k d -> p (k d)"),
                                       work[j][:T, 0:cols * D], ACT.Copy).then_inc(raw_made, 1)

                def guess(n, second):
                    act.wait_ge(ln_var, n * 2 + second + 1)
                    act.activation(lnv[:T], ve[:T], ACT.Ln).then_inc(ln_guess, 1)
                    act.wait_ge(ln_guess, n * 4 + 2 * second + 1)
                    act.activation(ra[:T], lnv[:T], ACT.Exp, scale=-0.5).then_inc(ln_guess, 1)

                def guess2(n):
                    act.wait_ge(ln2_var, n + 1)
                    act.activation(lnv2[:T], ve2[:T], ACT.Ln).then_inc(ln2_guess, 1)
                    act.wait_ge(ln2_guess, n * 2 + 1)
                    act.activation(ra2[:T], lnv2[:T], ACT.Exp, scale=-0.5).then_inc(ln2_guess, 1)

                def xt_hi(n):
                    for c in range(CT):
                        act.wait_ge(xt_done, n * 2 + c + 1)
                        if c == 0:
                            need(act, qkv_done, 6 * n)
                        act.activation(xth[:, c, 0:NP], work[c][:, 0:NP], ACT.Copy).then_inc(xth_made, 1)

                def qkv_hi(n):
                    for s in range(4):
                        act.wait_ge(qkv_done, n * 6 + s + 1)
                        if s == 0:
                            need(act, q_spread, 16 * HT * n)
                        if s == 2:
                            need(act, scores_done, UNITS * n)
                        dst = q_hl[:, 0, s % 2, :] if s < 2 else kh[:, s % 2, 0:NP]
                        act.activation(dst, work[s % 2][:, 0:NP], ACT.Copy).then_inc(qk_hi, 1)
                    for b in range(2):
                        act.wait_ge(qkv_done, n * 6 + 5 + b)
                        if b == 0:
                            need(act, pv_done, UNITS * n)
                        for kt, rows in ((0, K0), (1, K1)):
                            act.activation(v[:rows, b, kt, :, 0:HS],
                                           work[b][:rows, kt * D:kt * D + D].rearrange("p (h d) -> p h d", h=HEADS),
                                           ACT.Copy).then_inc(v_made, 1)

                def whole(w):
                    return probs[w % RING] if unit(w)[2] < 2 else probs[w % RING][0:K1, 0:HT * K1]

                def expo(n, w):
                    s = 2 * (w % 2)
                    act.wait_ge(scores_done, n * UNITS + w + 1)
                    need(act, pv_done, n * UNITS + w + 1 - RING)
                    if unit(w)[2] < 2:
                        src, dst = score[:, s:s + 2, 0:2 * N], whole(w).rearrange("p (a q) -> p a q", a=2)
                    else:
                        src, dst = score[0:K1, s, 0:HT * K1], whole(w)
                    act.activation(dst, src, ACT.Exp, scale=SCALE).then_inc(exp_done, 1)

                def loga(n, w):
                    act.wait_ge(clamp_done, n * UNITS + w + 1)
                    act.activation(whole(w), whole(w), ACT.Ln, bias=1.0).then_inc(ln_done, 1)

                def square(n, w):
                    act.wait_ge(max_done, n * UNITS + w + 1)
                    act.activation(whole(w), whole(w), ACT.Square).then_inc(square_done, 1)

                def attn_hi(n, g):
                    act.wait_ge(attn_made, n * 4 + g + 1)
                    if g == 0:
                        need(act, proj_done, 2 * n)
                    act.activation(ah[:, g, :], u[:, g, :], ACT.Copy).then_inc(ah_made, 1)

                def x2t_copy(n):
                    for c in range(CT):
                        act.wait_ge(x2t_done, n * 2 + c + 1)
                        if c == 0:
                            need(act, logits_done, n)
                        act.activation(x2t[:, c, :], work[c][:, 0:NP], ACT.Copy).then_inc(x2t_made, 1)

                def top_exps(n):
                    act.wait_ge(top_ready, n + 1)
                    act.activation(tope[:T], topd[:T], ACT.Exp).then_inc(top_exp, 1)

                def front_part(n, w):
                    if w == 1:
                        take_tok(n)
                    if w == 3:
                        guess(n, 0)
                    if w == 7:
                        guess(n, 1)
                    if w == 9:
                        xt_hi(n)

                def finish_part(n, w):
                    if w in (3, 5):
                        attn_hi(n, w - 3)
                        attn_hi(n, w - 2)
                    if w == 8:
                        guess2(n)
                    if w == 10:
                        x2t_copy(n)
                    if w == 12:
                        top_exps(n)

                x_hi(0)
                for w in range(UNITS):
                    front_part(0, w)
                x_hi(1)

                def body(i, finish, front, split):
                    qkv_hi(i)
                    for w in range(UNITS + 3):
                        if w < UNITS:
                            expo(i, w)
                        if finish:
                            finish_part(i - 1, w)
                        if front:
                            front_part(i + 1, w)
                        if 1 <= w <= UNITS:
                            loga(i, w - 1)
                        if 2 <= w < UNITS + 2:
                            square(i, w - 2)
                        if split and w == 6:
                            x_hi(i + 2)

                body(0, False, True, True)
                body(1, True, True, True)
                with act.Fori(2, PAIRS - 2) as i:
                    body(i, True, True, True)
                body(PAIRS - 2, True, True, False)
                body(PAIRS - 1, True, False, False)
                for w in range(UNITS + 3):
                    finish_part(PAIRS - 1, w)

            @block.vector
            def _(dve):
                wst = stage[:MELS, :].rearrange("p (f d) -> p f d", f=TAPS)
                steps = [0]

                def link(ins):
                    steps[0] += 1
                    ins.then_inc(own, 1)
                    dve.wait_ge(own, steps[0])

                link(dve.memset(p_bias[:].bitcast(F32), 0.0))
                link(dve.memset(one_rows[:].bitcast(F32), 0.0))
                link(dve.memset(one_line.bitcast(F32), 1.0))
                dve.wait_ge(w_loaded, 16 * 7)
                link(dve.tensor_copy(mel_wa[:MELS], wst))
                link(dve.tensor_copy(bias_hl[:, 0, :], bias_raw[:, 0, :]))
                link(dve.tensor_copy(p_bias_hl[:, 0, :], bias_raw[:, 1, :]))
                dve.tensor_copy(mel_wb[:MELS], wst).then_inc(dve_setup, 1)
                dve.tensor_tensor(mel_wl[:MELS], wst, mel_wa[:MELS].bitcast(F32), ALU.subtract).then_inc(dve_setup, 1)
                dve.tensor_tensor(bias_hl[:, 1, :], bias_raw[:, 0, :], bias_hl[:, 0, :].bitcast(F32),
                                  ALU.subtract).then_inc(dve_setup, 1)
                dve.tensor_tensor(p_bias_hl[:, 1, :], bias_raw[:, 1, :], p_bias_hl[:, 0, :].bitcast(F32),
                                  ALU.subtract).then_inc(dve_setup, 1)
                for t in (xth, xtl, kh, kl):
                    dve.memset(t[:, :, NP:KPAD].bitcast(F32), 0.0).then_inc(dve_setup, 1)
                dve.memset(ones_b[:], 1.0).then_inc(dve_setup, 1)
                dve.memset(v[:], 1.0).then_inc(dve_setup, 1)
                dve.memset(rden[:], 0.0).then_inc(dve_setup, 1)
                dve.memset(seen[0][:], 0.0).then_inc(dve_setup, 1)
                dve.memset(seen_b[:], 0.0).then_inc(dve_setup, 1)
                dve.wait_ge(pool_setup, 9)
                dve.tensor_copy(before[:], before_f[:]).then_inc(dve_setup, 1)
                SETUP = 14
                dve.wait_ge(dve_setup, SETUP)

                def split_rest():
                    sv = stage[:, 0:CT * 2 * D].rearrange("p (c n) -> p c n", c=CT)
                    dve.wait_ge(w_loaded, 16 * 8)
                    link(dve.tensor_copy(qk_wh[:], sv))
                    dve.tensor_tensor(qk_wl[:], sv, qk_wh[:].bitcast(F32), ALU.subtract).then_inc(w_stage_free, 1)
                    dve.wait_ge(w_loaded, 16 * 10)
                    sv2 = stage[:, 0:CT * D].rearrange("p (c n) -> p c n", c=CT)
                    sv3 = stage[:, CT * D:CT * D + 4 * D].rearrange("p (c n) -> p c n", c=4)
                    link(dve.tensor_copy(v_wh[:], sv2))
                    link(dve.tensor_copy(p_wh[:], sv3))
                    dve.tensor_tensor(v_wl[:], sv2, v_wh[:].bitcast(F32), ALU.subtract).then_inc(rest_split, 1)
                    dve.tensor_tensor(p_wl[:], sv3, p_wh[:].bitcast(F32), ALU.subtract).then_inc(rest_split, 1)

                def chain(signal, per, n, done):
                    count = [done]

                    def step(ins, apart=False):
                        count[0] += 1
                        ins.then_inc(signal, 1)
                        if apart:
                            wait_apart(dve, signal, n * per + count[0], dve_passed)
                        else:
                            dve.wait_ge(signal, n * per + count[0])
                    return step, count

                def mean_var(src, st, m, v_, signal, step):
                    for k in range(TILES):
                        last = dve.bn_stats(st[:T, k, :], src[:T, k, :])
                    step(last, True)
                    for k in range(TILES):
                        last = dve.bn_aggr(m[:T, k, :], st[:T, k, :])
                    step(last)
                    dve.tensor_scalar(v_[:T], m[:T, :, 1], EPS, None, ALU.add).then_inc(signal, 1)

                def newton(v_, a, b, c, r, step):
                    step(dve.tensor_tensor(b[:T], a[:T], a[:T], ALU.mult))
                    step(dve.scalar_tensor_tensor(out=c[:T], in0=b[:T], scalar=-0.5, in1=v_[:T],
                                                  op0=ALU.mult, op1=ALU.mult))
                    step(dve.scalar_tensor_tensor(out=r[:T], in0=c[:T], scalar=1.5, in1=a[:T],
                                                  op0=ALU.add, op1=ALU.mult))

                def normalise(dst, src, m, r):
                    for k in range(TILES):
                        last = dve.tensor_scalar(dst[:T, k, :], src[:T, k, :], m[:T, k, 0:1], r[:T, k:k + 1],
                                                 ALU.subtract, ALU.mult)
                    return last

                FRONT = 10

                def front_a(n):
                    step, _ = chain(front_own, FRONT, n, 0)
                    dve.wait_ge(raw_made, n * 2 + 2)
                    need(dve, xn_made, n)
                    mean_var(xn, stats, mv, ve, ln_var, step)

                def front_b(n):
                    step, _ = chain(front_own, FRONT, n, 2)
                    dve.wait_ge(ln_guess, n * 4 + 2)
                    newton(ve, ra, rb, rc, rstd, step)
                    normalise(xn, xn, mv, rstd).then_inc(xhat_made, 1)

                def front_c(n):
                    step, _ = chain(front_own, FRONT, n, 5)
                    dve.wait_ge(h0_made, n + 1)
                    mean_var(h0, stats, mv, ve, ln_var, step)

                def front_d(n):
                    step, c = chain(front_own, FRONT, n, 7)
                    dve.wait_ge(ln_guess, n * 4 + 4)
                    newton(ve, ra, rb, rc, rstd, step)
                    normalise(xn, h0, mv, rstd).then_inc(xn_made, 1)
                    assert c[0] == FRONT

                def xt_lo(n):
                    for c in range(CT):
                        dve.wait_ge(xth_made, n * 2 + c + 1)
                        dve.tensor_tensor(xtl[:, c, 0:NP], work[c][:, 0:NP], xth[:, c, 0:NP].bitcast(F32),
                                          ALU.subtract).then_inc(xtl_made, 1)

                def qkv_lo(n):
                    for s in range(4):
                        dve.wait_ge(qk_hi, n * 4 + s + 1)
                        dst, hi = (q_hl[:, 1, s % 2, :], q_hl[:, 0, s % 2, :]) if s < 2 else \
                            (kl[:, s % 2, 0:NP], kh[:, s % 2, 0:NP])
                        dve.tensor_tensor(dst, work[s % 2][:, 0:NP], hi.bitcast(F32), ALU.subtract).then_inc(qk_lo, 1)

                def whole(w):
                    return probs[w % RING] if unit(w)[2] < 2 else probs[w % RING][0:K1, 0:HT * K1]

                def clamp(n, w):
                    dve.wait_ge(exp_done, n * UNITS + w + 1)
                    dve.tensor_scalar(whole(w), whole(w), LN_MAX, None, ALU.min).then_inc(clamp_done, 1)

                def soft(n, w):
                    s = 2 * (w % 2)
                    dve.wait_ge(ln_done, n * UNITS + w + 1)
                    if unit(w)[2] < 2:
                        x_, a = score[:, s:s + 2, 0:2 * N], whole(w).rearrange("p (a q) -> p a q", a=2)
                    else:
                        x_, a = score[0:K1, s, 0:HT * K1], whole(w)
                    dve.scalar_tensor_tensor(out=a, in0=x_, scalar=SCALE, in1=a, op0=ALU.mult,
                                             op1=ALU.max).then_inc(max_done, 1)

                def take_u(n, ct):
                    dve.wait_ge(pv_done, n * UNITS + 6 * ct + 6)
                    if ct == 0:
                        need(dve, al_made, 4 * n)
                    for j in range(2):
                        dve.tensor_copy(u[:, 2 * ct + j, :], heads_out[j][:, 0:NP]).then_inc(u_made, 1)

                AT_DIVIDE, AT_RESIDUAL, AT_NORM, AT_TOP, AT_WEIGHTS, AT_PLACES = 0, 1, 3, 6, 9, 15
                FINISH = AT_PLACES + TILES + 5

                def divide(n):
                    step, _ = chain(finish_own, FINISH, n, AT_DIVIDE)
                    dve.wait_ge(den_moved, n * 64 + 64)
                    need(dve, spread_done, 4 * n)
                    step(dve.tensor_scalar(den[:], den[:], DEN_EPS, None, ALU.add))
                    dve.reciprocal(rden[0:HEADS, :], den[:]).then_inc(rden_made, 1)

                def scale_heads(n, g):
                    dve.wait_ge(spread_done, n * 4 + g + 1)
                    dve.tensor_tensor(u[:, g, :], u[:, g, :], work[g % 2][:, 0:NP], ALU.mult).then_inc(attn_made, 1)

                def residual(n):
                    step, _ = chain(finish_own, FINISH, n, AT_RESIDUAL)
                    need(dve, stored, 32 * n)
                    need(dve, xn2_made, n)
                    dve.wait_ge(h0_kept_moved, n * 16 + 16)
                    dve.wait_ge(proj_done, n * 2 + 1)
                    dve.tensor_tensor(h1[:T, 0:2, :], work[0][:T, :].rearrange("p (k d) -> p k d", k=2),
                                      h0_kept[:T, 0:2, :], ALU.add)
                    dve.wait_ge(proj_done, n * 2 + 2)
                    dve.tensor_tensor(h1[:T, 2, :], work[1][:T, 0:D], h0_kept[:T, 2, :], ALU.add).then_inc(h1_made, 1)
                    dve.wait_ge(h1_made, n + 1)
                    mean_var(h1, stats2, mv2, ve2, ln2_var, step)

                def norm2(n):
                    step, c = chain(finish_own, FINISH, n, AT_NORM)
                    dve.wait_ge(ln2_guess, n * 2 + 2)
                    need(dve, x2t_done, 2 * n)
                    newton(ve2, ra2, rb2, rc2, rstd2, step)
                    normalise(xn2, h1, mv2, rstd2).then_inc(xn2_made, 1)

                def top_two(n):
                    step, _ = chain(finish_own, FINISH, n, AT_TOP)
                    dve.wait_ge(logits_done, n + 1)
                    step(dve.tensor_tensor(lg[:T], work[0][:T, 0:TILES * E].rearrange("p (k e) -> p k e", k=TILES),
                                           br[:T].rearrange("p (a e) -> p a e", a=1).broadcast_to([T, TILES, E]), ALU.add), True)
                    for k in range(TILES):
                        last = dve.max(top[:T, k, :], lg[:T, k, :])
                    step(last)
                    need(dve, top_exp, n)
                    dve.tensor_tensor(topd[:T], top[:T], top[:T, :, 0:1].broadcast_to([T, TILES, 8]),
                                      ALU.subtract).then_inc(top_ready, 1)
                    for k in range(TILES):
                        last = dve.max_index(top_at[:T, k, :], top[:T, k, :], lg[:T, k, :])
                    step(last)

                def weights(n):
                    step, c = chain(finish_own, FINISH, n, AT_WEIGHTS)
                    dve.wait_ge(top_exp, n + 1)
                    step(dve.tensor_reduce(tsum[:T], tope[:T], AX.X, ALU.add))
                    step(dve.reciprocal(trec[:T], tsum[:T]))
                    need(dve, listed, n * (16 * 2 * TILES))
                    for j in range(2):
                        last = dve.tensor_tensor(entry[:T, j, :, 1], tope[:T, :, j], trec[:T], ALU.mult)
                    step(last)
                    for j in range(2):
                        last = dve.tensor_scalar(valid[:T, j, :], entry[:T, j, :, 1], 0.0, None, ALU.is_gt)
                    dve.tensor_copy(at_f[:T], top_at[:T, :, 0:2])
                    step(dve.tensor_copy(entry[:T, :, :, 0].bitcast(I32),
                                         token_id[:T].rearrange("p (a k) -> p a k", a=1).broadcast_to([T, 2, TILES])))
                    dve.tensor_scalar(token_id[:T], token_id[:T], float(NP), None, ALU.add)
                    for j in range(2):
                        last = dve.tensor_tensor(hot[:T, j],
                                                 expert_id[:T].rearrange("p (a e) -> p a e", a=1).broadcast_to([T, TILES, E]),
                                                 at_f[:T, :, j:j + 1].broadcast_to([T, TILES, E]), ALU.is_equal)
                    step(last)
                    for j in range(2):
                        last = dve.tensor_tensor(hot[:T, j], hot[:T, j],
                                                 valid[:T, j, :].rearrange("p (k a) -> p k a", a=1).broadcast_to([T, TILES, E]),
                                                 ALU.mult)
                    step(last)
                    dve.tensor_tensor(hot_b[:T], hot[:T, 0], hot[:T, 1], ALU.add).then_inc(hot_made, 1)

                def places(n):
                    step, c = chain(finish_own, FINISH, n, AT_PLACES)
                    dve.wait_ge(rank_done, n + 1)
                    dve.tensor_copy(rank[:T], work[1][:T, 0:TILES * E].rearrange("p (k e) -> p k e",
                                                                              k=TILES)).then_inc(rank_read, 1)
                    for k in range(TILES):
                        step(dve.tensor_tensor(seen[k + 1][:T], seen[k][:T], hot_b[:T, k, :], ALU.add))
                    dve.wait_ge(rank_read, n + 1)
                    dve.tensor_copy(seen[0][:T], seen[TILES][:T])
                    dve.tensor_copy(seen_b[:T], seen[TILES][:T])
                    for j in range(2):
                        last = dve.tensor_tensor(mine[:T, j], hot[:T, j], rank[:T], ALU.mult)
                    step(last)
                    step(dve.tensor_reduce(place[:T], mine[:T], AX.X, ALU.add))
                    step(dve.tensor_scalar(over[:T], place[:T], float(CAP), BIG, ALU.is_ge, ALU.mult))
                    step(dve.tensor_tensor(place2[:T], place[:T], over[:T], ALU.add))
                    dve.tensor_scalar(over[:T], valid[:T], -BIG, BIG, ALU.mult, ALU.add)
                    for j in range(2):
                        last = dve.scalar_tensor_tensor(out=place[:T, j], in0=at_f[:T, :, j], scalar=float(SLOTS),
                                                        in1=place2[:T, j], op0=ALU.mult, op1=ALU.add)
                    step(last)
                    dve.tensor_tensor(place_i[:T], place[:T], over[:T], ALU.add).then_inc(place_made, 1)
                    assert c[0] == FINISH, (c, FINISH)

                def front_part(n, w):
                    if w == 2:
                        front_a(n)
                    if w == 4:
                        front_b(n)
                    if w == 6:
                        front_c(n)
                    if w == 7:
                        front_d(n)
                    if w == 9:
                        xt_lo(n)

                def finish_part(n, w):
                    if w == 0:
                        divide(n)
                    if w in (2, 4):
                        scale_heads(n, w - 2)
                        scale_heads(n, w - 1)
                    if w == 7:
                        residual(n)
                    if w == 8:
                        norm2(n)
                    if w == 11:
                        top_two(n)
                    if w == 12:
                        weights(n)
                    if w == 13:
                        places(n)

                for w in range(UNITS):
                    front_part(0, w)
                split_rest()

                def body(i, finish, front):
                    qkv_lo(i)
                    for w in range(UNITS + 3):
                        if w < UNITS:
                            clamp(i, w)
                        if finish:
                            finish_part(i - 1, w)
                        if front:
                            front_part(i + 1, w)
                        if 1 <= w <= UNITS:
                            soft(i, w - 1)
                        if w == 9:
                            take_u(i, 0)
                    take_u(i, 1)

                body(0, False, True)
                body(1, True, True)
                with dve.Fori(2, PAIRS - 1) as i:
                    body(i, True, True)
                body(PAIRS - 1, True, False)
                for w in range(UNITS + 3):
                    finish_part(PAIRS - 1, w)

            @block.tensor
            def _(pe):
                def products(o, terms):
                    for t, (lhs, rhs) in enumerate(terms):
                        last = pe.matmul(o, lhs, rhs, start=(t == 0), stop=(t == len(terms) - 1))
                    return last

                def tok_tiles(n, tiles):
                    if 0 in tiles:
                        pe.wait_ge(x_stacked, n * 32 + 32)
                        pe.wait_ge(xl_made, n + 1)
                    need(pe, v_made, 4 * n - (2 if 0 in tiles else 0))
                    for k in tiles:
                        o = work[k // 2][:T, (k % 2) * D:(k % 2) * D + D]
                        last = products(o, [(patches(a, k, f), m[:STACK + (1 if f == 0 else 0), f, :])
                                            for f in range(TAPS) for a, m in ((xa, mel_wa), (xb, mel_wb))])
                    last.then_inc(tok_done, 1)

                def turn(n, src, signal):
                    for c in range(CT):
                        for k in range(TILES):
                            last = pe.transpose(work[c][:, k * T:k * T + T], src[:T, k, c * P:c * P + P], ident[:T, :T])
                        last.then_inc(signal, 1)

                def front_part(n, w, finish):
                    if w == 0:
                        tok_tiles(n, (0, 1))
                    if w == 1:
                        tok_tiles(n, (2,))
                    if w == 8:
                        pe.wait_ge(xn_made, n + 1)
                        if finish:
                            pe.wait_ge(h1_made, n - 1)
                        turn(n, xn, xt_done)

                def finish_part(n, w, front):
                    if w == 2:
                        pe.wait_ge(rden_made, n + 1)
                    if w in (2, 4):
                        for g in (w - 2, w - 1):
                            if g >= 2:
                                pe.wait_ge(attn_made, n * 4 + g - 1)
                            pe.matmul(work[g % 2][:, 0:NP], pick[:, g, :], rden[:], start=True,
                                      stop=True).then_inc(spread_done, 1)
                    if w == 6:
                        pe.wait_ge(al_made, n * 4 + 4)
                        for k in range(TILES):
                            o = work[k // 2][:T, (k % 2) * D:(k % 2) * D + D]
                            sl = slice(k * T, k * T + T)
                            last = products(o, [(one_rows[:, :], p_bias[:])] +
                                            [(a[:, g, sl], wt[:, g, :]) for g in range(4)
                                             for a, wt in ((ah, p_wh), (al, p_wh), (ah, p_wl))])
                            if k:
                                last.then_inc(proj_done, 1)
                    if w == 10:
                        pe.wait_ge(xn2_made, n + 1)
                        if front:
                            pe.wait_ge(xtl_made, n * 2 + 6)
                        turn(n, xn2, x2t_done)
                    if w == 11:
                        pe.wait_ge(x2t_made, n * 2 + 2)
                        for k in range(TILES):
                            last = products(work[0][:T, k * E:k * E + E],
                                            [(x2t[:, c, k * T:k * T + T], wr[:, c, :]) for c in range(CT)])
                        last.then_inc(logits_done, 1)
                    if w == 13:
                        pe.wait_ge(hot_made, n + 1)
                        for k in range(TILES):
                            last = products(work[1][:T, k * E:k * E + E],
                                            [(before[:T, :], hot_b[:T, k, :])] +
                                            [(ones_b[:T, :], hot_b[:T, j, :]) for j in range(k)] +
                                            [(ones_b[:T, :], seen_b[:T, :])])
                        last.then_inc(rank_done, 1)

                def qkv(n):
                    pe.wait_ge(xtl_made, n * 2 + 2)
                    for s in range(4):
                        if s == 1:
                            need(pe, rank_read, n - 1)
                        if s >= 2:
                            pe.wait_ge(qk_lo, n * 4 + s - 1)
                        products(work[s % 2][:, 0:NP],
                                 [(wt[:, c, s * P:s * P + P], xt[:, c, 0:NP])
                                  for c in range(CT) for wt, xt in ((qk_wh, xth), (qk_wh, xtl), (qk_wl, xth))]
                                 ).then_inc(qkv_done, 1)
                    for b in range(2):
                        pe.wait_ge(qk_lo, n * 4 + 3 + b)
                        for kt in range(2):
                            a = keys(b, kt)
                            last = products(work[b][:, kt * D:kt * D + D],
                                            [(xt[:, c, a:a + P], wt[:, c, :])
                                             for c in range(CT) for xt, wt in ((xth, v_wh), (xtl, v_wh), (xth, v_wl))])
                        last.then_inc(qkv_done, 1)

                def scores(n, w):
                    ct, b, part = unit(w)
                    s = 2 * (w % 2)
                    need(pe, max_done, n * UNITS + w - 1)
                    if w == 0:
                        pe.wait_ge(qk_lo, n * 4 + 4)
                        pe.wait_ge(q_spread, n * (16 * HT) + 16 * HT)
                    a = keys(b, part // 2)
                    for j in range(2 if part < 2 else 1):
                        h = part * 4 + 2 * j
                        if part < 2:
                            rhs = [q_diag[:, h:h + 2, x_, ct, b * N:b * N + N] for x_ in range(2)]
                            o = score[:, s + j, 0:2 * N].rearrange("p (h q) -> p h q", h=2)
                        else:
                            rhs = [q_diag[:, :, x_, ct, b * N + K0:b * N + N] for x_ in range(2)]
                            o = score[:, s, 0:HT * K1].rearrange("p (h q) -> p h q", h=HT)
                        last = products(o, [(kh[:, ct, a:a + P], rhs[0]), (kh[:, ct, a:a + P], rhs[1]),
                                            (kl[:, ct, a:a + P], rhs[0])])
                    last.then_inc(scores_done, 1)

                def weigh(n, w):
                    ct, b, part = unit(w)
                    buf = probs[w % RING]
                    if w == 0:
                        pe.wait_ge(v_made, n * 4 + 4)
                        need(pe, u_made, 4 * n)
                    if w == 6:
                        pe.wait_ge(u_made, n * 4 + 2)
                    wait_apart(pe, causal_done, n * UNITS + w + 1, pe_passed)
                    if part < 2:
                        for j in range(4):
                            last = pe.matmul(heads_out[part][32 * j:32 * j + 32, b * N:b * N + N],
                                             v[:, b, 0, HT * ct + 4 * part + j, :], buf[:, j * N:j * N + N],
                                             start=True, stop=False, skip_group_check=True)
                    else:
                        for g in range(2):
                            for j in range(4):
                                h = 4 * g + j
                                last = pe.matmul(heads_out[g][32 * j:32 * j + 32, b * N + K0:b * N + N],
                                                 v[0:K1, b, 1, HT * ct + h, :], buf[0:K1, h * K1:h * K1 + K1],
                                                 start=False, stop=True, skip_group_check=True)
                    last.then_inc(pv_done, 1)

                pe.wait_ge(dve_setup, 14)
                pe.wait_ge(setup_moved, 160)
                for w in range(UNITS):
                    front_part(0, w, False)
                pe.wait_ge(rest_split, 2)
                pe.wait_ge(q_cleared, 1)

                def body(i, finish, front):
                    qkv(i)
                    for w in range(UNITS + 3):
                        if w < UNITS:
                            scores(i, w)
                        if finish:
                            if w == 2:
                                if front:
                                    pe.wait_ge(raw_made, i * 2 + 4)
                                else:
                                    pe.wait_ge(v_made, i * 4 + 4)
                            finish_part(i - 1, w, front)
                        if front:
                            front_part(i + 1, w, finish)
                        if w >= 3:
                            weigh(i, w - 3)

                body(0, False, True)
                body(1, True, True)
                with pe.Fori(2, PAIRS - 1) as i:
                    body(i, True, True)
                body(PAIRS - 1, True, False)
                pe.wait_ge(rank_read, PAIRS - 1)
                for w in range(UNITS + 3):
                    finish_part(PAIRS - 1, w, False)

        with ExitStack() as mem:
            def sb(name, shape, dt=F32):
                return mem.enter_context(nc.sbuf_tensor(name, shape, dt))

            def bank(name):
                return mem.enter_context(nc.psum_tensor(name, [P, 512], F32))

            turned = [bank(f"turned{i}") for i in range(2)]
            inner = [bank(f"inner{i}") for i in range(4)]
            rows = [bank(f"rows{i}") for i in range(2)]

            ident2 = sb("ident2", [P, P])
            lists_sb = [sb(f"lists{i}", [P, STILES, 2]) for i in range(2)]
            got = [sb(f"got{i}", [P, STILES, D]) for i in range(2)]
            w1 = sb("w1", [P, CT, INNER])
            w2 = sb("w2", [P, ITILES, D])
            w1h = [sb(f"w1h{i}", [P, CT, INNER], F32R) for i in range(2)]
            w1l = [sb(f"w1l{i}", [P, CT, INNER], F32R) for i in range(2)]
            w2h = [sb(f"w2h{i}", [P, ITILES, D], F32R) for i in range(2)]
            w2l = [sb(f"w2l{i}", [P, ITILES, D], F32R) for i in range(2)]
            gth = sb("gth", [P, 2, CT, HALF], F32R)
            gtl = sb("gtl", [P, 2, CT, HALF], F32R)
            hh = sb("hh", [P, ITILES, HALF], F32R)
            hl = sb("hl", [P, ITILES, HALF], F32R)
            y = sb("y", [P, STILES, D])
            ROUND = ITILES // 2

            lists_loaded = [sem("lists_loaded0"), sem("lists_loaded1")]
            gathered = [sem("gathered0"), sem("gathered1")]
            w_here = sem("w_here")
            w_hi = sem("w_hi")
            w_lo = sem("w_lo")
            id_made = sem("id_made")
            got_clear = sem("got_clear")
            turned_done = sem("turned_done")
            gt_hi = sem("gt_hi")
            gt_lo = sem("gt_lo")
            inner_done = sem("inner_done")
            inner_hi = sem("inner_hi")
            inner_lo = sem("inner_lo")
            rows_done = sem("rows_done")
            y_made = sem("y_made")
            added = sem("added")
            pool_passed = sem("pool_passed_too")
            HT2 = STILES // 2

            block = mem.enter_context(nc.Block())

            @block.sync
            def _(sp):
                def load(n, m, lists_at, w1_at, w2_at):
                    if m["added"] is not None:
                        sp.wait_ge(added, m["added"])
                    sp.dma_start(lists_sb[n % 2][:S], lists_at).then_inc(lists_loaded[n % 2], 16)
                    if m["lo"] is not None:
                        sp.wait_ge(w_lo, m["lo"])
                    sp.dma_start(w1[:], w1_at).then_inc(w_here, 16)
                    sp.dma_start(w2[:], w2_at).then_inc(w_here, 16)

                for n in range(2):
                    load(n, dict(added=None, lo=2 * n or None), table_experts[n], w_in_v[n], w_out_v[n])
                with sp.Fori(0, E // 2 - 1) as step:
                    e = step * 2
                    at = [(dict(added=sp.snap(e * (16 * STILES) + 16 * STILES * (b + 1)), lo=sp.snap(e * 2 + 2 * (b + 2))),
                           table_experts[bass.ds(e + (2 + b), 1)].rearrange("e t s w -> (e t) s w"),
                           w_in_v[bass.ds(e + (2 + b), 1)].rearrange("e p c i -> (e p) c i"),
                           w_out_v[bass.ds(e + (2 + b), 1)].rearrange("e p t d -> (e p) t d")) for b in range(2)]
                    for b in range(2):
                        load(b, *at[b])

            @block.gpsimd
            def _(pool):
                pool.memset(ident2[:], 0.0).then_inc(id_made, 1)
                pool.wait_ge(id_made, 1)
                pool.affine_select(out=ident2[:], in_=ident2[:], compare_op=ALU.not_equal, fill=1.0, base=0,
                                   pattern=[[-1, P]], channel_multiplier=1).then_inc(id_made, 1)
                for b in range(2):
                    pool.memset(got[b][:], 0.0).then_inc(got_clear, 1)
                pool.wait_ge(got_clear, 2)

                def gather(m, b):
                    pool.wait_ge(lists_loaded[b], m * 16 + 16)
                    wait_apart(pool, turned_done, m * 8 + (4 * b - 4), pool_passed)
                    for s in range(STILES):
                        pool.indirect_dma_start(
                            out=got[b][:S, s, :], out_offset=None, in_=tokens_dram[:, :],
                            in_offset=bass.IndirectOffsetOnAxis(ap=lists_sb[b][:S, s, 0:1].bitcast(U32), axis=0),
                            bounds_check=TOKENS - 1, oob_is_err=False).then_inc(gathered[b], 16)

                def add(n, b):
                    need(pool, added, n * (16 * STILES))
                    for s in range(STILES):
                        wait_apart(pool, y_made, n * STILES + s + 1, pool_passed)
                        pool.indirect_dma_start(
                            out=out[:, :],
                            out_offset=bass.IndirectOffsetOnAxis(ap=lists_sb[b][:S, s, 0:1].bitcast(U32), axis=0),
                            in_=y[:S, s, :], in_offset=None, bounds_check=TOKENS - 1, oob_is_err=False,
                            compute_op=ALU.add).then_inc(added, 16)

                gather(0, 0)
                gather(0, 1)
                add(0, 0)
                gather(1, 0)
                add(1, 1)
                gather(1, 1)
                add(2, 0)
                with pool.Fori(1, E // 2 - 1) as step:
                    e = step * 2
                    gather(step + 1, 0)
                    add(e + 1, 1)
                    gather(step + 1, 1)
                    add(e + 2, 0)
                add(E - 1, 1)
                pool.wait_ge(added, 16 * STILES * E)

            @block.scalar
            def _(act):
                act.preload_act_table_set("natural_log_exp_and_others")

                def weights_hi(n, b):
                    act.wait_ge(w_here, n * 32 + 32)
                    need(act, rows_done, (n - 1) * STILES)
                    act.activation(w1h[b][:], w1[:], ACT.Copy).then_inc(w_hi, 1)
                    act.activation(w2h[b][:], w2[:], ACT.Copy).then_inc(w_hi, 1)

                def tokens_hi(n):
                    for a in range(2):
                        for c in range(CT):
                            act.wait_ge(turned_done, n * 4 + a * 2 + c + 1)
                            if a == 0 and c == 0:
                                need(act, inner_done, n * (2 * ITILES))
                            act.activation(gth[:, a, c, :], turned[c][:, 0:HALF], ACT.Copy).then_inc(gt_hi, 1)

                def relu_hi(n, a):
                    for t in range(ITILES):
                        act.wait_ge(inner_done, n * (2 * ITILES) + a * ITILES + t + 1)
                        if t == 0:
                            need(act, rows_done, n * STILES + a * HT2)
                        act.activation(hh[:, t, :], inner[t % 4][:, 0:HALF], ACT.Relu).then_inc(inner_hi, 1)

                def expert(n, b, prepare):
                    relu_hi(n, 0)
                    if prepare:
                        weights_hi(n + 1, 1 - b)
                    relu_hi(n, 1)
                    if prepare:
                        tokens_hi(n + 1)

                weights_hi(0, 0)
                tokens_hi(0)
                expert(0, 0, True)
                expert(1, 1, True)
                with act.Fori(1, E // 2 - 1) as step:
                    e = step * 2
                    expert(e, 0, True)
                    expert(e + 1, 1, True)
                expert(E - 2, 0, True)
                expert(E - 1, 1, False)

            @block.vector
            def _(dve):
                def weights_lo(n, b):
                    dve.wait_ge(w_hi, n * 2 + 2)
                    dve.tensor_tensor(w1l[b][:], w1[:], w1h[b][:].bitcast(F32), ALU.subtract).then_inc(w_lo, 1)
                    dve.tensor_tensor(w2l[b][:], w2[:], w2h[b][:].bitcast(F32), ALU.subtract).then_inc(w_lo, 1)

                def tokens_lo(n):
                    for a in range(2):
                        for c in range(CT):
                            dve.wait_ge(gt_hi, n * 4 + a * 2 + c + 1)
                            dve.tensor_tensor(gtl[:, a, c, :], turned[c][:, 0:HALF], gth[:, a, c, :].bitcast(F32),
                                              ALU.subtract).then_inc(gt_lo, 1)

                def relu_lo(n, a):
                    for t in range(ITILES):
                        dve.wait_ge(inner_hi, n * (2 * ITILES) + a * ITILES + t + 1)
                        dve.scalar_tensor_tensor(out=hl[:, t, :], in0=inner[t % 4][:, 0:HALF], scalar=0.0,
                                                 in1=hh[:, t, :].bitcast(F32), op0=ALU.max,
                                                 op1=ALU.subtract).then_inc(inner_lo, 1)

                def take_rows(n, b, a):
                    for s in range(a * HT2, a * HT2 + HT2):
                        dve.wait_ge(rows_done, n * STILES + s + 1)
                        need(dve, added, n * (16 * STILES) - 16 * STILES + 16 * STILES)
                        dve.tensor_scalar(y[:S, s, :], rows[s % 2][:S, 0:D], lists_sb[b][:S, s, 1:2], None,
                                          ALU.mult).then_inc(y_made, 1)

                def expert(n, b, prepare):
                    relu_lo(n, 0)
                    take_rows(n, b, 0)
                    if prepare:
                        weights_lo(n + 1, 1 - b)
                    relu_lo(n, 1)
                    if prepare:
                        tokens_lo(n + 1)
                    take_rows(n, b, 1)

                weights_lo(0, 0)
                tokens_lo(0)
                expert(0, 0, True)
                expert(1, 1, True)
                with dve.Fori(1, E // 2 - 1) as step:
                    e = step * 2
                    expert(e, 0, True)
                    expert(e + 1, 1, True)
                expert(E - 2, 0, True)
                expert(E - 1, 1, False)

            @block.tensor
            def _(pe):
                def turn(n, b):
                    for a in range(2):
                        for c in range(CT):
                            if a == 0 and c == 0:
                                pe.wait_ge(gathered[b], n * (8 * STILES) + (16 - 8 * b) * STILES)
                            need(pe, gt_lo, n * 4 + a * 2 + c - 1)
                            for s in range(HT2):
                                last = pe.transpose(turned[c][:, s * S:s * S + S],
                                                    got[b][:S, a * HT2 + s, c * P:c * P + P], ident2[:S, :S])
                            last.then_inc(turned_done, 1)

                def first(n, b, a):
                    if a == 0:
                        pe.wait_ge(w_lo, n * 2 + 2)
                    pe.wait_ge(gt_lo, n * 4 + a * 2 + 2)
                    for t in range(ITILES):
                        need(pe, inner_lo, n * (2 * ITILES) + a * ITILES + t - 3)
                        k = 0
                        for c in range(CT):
                            for w_, g_ in ((w1h, gth), (w1h, gtl), (w1l, gth)):
                                last = pe.matmul(inner[t % 4][:, 0:HALF], w_[b][:, c, t * P:t * P + P], g_[:, a, c, :],
                                                 start=(k == 0), stop=(k == 3 * CT - 1))
                                k += 1
                        last.then_inc(inner_done, 1)

                def second(n, b, a):
                    for s in range(a * HT2, a * HT2 + HT2):
                        need(pe, y_made, n * STILES + s - 1)
                        if s == a * HT2:
                            pe.wait_ge(inner_lo, n * (2 * ITILES) + (a + 1) * ITILES)
                        at = (s - a * HT2) * S
                        k = 0
                        for t in range(ITILES):
                            for h_, w_ in ((hh, w2h), (hl, w2h), (hh, w2l)):
                                last = pe.matmul(rows[s % 2][:S, 0:D], h_[:, t, at:at + S], w_[b][:, t, :],
                                                 start=(k == 0), stop=(k == 3 * ITILES - 1))
                                k += 1
                        last.then_inc(rows_done, 1)

                pe.wait_ge(id_made, 2)
                turn(0, 0)

                def expert(n, b, prepare):
                    first(n, b, 0)
                    second(n, b, 0)
                    first(n, b, 1)
                    if prepare:
                        turn(n + 1, 1 - b)
                    second(n, b, 1)

                expert(0, 0, True)
                expert(1, 1, True)
                with pe.Fori(1, E // 2 - 1) as step:
                    e = step * 2
                    expert(e, 0, True)
                    expert(e + 1, 1, True)
                expert(E - 2, 0, True)
                expert(E - 1, 1, False)


def kernel(x, L0_tok_W, L0_tok_b, L0_tok_gamma, L0_tok_beta, L0_attn_w_qkv, L0_attn_w_proj, L0_attn_b_proj,
           L0_ffn_W_router, L0_ffn_b_router, L0_ffn_experts_inter, L0_ffn_experts_out):
    import numpy as np
    import concourse.bacc as bacc
    from concourse.bass_utils import run_bass_kernel_spmd

    D = L0_tok_W.shape[1]
    mels = x.shape[1]
    taps = L0_tok_W.shape[0] // mels
    w_qkv = np.asarray(L0_attn_w_qkv)
    w_proj = np.asarray(L0_attn_w_proj)
    heads, hs = 16, D // 16
    wp_t = np.zeros((heads, 2 * hs, D), w_proj.dtype)
    wp_t[:, :hs, :] = w_proj.T.reshape(heads, hs, D)
    given = {
        "x": np.asarray(x),
        "tok_w": np.asarray(L0_tok_W).reshape(mels, taps, D),
        "tok_b": np.asarray(L0_tok_b).reshape(1, D),
        "gamma": np.asarray(L0_tok_gamma),
        "beta": np.asarray(L0_tok_beta),
        "wqk_t": np.ascontiguousarray(w_qkv[:2 * D].T),
        "wv_t": np.ascontiguousarray(w_qkv[2 * D:].T),
        "wp_t": wp_t.reshape(heads * 2 * hs, D),
        "b_proj": np.asarray(L0_attn_b_proj).reshape(1, D),
        "wr_t": np.ascontiguousarray(np.asarray(L0_ffn_W_router).T),
        "b_router": np.asarray(L0_ffn_b_router),
        "w_in": np.asarray(L0_ffn_experts_inter),
        "w_out": np.asarray(L0_ffn_experts_out),
    }
    batches, _, frames = given["x"].shape
    tokens = (frames - taps) // (taps // 2) + 1
    experts = given["w_in"].shape[0]
    nc = bacc.Bacc("TRN2", target_bir_lowering=False, num_devices=1)
    arrays = {f"in_{k}": np.ascontiguousarray(a) for k, a in given.items()}
    args = [nc.dram_tensor(k, a.shape, mybir.dt.from_np(a.dtype), kind="ExternalInput").ap() for k, a in arrays.items()]
    out = nc.dram_tensor("out", (batches * tokens, D), F32, kind="ExternalOutput").ap()
    tokens_dram = nc.dram_tensor("tokens", (batches * tokens, D), F32, kind="Internal").ap()
    table_dram = nc.dram_tensor("table", (experts * 8 * 117, 2), F32, kind="Internal").ap()
    audio_tower(nc, *args, out, tokens_dram, table_dram)
    r = run_bass_kernel_spmd(nc, [arrays], core_ids=[0])
    return r.results[0]["out"].reshape(batches, tokens, D)
```

```python
from contextlib import ExitStack

import concourse.bass as bass
from concourse import mybir

ALU = mybir.AluOpType
ACT = mybir.ActivationFunctionType
AX = mybir.AxisListType
F32 = mybir.dt.float32
F32R = mybir.dt.float32r
BF16 = mybir.dt.bfloat16
I32 = mybir.dt.int32
U32 = mybir.dt.uint32

P = 128
EPS = 1e-5
DEN_EPS = 1e-9
LN_MAX = 2.0 ** 60


def words(ap):
    return ap.bitcast(F32)


def need(eng, sem, value):
    if isinstance(value, int) and value <= 0:
        return
    eng.wait_ge(sem, value)


def wait_apart(eng, sem, value, passed):
    if isinstance(value, int):
        return need(eng, sem, value)
    eng.wait_ge(sem, value)
    eng.sem_inc(passed, 1)


def audio_tower(nc, x, tok_w, tok_b, gamma, beta, wqk_t, wv_t, wp_t, b_proj, wr_t, b_router, w_in, w_out,
                out, tokens_dram, table_dram):
    B, MELS, FRAMES = x.shape
    D = tok_w.shape[2]
    TAPS = tok_w.shape[1]
    HOP = TAPS // 2
    N = (FRAMES - TAPS) // HOP + 1
    PAIRS = B // 2
    NP = 2 * N
    T = 124
    TILES = NP // T
    TOKENS = B * N
    CT = D // P
    HEADS, HS = 16, D // 16
    HT = P // HS
    K0 = P
    K1 = N - K0
    E, INNER = w_in.shape[0], w_in.shape[2]
    CAP = -(-(TOKENS * 5) // (E * 4))
    S = 117
    STILES = 8
    SLOTS = S * STILES
    ITILES = INNER // P
    HALF = SLOTS // 2
    BIG = float(1 << 20)
    SCALE = HS ** -0.5
    STACK = MELS + MELS // 2
    BATCH_COLS = N * HOP
    MID = BATCH_COLS + BATCH_COLS + HOP
    MID_HALF = HOP * T // 2
    XCOLS = MID + 2 * MID_HALF
    assert TAPS == 2 * HOP and TILES == 3 and N - T == T // 2
    UNITS = 12
    LOOP_FROM, LOOP_TO = 4, (PAIRS - 3) // 2 * 2
    assert TILES * T == NP and SLOTS >= CAP and HALF <= 512 and CAP * E * 4 >= TOKENS * 5

    out_pairs = out.rearrange("(p k t) d -> p t k d", k=TILES, t=T)
    tokens_pairs = tokens_dram.rearrange("(p k t) d -> p t k d", k=TILES, t=T)
    table_experts = table_dram.rearrange("(e s t) w -> e t s w", e=E, s=STILES)
    w_in_v = w_in.rearrange("e (c p) i -> e p c i", p=P)
    w_out_v = w_out.rearrange("e (t p) d -> e p t d", p=P)

    with ExitStack() as ctx:
        sems = {}

        def sem(name):
            sems[name] = ctx.enter_context(nc.semaphore(name))
            return sems[name]

        with ExitStack() as mem:
            def sb(name, shape, dt=F32):
                return mem.enter_context(nc.sbuf_tensor(name, shape, dt))

            def bank(name):
                return mem.enter_context(nc.psum_tensor(name, [P, 512], F32))

            score = mem.enter_context(nc.psum_tensor("score", [P, 4, 512], F32))
            heads_out = [bank(f"heads_out{i}") for i in range(2)]
            work = [bank(f"work{i}") for i in range(2)]

            ASIDE = NP + 12

            ident = sb("ident", [P, P])
            pick = sb("pick", [P, 4, P])
            before_f = sb("before_f", [P, T])
            before = sb("before", [P, T], BF16)
            ones_b = sb("ones_b", [P, T], BF16)
            expert_id = sb("expert_id", [P, E])
            token_id = sb("token_id", [P, TILES])
            mel_wa = sb("mel_wa", [P, TAPS, D], F32R)
            mel_wb = sb("mel_wb", [P, TAPS, D], F32R)
            bias_raw = sb("bias_raw", [1, 2, D])
            qk_wh = sb("qk_wh", [P, CT, 2 * D], F32R)
            qk_wl = sb("qk_wl", [P, CT, 2 * D], F32R)
            v_wh = sb("v_wh", [P, CT, D], F32R)
            v_wl = sb("v_wl", [P, CT, D], F32R)
            p_wh = sb("p_wh", [P, 4, D], F32R)
            p_wl = sb("p_wl", [P, 4, D], F32R)
            p_bias = sb("p_bias", [P, D], F32R)
            one_rows = sb("one_rows", [P, T], F32R)
            wr = sb("wr", [P, CT, E])
            br = sb("br", [P, E])
            gam = sb("gam", [P, D])
            bet = sb("bet", [P, D])

            xraw = sb("xraw", [P, XCOLS])
            xa = sb("xa", [P, XCOLS], F32R)
            xb = sb("xb", [P, XCOLS], F32R)
            h0 = sb("h0", [P, TILES, D])
            h0_next = sb("h0_next", [P, TILES, D])
            h0_kept = sb("h0_kept", [P, TILES, D])
            xn = sb("xn", [P, TILES, D])
            stats = sb("stats", [P, TILES, 6])
            mv = sb("mv", [P, TILES, 2])
            ve = sb("ve", [P, TILES])
            lnv = sb("lnv", [P, TILES])
            ra = sb("ra", [P, TILES])
            rb = sb("rb", [P, TILES])
            rc = sb("rc", [P, TILES])
            rstd = sb("rstd", [P, TILES])
            KPAD = N + K0 + P
            xth = sb("xth", [P, CT, KPAD], F32R)
            xtl = sb("xtl", [P, CT, KPAD], F32R)
            q_hl = sb("q_hl", [P, 2, CT, NP], F32R)
            q_diag = sb("q_diag", [P, HT, 2, CT, NP], F32R)
            kh = sb("kh", [P, CT, KPAD], F32R)
            kl = sb("kl", [P, CT, KPAD], F32R)
            v = [sb(f"v{i}", [P, 2, 2, HEADS, 2 * HS]) for i in range(2)]
            RING = 4
            probs_all = sb("probs_all", [P, RING, 4 * N])
            probs = [probs_all[:, i, :] for i in range(RING)]
            stage = probs_all[:].rearrange("p r q -> p (r q)")[:, 0:TAPS * D]
            flat = q_diag[:].rearrange("p h s c q -> p (h s c q)")
            mel_wl = flat[:, 0:TAPS * D].rearrange("p (f d) -> p f d", f=TAPS)
            one_line = flat[0:1, TAPS * D:TAPS * D + XCOLS]
            bias_at = TAPS * D + XCOLS
            bias_hl = flat[0:1, bias_at:bias_at + 2 * D].rearrange("p (s d) -> p s d", s=2)
            p_bias_hl = flat[0:1, bias_at + 2 * D:bias_at + 4 * D].rearrange("p (s d) -> p s d", s=2)
            u = sb("u", [P, 4, NP])
            DEN_CUT = 6
            den = sb("den", [HEADS * DEN_CUT, NP // DEN_CUT])
            den_eps = sb("den_eps", [HEADS * DEN_CUT, NP // DEN_CUT])
            den_inv = sb("den_inv", [HEADS * DEN_CUT, NP // DEN_CUT])
            rden = sb("rden", [P, NP])
            ah = sb("ah", [P, 4, NP], F32R)
            al = sb("al", [P, 4, NP], F32R)
            h1 = sb("h1", [P, TILES, D])
            xn2 = sb("xn2", [P, TILES, D])
            stats2 = sb("stats2", [P, TILES, 6])
            mv2 = sb("mv2", [P, TILES, 2])
            ve2 = sb("ve2", [P, TILES])
            lnv2 = sb("lnv2", [P, TILES])
            ra2 = sb("ra2", [P, TILES])
            rb2 = sb("rb2", [P, TILES])
            rc2 = sb("rc2", [P, TILES])
            rstd2 = sb("rstd2", [P, TILES])
            x2t = sb("x2t", [P, CT, NP])
            lg = sb("lg", [P, TILES, E])
            top = sb("top", [P, TILES, 8])
            top_at = sb("top_at", [P, TILES, 8], U32)
            topd = sb("topd", [P, TILES, 8])
            tope = sb("tope", [P, TILES, 8])
            tsum = sb("tsum", [P, TILES])
            trec = sb("trec", [P, TILES])
            at_f = sb("at_f", [P, TILES, 2])
            valid = sb("valid", [P, 2, TILES])
            hot = sb("hot", [P, 2, TILES, E])
            hot_b = sb("hot_b", [P, TILES, E], BF16)
            seen = [sb(f"seen{i}", [P, E]) for i in range(TILES + 1)]
            seen_b = sb("seen_b", [P, E], BF16)
            rank = sb("rank", [P, TILES, E])
            mine = sb("mine", [P, 2, TILES, E])
            place = sb("place", [P, 2, TILES])
            over = sb("over", [P, 2, TILES])
            place2 = sb("place2", [P, 2, TILES])
            place_i = sb("place_i", [P, 2, TILES], U32)
            entry = sb("entry", [P, 2, TILES, 2])
            blank = sb("blank", [96, 2 * E * SLOTS // 96], I32)

            w_loaded = sem("w_loaded")
            w_stage_free = sem("w_stage_free")
            dve_setup = sem("dve_setup")
            pool_setup = sem("pool_setup")
            setup_moved = sem("setup_moved")
            x_loaded = sem("x_loaded")
            xh_made = sem("xh_made")
            xl_made = sem("xl_made")
            x_stacked = sem("x_stacked")
            tok_done = sem("tok_done")
            ln_var = sem("ln_var")
            ln_guess = sem("ln_guess")
            xhat_made = sem("xhat_made")
            h0_made = sem("h0_made")
            xn_made = sem("xn_made")
            xt_done = sem("xt_done")
            xth_made = sem("xth_made")
            xtl_made = sem("xtl_made")
            qk_done = sem("qk_done")
            v_done = sem("v_done")
            qk_hi = sem("qk_hi")
            qk_lo = sem("qk_lo")
            v_made = sem("v_made")
            q_spread = [sem(f"q_spread{c}") for c in range(CT)]
            scores_done = sem("scores_done")
            exp_done = sem("exp_done")
            clamp_done = sem("clamp_done")
            ln_done = sem("ln_done")
            max_done = sem("max_done")
            square_done = sem("square_done")
            causal_done = sem("causal_done")
            pv_done = sem("pv_done")
            u_made = sem("u_made")
            den_moved = sem("den_moved")
            inv_made = sem("inv_made")
            rden_moved = sem("rden_moved")
            spread_done = sem("spread_done")
            attn_made = sem("attn_made")
            ah_made = sem("ah_made")
            al_made = sem("al_made")
            proj_done = sem("proj_done")
            h1_made = sem("h1_made")
            ln2_var = sem("ln2_var")
            ln2_guess = sem("ln2_guess")
            xn2_made = sem("xn2_made")
            h1_stored = sem("h1_stored")
            tokens_stored = sem("tokens_stored")
            x2t_done = sem("x2t_done")
            x2t_made = sem("x2t_made")
            logits_done = sem("logits_done")
            top_ready = sem("top_ready")
            top_exp = sem("top_exp")
            hot_made = sem("hot_made")
            rank_done = sem("rank_done")
            rank_read = sem("rank_read")
            place_made = sem("place_made")
            listed = sem("listed")
            own = sem("own")
            front_own = sem("front_own")
            divide_own, residual_own, norm2_own, top_own, weights_own, places_own = (
                sem(f"{part}_own") for part in ("divide", "residual", "norm2", "top", "weights", "places"))
            table_blank = sem("table_blank")
            pool_passed = sem("pool_passed")
            dve_passed = sem("dve_passed")
            pe_passed = sem("pe_passed")
            sp_passed = sem("sp_passed")
            rest_split = sem("rest_split")
            q_cleared = sem("q_cleared")
            raw_made = sem("raw_made")
            h0_scaled = sem("h0_scaled")
            h0_next_moved = sem("h0_next_moved")
            h0_kept_moved = sem("h0_kept_moved")

            def here(n):
                return not isinstance(n, int) or 0 <= n < PAIRS

            def upto(value, most):
                return min(value, most) if isinstance(value, int) else value

            def behind(i, w, lag):
                return (i, w - lag) if w >= lag else (i - 1, w - lag + UNITS)

            def walk(eng, body):
                for i in range(-2, LOOP_FROM):
                    body(i, i % 2)
                with eng.Fori(LOOP_FROM // 2, LOOP_TO // 2) as half:
                    body(half * 2, 0)
                    body(half * 2 + 1, 1)
                for i in range(LOOP_TO, PAIRS + 3):
                    body(i, i % 2)

            def keys(b, kt):
                return b * N + kt * K0

            def unit(w):
                return w // 6, w // 3 % 2, w % 3

            def patches(t, k, f):
                rows = STACK + 1 if f == 0 else STACK
                at = MID + f - HOP if k == 1 and f >= HOP else HOP * T * k + f
                return t[:rows, at:at + HOP * (T - 1) + 1:HOP]

            def frames(n):
                if isinstance(n, int):
                    src = x[2 * n], x[2 * n + 1]
                else:
                    src = [x[bass.ds(2 * n + b, 1)].rearrange("b m t -> (b m) t") for b in range(2)]
                return [(xraw[:MELS, 0:BATCH_COLS], src[0][:, 0:BATCH_COLS]),
                        (xraw[:MELS, BATCH_COLS:MID], src[1][:, 0:BATCH_COLS + HOP]),
                        (xraw[:MELS, MID:MID + MID_HALF], src[0][:, HOP * (T + 1):HOP * (T + 1) + MID_HALF]),
                        (xraw[:MELS, MID + MID_HALF:XCOLS], src[1][:, HOP:HOP + MID_HALF])]

            block = mem.enter_context(nc.Block())

            @block.sync
            def _(sp):
                sp.dma_start(stage[:MELS, :], tok_w.rearrange("m f d -> m (f d)")).then_inc(w_loaded, 16)
                sp.dma_start(bias_raw[:, 0, :], tok_b).then_inc(w_loaded, 16)
                sp.dma_start(bias_raw[:, 1, :], b_proj).then_inc(w_loaded, 16)
                sp.dma_start(wr[:], wr_t.rearrange("(c p) e -> p c e", p=P)).then_inc(w_loaded, 16)
                sp.dma_start(br[:], b_router.partition_broadcast(P)).then_inc(w_loaded, 16)
                sp.dma_start(gam[:], gamma.partition_broadcast(P)).then_inc(w_loaded, 16)
                sp.dma_start(bet[:], beta.partition_broadcast(P)).then_inc(w_loaded, 16)
                for cols, src in frames(0):
                    sp.dma_start(cols, src).then_inc(x_loaded, 16)
                sp.wait_ge(dve_setup, 4)
                sp.dma_start(words(mel_wa[MELS:STACK, :, :]), words(mel_wl[0:STACK - MELS, :, :])).then_inc(setup_moved, 16)
                sp.dma_start(words(mel_wb[MELS:STACK, :, :]), words(mel_wl[STACK - MELS:MELS, :, :])).then_inc(setup_moved, 16)
                sp.dma_start(words(mel_wa[STACK:STACK + 1, 0, :]), words(bias_hl[:, 0])).then_inc(setup_moved, 16)
                sp.dma_start(words(mel_wb[STACK:STACK + 1, 0, :]), words(bias_hl[:, 1])).then_inc(setup_moved, 16)
                sp.dma_start(words(p_bias[0:1, :]), words(p_bias_hl[:, 0])).then_inc(setup_moved, 16)
                sp.dma_start(words(p_bias[1:2, :]), words(p_bias_hl[:, 1])).then_inc(setup_moved, 16)
                sp.dma_start(words(xa[STACK:STACK + 1, :]), words(one_line)).then_inc(setup_moved, 16)
                sp.dma_start(words(xb[STACK:STACK + 1, :]), words(one_line)).then_inc(setup_moved, 16)
                sp.dma_start(words(one_rows[0:1, :]), words(one_line[:, 0:T])).then_inc(setup_moved, 16)
                sp.dma_start(words(one_rows[1:2, :]), words(one_line[:, 0:T])).then_inc(setup_moved, 16)
                sp.dma_start(stage[:, 0:CT * 2 * D].rearrange("p (c n) -> p c n", c=CT),
                             wqk_t.rearrange("(c p) n -> p c n", p=P)).then_inc(w_loaded, 16)
                sp.wait_ge(pool_setup, 9)
                sp.dma_start(table_dram.rearrange("(p n) w -> p (n w)", p=96).bitcast(I32), blank[:]).then_inc(table_blank, 16)

                def stack(n):
                    h = STACK - MELS
                    sp.wait_ge(xh_made, n)
                    sp.dma_start(words(xa[MELS:STACK, :]), words(xa[0:h, :])).then_inc(x_stacked, 16)
                    sp.dma_start(words(xb[MELS:STACK, :]), words(xa[h:MELS, :])).then_inc(x_stacked, 16)

                def load_x(n2, parts):
                    sp.wait_ge(xl_made, n2)
                    for cols, src in parts:
                        sp.dma_start(cols, src).then_inc(x_loaded, 16)

                def count(value):
                    return value if isinstance(value, int) else sp.snap(value)

                def spread_q(n, ct):
                    wait_apart(sp, qk_lo, n * 4 + 2 * ct + 1, sp_passed)
                    need(sp, scores_done, n * UNITS + 6 * ct - 6)
                    for h in range(HT):
                        sp.dma_start(words(q_diag[HS * h:HS * h + HS, h, :, ct]),
                                     words(q_hl[HS * h:HS * h + HS, :, ct])).then_inc(q_spread[ct], 16)

                def move_den(n):
                    wait_apart(sp, u_made, n * 4 + 4, sp_passed)
                    need(sp, inv_made, n)
                    for g in range(4):
                        h = 4 * g * DEN_CUT
                        sp.dma_start(den[h:h + 4 * DEN_CUT, :], u[HS:P:2 * HS, g, :]).then_inc(den_moved, 16)

                def move_rden(n):
                    wait_apart(sp, inv_made, n + 1, sp_passed)
                    need(sp, spread_done, 4 * n)
                    sp.dma_start(rden[0:HEADS, :], den_inv[:]).then_inc(rden_moved, 16)

                def keep_h0(i):
                    if here(i):
                        if not isinstance(i, int) or i:
                            wait_apart(sp, h1_made, i, sp_passed)
                        sp.wait_ge(h0_next_moved, i * 16 + 16)
                        sp.dma_start(h0_kept[:T], h0_next[:T]).then_inc(h0_kept_moved, 16)
                    if here(i + 1):
                        if here(i):
                            wait_apart(sp, h0_kept_moved, i * 16 + 16, sp_passed)
                        sp.wait_ge(h0_made, i + 2)
                        sp.dma_start(h0_next[:T], h0[:T]).then_inc(h0_next_moved, 16)

                def store_h1(n, at):
                    sp.wait_ge(h1_made, n + 1)
                    sp.dma_start(at, h1[:T]).then_inc(h1_stored, 16)

                def store_tokens(n, at):
                    sp.wait_ge(xn2_made, n + 1)
                    sp.dma_start(at, xn2[:T]).then_inc(tokens_stored, 16)

                def rows_at(a, n):
                    return a[n] if isinstance(n, int) else a[bass.ds(n, 1)].rearrange("p t k d -> (p t) k d")

                def body(i, parity):
                    if here(i - 2):
                        store_tokens(count(i - 2), rows_at(tokens_pairs, i - 2))
                    if here(i - 1):
                        move_den(i - 1)
                    if here(i):
                        spread_q(i, 1)
                    if here(i - 1):
                        move_rden(i - 1)
                    if here(i + 2):
                        stack(count(i + 3))
                    if here(i + 3):
                        load_x(count(2 * i + 6), frames(i + 3))
                    if isinstance(i, int) and i == -1:
                        sp.wait_ge(w_stage_free, 1)
                        sp.dma_start(stage[:, 0:CT * D].rearrange("p (c n) -> p c n", c=CT),
                                     wv_t.rearrange("(c p) n -> p c n", p=P)).then_inc(w_loaded, 16)
                        sp.dma_start(stage[:, CT * D:CT * D + 4 * D].rearrange("p (c n) -> p c n", c=4),
                                     wp_t.rearrange("(c p) n -> p c n", p=P)).then_inc(w_loaded, 16)
                    if here(i + 1):
                        spread_q(i + 1, 0)
                    keep_h0(i)
                    if here(i - 1):
                        store_h1(count(i - 1), rows_at(out_pairs, i - 1))

                walk(sp, body)
                sp.wait_ge(h1_stored, 16 * PAIRS)
                sp.wait_ge(tokens_stored, 16 * PAIRS)

            @block.gpsimd
            def _(pool):
                setup = [0]

                def made(ins, wait=False):
                    setup[0] += 1
                    ins.then_inc(pool_setup, 1)
                    if wait:
                        pool.wait_ge(pool_setup, setup[0])

                made(pool.memset(ident[:], 0.0))
                made(pool.memset(pick[:], 0.0))
                made(pool.memset(before_f[:], 1.0))
                made(pool.memset(blank[:], 1 << 20), True)
                made(pool.affine_select(out=ident[:], in_=ident[:], compare_op=ALU.not_equal, fill=1.0, base=0,
                                        pattern=[[-1, P]], channel_multiplier=1))
                made(pool.affine_select(out=pick[:].rearrange("p g (j d) -> p g j d", j=4),
                                        in_=pick[:].rearrange("p g (j d) -> p g j d", j=4),
                                        compare_op=ALU.not_equal, fill=1.0, base=0,
                                        pattern=[[4, 4], [1, 4], [0, 2 * HS]], channel_multiplier=-1))
                made(pool.affine_select(out=before_f[:], in_=before_f[:], compare_op=ALU.is_gt, fill=0.0, base=0,
                                        pattern=[[1, T]], channel_multiplier=-1))
                made(pool.iota(expert_id[:], pattern=[[1, E]], base=0, channel_multiplier=0,
                               allow_small_or_imprecise_dtypes=True))
                made(pool.iota(token_id[:], pattern=[[T, TILES]], base=0, channel_multiplier=1,
                               allow_small_or_imprecise_dtypes=True))

                def x_lo(n, half):
                    pool.wait_ge(xh_made, n + 1)
                    need(pool, tok_done, 2 * n)
                    cols = slice(half * (XCOLS // 2), (half + 1) * (XCOLS // 2))
                    pool.tensor_tensor(xb[:MELS, cols], xraw[:MELS, cols], xa[:MELS, cols].bitcast(F32),
                                       ALU.subtract).then_inc(xl_made, 1)

                def affine(n):
                    pool.wait_ge(xhat_made, n + 1)
                    need(pool, h0_next_moved, 16 * n)
                    g = gam[:T].rearrange("p (a d) -> p a d", a=1).broadcast_to([T, TILES, D])
                    b = bet[:T].rearrange("p (a d) -> p a d", a=1).broadcast_to([T, TILES, D])
                    pool.tensor_tensor(h0[:T], xn[:T], g, ALU.mult).then_inc(h0_scaled, 1)
                    pool.wait_ge(h0_scaled, n + 1)
                    pool.tensor_tensor(h0[:T], h0[:T], b, ALU.add).then_inc(h0_made, 1)

                def causal(n, w):
                    ct, b, part = unit(w)
                    buf = probs[w % RING]
                    wait_apart(pool, square_done, n * UNITS + w + 1, pool_passed)
                    if part < 2:
                        a = buf.rearrange("p (h q) -> p h q", h=4)[:, :, 0:K0]
                        pattern = [[0, 4], [1, K0]]
                    else:
                        a = buf[0:K1, 0:HT * K1].rearrange("p (h q) -> p h q", h=HT)
                        pattern = [[0, HT], [1, K1]]
                    pool.affine_select(out=a, in_=a, compare_op=ALU.is_ge, fill=0.0, base=0, pattern=pattern,
                                       channel_multiplier=-1).then_inc(causal_done, 1)

                def attn_lo(n, g):
                    pool.wait_ge(ah_made, n * 4 + g + 1)
                    if g == 0:
                        need(pool, proj_done, 2 * n)
                    pool.tensor_tensor(al[:, g, :], u[:, g, :], ah[:, g, :].bitcast(F32), ALU.subtract).then_inc(al_made, 1)

                def lists(n, k):
                    wait_apart(pool, place_made, n + 1, pool_passed)
                    for c in range(2):
                        pool.indirect_dma_start(
                            out=table_dram[:, :],
                            out_offset=bass.IndirectOffsetOnAxis(ap=place_i[:T, c, k:k + 1], axis=0),
                            in_=entry[:T, c, k, :], in_offset=None,
                            bounds_check=E * SLOTS - 1, oob_is_err=False).then_inc(listed, 16)

                def body(i, parity):
                    if isinstance(i, int) and i == -1:
                        pool.wait_ge(setup_moved, 160)
                        pool.memset(q_diag[:].bitcast(F32), 0.0).then_inc(q_cleared, 1)
                    if isinstance(i, int) and i == 3:
                        pool.wait_ge(table_blank, 16)
                    for w in range(UNITS):
                        n, u_ = behind(i, w, 2)
                        if here(n):
                            causal(n, u_)
                        if w == 3 and here(i + 1):
                            affine(i + 1)
                        if w in (5, 6) and here(i + 2):
                            x_lo(i + 2, w - 5)
                        if w in (7, 8) and here(i - 1):
                            attn_lo(i - 1, 2 * w - 14)
                            attn_lo(i - 1, 2 * w - 13)
                        if w in (0, 1, 2) and here(i - 3):
                            lists(i - 3, w)

                walk(pool, body)
                pool.wait_ge(listed, 16 * 2 * TILES * PAIRS)

            @block.scalar
            def _(act):
                act.preload_act_table_set("natural_log_exp_and_others")

                def x_hi(n):
                    act.wait_ge(x_loaded, n * 64 + 64)
                    need(act, tok_done, 2 * n)
                    act.activation(xa[:MELS, :], xraw[:MELS, :], ACT.Copy).then_inc(xh_made, 1)

                def take_tok(n, j):
                    act.wait_ge(tok_done, n * 2 + j + 1)
                    if j == 0:
                        need(act, xt_done, 2 * n)
                    cols = TILES - 2 if j else 2
                    act.activation(xn[:T, 2 * j:2 * j + cols, :].rearrange("p k d -> p (k d)"),
                                   work[j][:T, 0:cols * D], ACT.Copy).then_inc(raw_made, 1)

                def guess(n, second):
                    act.wait_ge(ln_var, n * 2 + second + 1)
                    act.activation(lnv[:T], ve[:T], ACT.Ln).then_inc(ln_guess, 1)
                    act.wait_ge(ln_guess, n * 4 + 2 * second + 1)
                    act.activation(ra[:T], lnv[:T], ACT.Exp, scale=-0.5).then_inc(ln_guess, 1)

                def guess2(n):
                    act.wait_ge(ln2_var, n + 1)
                    act.activation(lnv2[:T], ve2[:T], ACT.Ln).then_inc(ln2_guess, 1)
                    act.wait_ge(ln2_guess, n * 2 + 1)
                    act.activation(ra2[:T], lnv2[:T], ACT.Exp, scale=-0.5).then_inc(ln2_guess, 1)

                def xt_hi(n):
                    for c in range(CT):
                        act.wait_ge(xt_done, n * 2 + c + 1)
                        if c == 1:
                            need(act, logits_done, n - 2)
                        if c == 0:
                            need(act, qk_done, 4 * n)
                        act.activation(xth[:, c, 0:NP], work[c][:, 0:NP], ACT.Copy).then_inc(xth_made, 1)

                def qk_hi_part(n, ct):
                    act.wait_ge(qk_done, n * 4 + 2 * ct + 1)
                    need(act, q_spread[ct], 16 * HT * n)
                    act.activation(q_hl[:, 0, ct, :], work[0][:, 0:NP], ACT.Copy).then_inc(qk_hi, 1)
                    act.wait_ge(qk_done, n * 4 + 2 * ct + 2)
                    need(act, scores_done, UNITS * n + 6 * ct - 6)
                    act.activation(kh[:, ct, 0:NP], work[1][:, 0:NP], ACT.Copy).then_inc(qk_hi, 1)

                def take_v(n, parity):
                    for b in range(2):
                        act.wait_ge(v_done, n * 2 + b + 1)
                        if b == 0:
                            need(act, pv_done, UNITS * (n - 1))
                        for kt, rows in ((0, K0), (1, K1)):
                            act.activation(v[parity][:rows, b, kt, :, 0:HS],
                                           work[b][:rows, kt * D:kt * D + D].rearrange("p (h d) -> p h d", h=HEADS),
                                           ACT.Copy).then_inc(v_made, 1)

                def whole(w):
                    return probs[w % RING] if unit(w)[2] < 2 else probs[w % RING][0:K1, 0:HT * K1]

                def expo(n, w):
                    s = 2 * (w % 2)
                    act.wait_ge(scores_done, n * UNITS + w + 1)
                    need(act, pv_done, n * UNITS + w + 1 - RING)
                    if unit(w)[2] < 2:
                        src, dst = score[:, s:s + 2, 0:2 * N], whole(w).rearrange("p (a q) -> p a q", a=2)
                    else:
                        src, dst = score[0:K1, s, 0:HT * K1], whole(w)
                    act.activation(dst, src, ACT.Exp, scale=SCALE).then_inc(exp_done, 1)

                def loga(n, w):
                    act.wait_ge(clamp_done, n * UNITS + w + 1)
                    act.activation(whole(w), whole(w), ACT.Ln, bias=1.0).then_inc(ln_done, 1)

                def square(n, w):
                    act.wait_ge(max_done, n * UNITS + w + 1)
                    act.activation(whole(w), whole(w), ACT.Square).then_inc(square_done, 1)

                def take_u(n, ct):
                    act.wait_ge(pv_done, n * UNITS + 6 * ct + 6)
                    if ct == 0:
                        need(act, al_made, 4 * n)
                    for j in range(2):
                        act.activation(u[:, 2 * ct + j, :], heads_out[j][:, 0:NP], ACT.Copy).then_inc(u_made, 1)

                def attn_hi(n, g):
                    act.wait_ge(attn_made, n * 4 + g + 1)
                    if g == 0:
                        need(act, proj_done, 2 * n)
                    act.activation(ah[:, g, :], u[:, g, :], ACT.Copy).then_inc(ah_made, 1)

                def x2t_copy(n):
                    for c in range(CT):
                        act.wait_ge(x2t_done, n * 2 + c + 1)
                        if c == 0:
                            need(act, logits_done, n)
                        act.activation(x2t[:, c, :], work[c][:, 0:NP], ACT.Copy).then_inc(x2t_made, 1)

                def top_exps(n):
                    act.wait_ge(top_ready, n + 1)
                    act.activation(tope[:T], topd[:T], ACT.Exp).then_inc(top_exp, 1)

                def body(i, parity):
                    for w in range(UNITS):
                        if w == 3 and here(i - 1):
                            take_u(i - 1, 1)
                        if w == 9 and here(i):
                            take_u(i, 0)
                        if w == 8 and here(i - 2):
                            top_exps(i - 2)
                        if w == 11 and here(i + 1):
                            take_v(i + 1, 1 - parity)
                        n, u_ = behind(i, w, 1)
                        if here(n):
                            loga(n, u_)
                        if here(i):
                            expo(i, w)
                        n, u_ = behind(i, w, 2)
                        if here(n):
                            square(n, u_)
                        if w == 0:
                            if here(i + 1):
                                take_tok(i + 1, 0)
                            if here(i - 2):
                                guess2(i - 2)
                        if w == 1 and here(i + 1):
                            take_tok(i + 1, 1)
                        if w == 2:
                            if here(i + 1):
                                guess(i + 1, 0)
                            if here(i):
                                qk_hi_part(i, 1)
                        if w == 4:
                            if here(i - 2):
                                x2t_copy(i - 2)
                            if here(i + 2):
                                x_hi(i + 2)
                        if w == 6 and here(i + 1):
                            guess(i + 1, 1)
                        if w == 7 and here(i + 1):
                            xt_hi(i + 1)
                        if w in (7, 8) and here(i - 1):
                            attn_hi(i - 1, 2 * w - 14)
                            attn_hi(i - 1, 2 * w - 13)
                        if w == 9 and here(i + 1):
                            qk_hi_part(i + 1, 0)

                walk(act, body)

            @block.vector
            def _(dve):
                wst = stage[:MELS, :].rearrange("p (f d) -> p f d", f=TAPS)
                steps = [0]

                def link(ins):
                    steps[0] += 1
                    ins.then_inc(own, 1)
                    dve.wait_ge(own, steps[0])

                link(dve.memset(p_bias[:].bitcast(F32), 0.0))
                link(dve.memset(one_rows[:].bitcast(F32), 0.0))
                link(dve.memset(one_line.bitcast(F32), 1.0))
                dve.wait_ge(w_loaded, 16 * 7)
                link(dve.tensor_copy(mel_wa[:MELS], wst))
                link(dve.tensor_copy(bias_hl[:, 0, :], bias_raw[:, 0, :]))
                link(dve.tensor_copy(p_bias_hl[:, 0, :], bias_raw[:, 1, :]))
                dve.tensor_copy(mel_wb[:MELS], wst).then_inc(dve_setup, 1)
                dve.tensor_tensor(mel_wl[:MELS], wst, mel_wa[:MELS].bitcast(F32), ALU.subtract).then_inc(dve_setup, 1)
                dve.tensor_tensor(bias_hl[:, 1, :], bias_raw[:, 0, :], bias_hl[:, 0, :].bitcast(F32),
                                  ALU.subtract).then_inc(dve_setup, 1)
                dve.tensor_tensor(p_bias_hl[:, 1, :], bias_raw[:, 1, :], p_bias_hl[:, 0, :].bitcast(F32),
                                  ALU.subtract).then_inc(dve_setup, 1)
                for t in (xth, xtl, kh, kl):
                    dve.memset(t[:, :, NP:KPAD].bitcast(F32), 0.0).then_inc(dve_setup, 1)
                dve.memset(ones_b[:], 1.0).then_inc(dve_setup, 1)
                for t in v:
                    dve.memset(t[:], 1.0).then_inc(dve_setup, 1)
                dve.memset(rden[:], 0.0).then_inc(dve_setup, 1)
                dve.memset(seen[0][:], 0.0).then_inc(dve_setup, 1)
                dve.memset(seen_b[:], 0.0).then_inc(dve_setup, 1)
                dve.wait_ge(pool_setup, 9)
                dve.tensor_copy(before[:], before_f[:]).then_inc(dve_setup, 1)
                SETUP = 15
                dve.wait_ge(dve_setup, SETUP)

                def split_rest():
                    sv = stage[:, 0:CT * 2 * D].rearrange("p (c n) -> p c n", c=CT)
                    dve.wait_ge(w_loaded, 16 * 8)
                    link(dve.tensor_copy(qk_wh[:], sv))
                    dve.tensor_tensor(qk_wl[:], sv, qk_wh[:].bitcast(F32), ALU.subtract).then_inc(w_stage_free, 1)
                    dve.wait_ge(w_loaded, 16 * 10)
                    sv2 = stage[:, 0:CT * D].rearrange("p (c n) -> p c n", c=CT)
                    sv3 = stage[:, CT * D:CT * D + 4 * D].rearrange("p (c n) -> p c n", c=4)
                    link(dve.tensor_copy(v_wh[:], sv2))
                    link(dve.tensor_copy(p_wh[:], sv3))
                    dve.tensor_tensor(v_wl[:], sv2, v_wh[:].bitcast(F32), ALU.subtract).then_inc(rest_split, 1)
                    dve.tensor_tensor(p_wl[:], sv3, p_wh[:].bitcast(F32), ALU.subtract).then_inc(rest_split, 1)

                def chain(signal, per, n, done):
                    count = [done]

                    def step(ins, apart=False):
                        count[0] += 1
                        ins.then_inc(signal, 1)
                        if apart:
                            wait_apart(dve, signal, n * per + count[0], dve_passed)
                        else:
                            dve.wait_ge(signal, n * per + count[0])
                    return step, count

                def mean_var(src, st, m, v_, signal, step):
                    for k in range(TILES):
                        last = dve.bn_stats(st[:T, k, :], src[:T, k, :])
                    step(last, True)
                    for k in range(TILES):
                        last = dve.bn_aggr(m[:T, k, :], st[:T, k, :])
                    step(last)
                    dve.tensor_scalar(v_[:T], m[:T, :, 1], EPS, None, ALU.add).then_inc(signal, 1)

                def newton(v_, a, b, c, r, step):
                    step(dve.tensor_tensor(b[:T], a[:T], a[:T], ALU.mult))
                    step(dve.scalar_tensor_tensor(out=c[:T], in0=b[:T], scalar=-0.5, in1=v_[:T],
                                                  op0=ALU.mult, op1=ALU.mult))
                    step(dve.scalar_tensor_tensor(out=r[:T], in0=c[:T], scalar=1.5, in1=a[:T],
                                                  op0=ALU.add, op1=ALU.mult))

                def normalise(dst, src, m, r):
                    for k in range(TILES):
                        last = dve.tensor_scalar(dst[:T, k, :], src[:T, k, :], m[:T, k, 0:1], r[:T, k:k + 1],
                                                 ALU.subtract, ALU.mult)
                    return last

                FRONT = 10

                def front_a(n):
                    step, _ = chain(front_own, FRONT, n, 0)
                    dve.wait_ge(raw_made, n * 2 + 2)
                    need(dve, xn_made, n)
                    mean_var(xn, stats, mv, ve, ln_var, step)

                def front_b(n):
                    step, _ = chain(front_own, FRONT, n, 2)
                    dve.wait_ge(ln_guess, n * 4 + 2)
                    newton(ve, ra, rb, rc, rstd, step)
                    normalise(xn, xn, mv, rstd).then_inc(xhat_made, 1)

                def front_c(n):
                    step, _ = chain(front_own, FRONT, n, 5)
                    dve.wait_ge(h0_made, n + 1)
                    mean_var(h0, stats, mv, ve, ln_var, step)

                def front_d(n):
                    step, c = chain(front_own, FRONT, n, 7)
                    dve.wait_ge(ln_guess, n * 4 + 4)
                    newton(ve, ra, rb, rc, rstd, step)
                    normalise(xn, h0, mv, rstd).then_inc(xn_made, 1)
                    assert c[0] == FRONT

                def xt_lo(n):
                    for c in range(CT):
                        dve.wait_ge(xth_made, n * 2 + c + 1)
                        dve.tensor_tensor(xtl[:, c, 0:NP], work[c][:, 0:NP], xth[:, c, 0:NP].bitcast(F32),
                                          ALU.subtract).then_inc(xtl_made, 1)

                def qk_lo_part(n, ct):
                    dve.wait_ge(qk_hi, n * 4 + 2 * ct + 1)
                    dve.tensor_tensor(q_hl[:, 1, ct, :], work[0][:, 0:NP], q_hl[:, 0, ct, :].bitcast(F32),
                                      ALU.subtract).then_inc(qk_lo, 1)
                    dve.wait_ge(qk_hi, n * 4 + 2 * ct + 2)
                    dve.tensor_tensor(kl[:, ct, 0:NP], work[1][:, 0:NP], kh[:, ct, 0:NP].bitcast(F32),
                                      ALU.subtract).then_inc(qk_lo, 1)

                def whole(w):
                    return probs[w % RING] if unit(w)[2] < 2 else probs[w % RING][0:K1, 0:HT * K1]

                def clamp(n, w):
                    dve.wait_ge(exp_done, n * UNITS + w + 1)
                    dve.tensor_scalar(whole(w), whole(w), LN_MAX, None, ALU.min).then_inc(clamp_done, 1)

                def soft(n, w):
                    s = 2 * (w % 2)
                    dve.wait_ge(ln_done, n * UNITS + w + 1)
                    if unit(w)[2] < 2:
                        x_, a = score[:, s:s + 2, 0:2 * N], whole(w).rearrange("p (a q) -> p a q", a=2)
                    else:
                        x_, a = score[0:K1, s, 0:HT * K1], whole(w)
                    dve.scalar_tensor_tensor(out=a, in0=x_, scalar=SCALE, in1=a, op0=ALU.mult,
                                             op1=ALU.max).then_inc(max_done, 1)

                def divide(n):
                    step, _ = chain(divide_own, 1, n, 0)
                    dve.wait_ge(den_moved, n * 64 + 64)
                    need(dve, rden_moved, 16 * n)
                    step(dve.tensor_scalar(den_eps[:], den[:], DEN_EPS, None, ALU.add))
                    dve.reciprocal(den_inv[:], den_eps[:]).then_inc(inv_made, 1)

                def scale_heads(n, g):
                    dve.wait_ge(spread_done, n * 4 + g + 1)
                    dve.tensor_tensor(u[:, g, :], u[:, g, :], work[g % 2][:, 0:NP], ALU.mult).then_inc(attn_made, 1)

                def residual(n):
                    step, _ = chain(residual_own, 2, n, 0)
                    need(dve, h1_stored, 16 * n)
                    need(dve, xn2_made, n)
                    dve.wait_ge(h0_kept_moved, n * 16 + 16)
                    dve.wait_ge(proj_done, n * 2 + 1)
                    dve.tensor_tensor(h1[:T, 0:2, :], work[0][:T, :].rearrange("p (k d) -> p k d", k=2),
                                      h0_kept[:T, 0:2, :], ALU.add)
                    dve.wait_ge(proj_done, n * 2 + 2)
                    dve.tensor_tensor(h1[:T, 2, :], work[1][:T, 0:D], h0_kept[:T, 2, :], ALU.add).then_inc(h1_made, 1)
                    dve.wait_ge(h1_made, n + 1)
                    mean_var(h1, stats2, mv2, ve2, ln2_var, step)

                def norm2(n):
                    step, c = chain(norm2_own, 3, n, 0)
                    dve.wait_ge(ln2_guess, n * 2 + 2)
                    need(dve, x2t_done, 2 * n)
                    need(dve, tokens_stored, 16 * n)
                    newton(ve2, ra2, rb2, rc2, rstd2, step)
                    normalise(xn2, h1, mv2, rstd2).then_inc(xn2_made, 1)

                def top_two(n):
                    step, _ = chain(top_own, 3, n, 0)
                    dve.wait_ge(logits_done, n + 1)
                    step(dve.tensor_tensor(lg[:T], work[1][:T, ASIDE:ASIDE + TILES * E].rearrange("p (k e) -> p k e", k=TILES),
                                           br[:T].rearrange("p (a e) -> p a e", a=1).broadcast_to([T, TILES, E]), ALU.add), True)
                    for k in range(TILES):
                        last = dve.max(top[:T, k, :], lg[:T, k, :])
                    step(last)
                    need(dve, top_exp, n)
                    dve.tensor_tensor(topd[:T], top[:T], top[:T, :, 0:1].broadcast_to([T, TILES, 8]),
                                      ALU.subtract).then_inc(top_ready, 1)
                    for k in range(TILES):
                        last = dve.max_index(top_at[:T, k, :], top[:T, k, :], lg[:T, k, :])
                    step(last)

                def weights(n):
                    step, c = chain(weights_own, 6, n, 0)
                    dve.wait_ge(top_exp, n + 1)
                    step(dve.tensor_reduce(tsum[:T], tope[:T], AX.X, ALU.add))
                    step(dve.reciprocal(trec[:T], tsum[:T]))
                    need(dve, listed, n * (16 * 2 * TILES))
                    for j in range(2):
                        last = dve.tensor_tensor(entry[:T, j, :, 1], tope[:T, :, j], trec[:T], ALU.mult)
                    step(last)
                    for j in range(2):
                        last = dve.tensor_scalar(valid[:T, j, :], entry[:T, j, :, 1], 0.0, None, ALU.is_gt)
                    dve.tensor_copy(at_f[:T], top_at[:T, :, 0:2])
                    step(dve.tensor_copy(entry[:T, :, :, 0].bitcast(I32),
                                         token_id[:T].rearrange("p (a k) -> p a k", a=1).broadcast_to([T, 2, TILES])))
                    dve.tensor_scalar(token_id[:T], token_id[:T], float(NP), None, ALU.add)
                    for j in range(2):
                        last = dve.tensor_tensor(hot[:T, j],
                                                 expert_id[:T].rearrange("p (a e) -> p a e", a=1).broadcast_to([T, TILES, E]),
                                                 at_f[:T, :, j:j + 1].broadcast_to([T, TILES, E]), ALU.is_equal)
                    step(last)
                    for j in range(2):
                        last = dve.tensor_tensor(hot[:T, j], hot[:T, j],
                                                 valid[:T, j, :].rearrange("p (k a) -> p k a", a=1).broadcast_to([T, TILES, E]),
                                                 ALU.mult)
                    step(last)
                    dve.tensor_tensor(hot_b[:T], hot[:T, 0], hot[:T, 1], ALU.add).then_inc(hot_made, 1)

                def read_ranks(n):
                    dve.wait_ge(rank_done, n + 1)
                    dve.tensor_copy(rank[:T], work[1][:T, ASIDE:ASIDE + TILES * E].rearrange("p (k e) -> p k e",
                                                                              k=TILES)).then_inc(rank_read, 1)

                def places(n):
                    step, c = chain(places_own, TILES + 5, n, 0)
                    for k in range(TILES):
                        step(dve.tensor_tensor(seen[k + 1][:T], seen[k][:T], hot_b[:T, k, :], ALU.add))
                    dve.wait_ge(rank_read, n + 1)
                    dve.tensor_copy(seen[0][:T], seen[TILES][:T])
                    dve.tensor_copy(seen_b[:T], seen[TILES][:T])
                    for j in range(2):
                        last = dve.tensor_tensor(mine[:T, j], hot[:T, j], rank[:T], ALU.mult)
                    step(last)
                    step(dve.tensor_reduce(place[:T], mine[:T], AX.X, ALU.add))
                    step(dve.tensor_scalar(over[:T], place[:T], float(CAP), BIG, ALU.is_ge, ALU.mult))
                    step(dve.tensor_tensor(place2[:T], place[:T], over[:T], ALU.add))
                    dve.tensor_scalar(over[:T], valid[:T], -BIG, BIG, ALU.mult, ALU.add)
                    for j in range(2):
                        last = dve.scalar_tensor_tensor(out=place[:T, j], in0=at_f[:T, :, j], scalar=float(SLOTS),
                                                        in1=place2[:T, j], op0=ALU.mult, op1=ALU.add)
                    step(last)
                    dve.tensor_tensor(place_i[:T], place[:T], over[:T], ALU.add).then_inc(place_made, 1)
                    assert c[0] == TILES + 5

                def body(i, parity):
                    for w in range(UNITS):
                        n, u_ = behind(i, w, 1)
                        if here(n):
                            soft(n, u_)
                        if here(i):
                            clamp(i, w)
                        if w == 0 and here(i - 2):
                            norm2(i - 2)
                        if w == 1 and here(i + 1):
                            front_a(i + 1)
                        if w == 2:
                            if here(i + 1):
                                front_b(i + 1)
                            if here(i):
                                qk_lo_part(i, 1)
                        if w == 4 and here(i - 1):
                            divide(i - 1)
                        if w == 5 and here(i + 1):
                            front_c(i + 1)
                        if w == 6:
                            if isinstance(i, int) and i == -1:
                                split_rest()
                            if here(i - 1):
                                scale_heads(i - 1, 0)
                                scale_heads(i - 1, 1)
                            if here(i + 1):
                                front_d(i + 1)
                        if w == 7:
                            if here(i - 1):
                                scale_heads(i - 1, 2)
                                scale_heads(i - 1, 3)
                            if here(i + 1):
                                xt_lo(i + 1)
                            if here(i - 2):
                                top_two(i - 2)
                        if w == 8 and here(i - 2):
                            weights(i - 2)
                        if w == 9 and here(i + 1):
                            qk_lo_part(i + 1, 0)
                        if w == 10:
                            if here(i - 1):
                                residual(i - 1)
                            if here(i - 2):
                                read_ranks(i - 2)
                        if w == 11 and here(i - 2):
                            places(i - 2)

                walk(dve, body)

            @block.tensor
            def _(pe):
                def products(o, terms):
                    for t, (lhs, rhs) in enumerate(terms):
                        last = pe.matmul(o, lhs, rhs, start=(t == 0), stop=(t == len(terms) - 1))
                    return last

                def tok_tiles(n, tiles):
                    if 0 in tiles:
                        pe.wait_ge(x_stacked, n * 32 + 32)
                        pe.wait_ge(xl_made, 2 * n + 2)
                        need(pe, v_made, 4 * n)
                    for k in tiles:
                        o = work[k // 2][:T, (k % 2) * D:(k % 2) * D + D]
                        last = products(o, [(patches(a, k, f), m[:STACK + (1 if f == 0 else 0), f, :])
                                            for f in range(TAPS) for a, m in ((xa, mel_wa), (xb, mel_wb))])
                    last.then_inc(tok_done, 1)

                def turn(src, c, signal):
                    for k in range(TILES):
                        last = pe.transpose(work[c][:, k * T:k * T + T], src[:T, k, c * P:c * P + P], ident[:T, :T])
                    last.then_inc(signal, 1)

                def turn_x(n):
                    pe.wait_ge(xn_made, n + 1)
                    need(pe, attn_made, 4 * (n - 1))
                    need(pe, qk_lo, 4 * n)
                    turn(xn, 0, xt_done)
                    turn(xn, 1, xt_done)

                def turn_x2(n):
                    pe.wait_ge(xn2_made, n + 1)
                    pe.wait_ge(qk_lo, upto(4 * n + 12, 4 * PAIRS))
                    turn(xn2, 0, x2t_done)
                    turn(xn2, 1, x2t_done)

                def spread_rden(n, g):
                    if g == 0:
                        pe.wait_ge(rden_moved, 16 * n + 16)
                        pe.wait_ge(qk_lo, upto(4 * n + 8, 4 * PAIRS))
                        need(pe, x2t_made, 2 * n)
                    if g >= 2:
                        pe.wait_ge(attn_made, n * 4 + g - 1)
                    pe.matmul(work[g % 2][:, 0:NP], pick[:, g, :], rden[:], start=True,
                              stop=True).then_inc(spread_done, 1)

                def project(n, tiles):
                    if 0 in tiles:
                        pe.wait_ge(al_made, n * 4 + 4)
                        pe.wait_ge(qk_lo, upto(4 * n + 10, 4 * PAIRS))
                    for k in tiles:
                        o = work[k // 2][:T, (k % 2) * D:(k % 2) * D + D]
                        sl = slice(k * T, k * T + T)
                        last = products(o, [(one_rows[:, :], p_bias[:])] +
                                        [(a[:, g, sl], wt[:, g, :]) for g in range(4)
                                         for a, wt in ((ah, p_wh), (al, p_wh), (ah, p_wl))])
                        if k:
                            last.then_inc(proj_done, 1)

                def logits(n):
                    pe.wait_ge(x2t_made, n * 2 + 2)
                    pe.wait_ge(attn_made, upto(4 * n + 8, 4 * PAIRS))
                    for k in range(TILES):
                        last = products(work[1][:T, ASIDE + k * E:ASIDE + k * E + E],
                                        [(x2t[:, c, k * T:k * T + T], wr[:, c, :]) for c in range(CT)])
                    last.then_inc(logits_done, 1)

                def ranks(n):
                    pe.wait_ge(hot_made, n + 1)
                    pe.wait_ge(qk_lo, upto(4 * n + 14, 4 * PAIRS))
                    for k in range(TILES):
                        last = products(work[1][:T, ASIDE + k * E:ASIDE + k * E + E],
                                        [(before[:T, :], hot_b[:T, k, :])] +
                                        [(ones_b[:T, :], hot_b[:T, j, :]) for j in range(k)] +
                                        [(ones_b[:T, :], seen_b[:T, :])])
                    last.then_inc(rank_done, 1)

                def qk(n, ct):
                    pe.wait_ge(xtl_made, n * 2 + 2)
                    if ct:
                        pe.wait_ge(raw_made, upto(2 * n + 4, 2 * PAIRS))
                    else:
                        need(pe, top_ready, n - 2)
                    for s in range(2):
                        col = (2 * s + ct) * P
                        products(work[s][:, 0:NP],
                                 [(wt[:, c, col:col + P], xt[:, c, 0:NP])
                                  for c in range(CT) for wt, xt in ((qk_wh, xth), (qk_wh, xtl), (qk_wl, xth))]
                                 ).then_inc(qk_done, 1)

                def values(n):
                    pe.wait_ge(qk_lo, n * 4 + 2)
                    need(pe, h1_made, n - 1)
                    need(pe, rank_read, n - 2)
                    for b in range(2):
                        for kt in range(2):
                            a = keys(b, kt)
                            last = products(work[b][:, kt * D:kt * D + D],
                                            [(xt[:, c, a:a + P], wt[:, c, :])
                                             for c in range(CT) for xt, wt in ((xth, v_wh), (xtl, v_wh), (xth, v_wl))])
                        last.then_inc(v_done, 1)

                def scores(n, w):
                    ct, b, part = unit(w)
                    s = 2 * (w % 2)
                    need(pe, max_done, n * UNITS + w - 1)
                    if w % 6 == 0:
                        pe.wait_ge(qk_lo, n * 4 + 2 * ct + 2)
                        pe.wait_ge(q_spread[ct], n * (16 * HT) + 16 * HT)
                    a = keys(b, part // 2)
                    for j in range(2 if part < 2 else 1):
                        h = part * 4 + 2 * j
                        if part < 2:
                            rhs = [q_diag[:, h:h + 2, x_, ct, b * N:b * N + N] for x_ in range(2)]
                            o = score[:, s + j, 0:2 * N].rearrange("p (h q) -> p h q", h=2)
                        else:
                            rhs = [q_diag[:, :, x_, ct, b * N + K0:b * N + N] for x_ in range(2)]
                            o = score[:, s, 0:HT * K1].rearrange("p (h q) -> p h q", h=HT)
                        last = products(o, [(kh[:, ct, a:a + P], rhs[0]), (kh[:, ct, a:a + P], rhs[1]),
                                            (kl[:, ct, a:a + P], rhs[0])])
                    last.then_inc(scores_done, 1)

                def weigh(n, w, values_at):
                    ct, b, part = unit(w)
                    buf = probs[w % RING]
                    if w == 0:
                        pe.wait_ge(v_made, n * 4 + 4)
                        need(pe, u_made, 4 * n)
                    if w == 6:
                        pe.wait_ge(u_made, n * 4 + 2)
                    wait_apart(pe, causal_done, n * UNITS + w + 1, pe_passed)
                    if part < 2:
                        for j in range(4):
                            last = pe.matmul(heads_out[part][32 * j:32 * j + 32, b * N:b * N + N],
                                             values_at[:, b, 0, HT * ct + 4 * part + j, :], buf[:, j * N:j * N + N],
                                             start=True, stop=False, skip_group_check=True)
                    else:
                        for g in range(2):
                            for j in range(4):
                                h = 4 * g + j
                                last = pe.matmul(heads_out[g][32 * j:32 * j + 32, b * N + K0:b * N + N],
                                                 values_at[0:K1, b, 1, HT * ct + h, :], buf[0:K1, h * K1:h * K1 + K1],
                                                 start=False, stop=True, skip_group_check=True)
                    last.then_inc(pv_done, 1)

                pe.wait_ge(dve_setup, 15)
                pe.wait_ge(setup_moved, 160)

                def body(i, parity):
                    for w in range(UNITS):
                        n, u_ = behind(i, w, 3)
                        if here(n):
                            weigh(n, u_, v[parity if w >= 3 else 1 - parity])
                        n, u_ = behind(i + 1, w, UNITS - 1)
                        if here(n):
                            scores(n, u_)
                        if w == 0 and here(i + 1):
                            tok_tiles(i + 1, (2,))
                        if w == 1 and here(i):
                            qk(i, 1)
                        if w == 3 and here(i - 2):
                            turn_x2(i - 2)
                        if w == 5 and here(i - 1):
                            spread_rden(i - 1, 0)
                            spread_rden(i - 1, 1)
                        if w == 6 and here(i - 1):
                            spread_rden(i - 1, 2)
                            spread_rden(i - 1, 3)
                        if w == 7:
                            if here(i + 1):
                                turn_x(i + 1)
                            if here(i - 2):
                                logits(i - 2)
                        if w == 8 and here(i + 1):
                            if isinstance(i, int) and i == -1:
                                pe.wait_ge(rest_split, 2)
                                pe.wait_ge(q_cleared, 1)
                            qk(i + 1, 0)
                        if w == 9:
                            if here(i - 1):
                                project(i - 1, (0, 1))
                            if here(i - 2):
                                ranks(i - 2)
                            if here(i - 1):
                                project(i - 1, (2,))
                        if w == 10 and here(i + 1):
                            values(i + 1)
                        if w == 11 and here(i + 2):
                            tok_tiles(i + 2, (0, 1))

                walk(pe, body)

        with ExitStack() as mem:
            def sb(name, shape, dt=F32):
                return mem.enter_context(nc.sbuf_tensor(name, shape, dt))

            def bank(name):
                return mem.enter_context(nc.psum_tensor(name, [P, 512], F32))

            turned = [bank(f"turned{i}") for i in range(2)]
            inner = [bank(f"inner{i}") for i in range(4)]
            rows = [bank(f"rows{i}") for i in range(2)]

            ident2 = sb("ident2", [P, P])
            lists_sb = [sb(f"lists{i}", [P, STILES, 2]) for i in range(2)]
            got = [sb(f"got{i}", [P, STILES, D]) for i in range(2)]
            w1 = sb("w1", [P, CT, INNER])
            w2 = sb("w2", [P, ITILES, D])
            w1h = [sb(f"w1h{i}", [P, CT, INNER], F32R) for i in range(2)]
            w1l = [sb(f"w1l{i}", [P, CT, INNER], F32R) for i in range(2)]
            w2h = [sb(f"w2h{i}", [P, ITILES, D], F32R) for i in range(2)]
            w2l = [sb(f"w2l{i}", [P, ITILES, D], F32R) for i in range(2)]
            gth = sb("gth", [P, 2, CT, HALF], F32R)
            gtl = sb("gtl", [P, 2, CT, HALF], F32R)
            hh = sb("hh", [P, ITILES, HALF], F32R)
            hl = sb("hl", [P, ITILES, HALF], F32R)
            y = sb("y", [P, STILES, D])
            ROUND = ITILES // 2

            lists_loaded = [sem("lists_loaded0"), sem("lists_loaded1")]
            gathered = [sem("gathered0"), sem("gathered1")]
            w_here = sem("w_here")
            w_hi = sem("w_hi")
            w_lo = sem("w_lo")
            id_made = sem("id_made")
            got_clear = sem("got_clear")
            turned_done = sem("turned_done")
            gt_hi = sem("gt_hi")
            gt_lo = sem("gt_lo")
            inner_done = sem("inner_done")
            inner_hi = sem("inner_hi")
            inner_lo = sem("inner_lo")
            rows_done = sem("rows_done")
            y_made = sem("y_made")
            added = sem("added")
            pool_passed = sem("pool_passed_too")
            HT2 = STILES // 2

            block = mem.enter_context(nc.Block())

            @block.sync
            def _(sp):
                def load(n, m, lists_at, w1_at, w2_at):
                    if m["added"] is not None:
                        sp.wait_ge(added, m["added"])
                    sp.dma_start(lists_sb[n % 2][:S], lists_at).then_inc(lists_loaded[n % 2], 16)
                    if m["lo"] is not None:
                        sp.wait_ge(w_lo, m["lo"])
                    sp.dma_start(w1[:], w1_at).then_inc(w_here, 16)
                    sp.dma_start(w2[:], w2_at).then_inc(w_here, 16)

                for n in range(2):
                    load(n, dict(added=None, lo=2 * n or None), table_experts[n], w_in_v[n], w_out_v[n])
                with sp.Fori(0, E // 2 - 1) as step:
                    e = step * 2
                    at = [(dict(added=sp.snap(e * (16 * STILES) + 16 * STILES * (b + 1)), lo=sp.snap(e * 2 + 2 * (b + 2))),
                           table_experts[bass.ds(e + (2 + b), 1)].rearrange("e t s w -> (e t) s w"),
                           w_in_v[bass.ds(e + (2 + b), 1)].rearrange("e p c i -> (e p) c i"),
                           w_out_v[bass.ds(e + (2 + b), 1)].rearrange("e p t d -> (e p) t d")) for b in range(2)]
                    for b in range(2):
                        load(b, *at[b])

            @block.gpsimd
            def _(pool):
                pool.memset(ident2[:], 0.0).then_inc(id_made, 1)
                pool.wait_ge(id_made, 1)
                pool.affine_select(out=ident2[:], in_=ident2[:], compare_op=ALU.not_equal, fill=1.0, base=0,
                                   pattern=[[-1, P]], channel_multiplier=1).then_inc(id_made, 1)
                for b in range(2):
                    pool.memset(got[b][:], 0.0).then_inc(got_clear, 1)
                pool.wait_ge(got_clear, 2)

                def gather(m, b):
                    pool.wait_ge(lists_loaded[b], m * 16 + 16)
                    wait_apart(pool, turned_done, m * 8 + (4 * b - 4), pool_passed)
                    for s in range(STILES):
                        pool.indirect_dma_start(
                            out=got[b][:S, s, :], out_offset=None, in_=tokens_dram[:, :],
                            in_offset=bass.IndirectOffsetOnAxis(ap=lists_sb[b][:S, s, 0:1].bitcast(U32), axis=0),
                            bounds_check=TOKENS - 1, oob_is_err=False).then_inc(gathered[b], 16)

                def add(n, b):
                    need(pool, added, n * (16 * STILES))
                    for s in range(STILES):
                        wait_apart(pool, y_made, n * STILES + s + 1, pool_passed)
                        pool.indirect_dma_start(
                            out=out[:, :],
                            out_offset=bass.IndirectOffsetOnAxis(ap=lists_sb[b][:S, s, 0:1].bitcast(U32), axis=0),
                            in_=y[:S, s, :], in_offset=None, bounds_check=TOKENS - 1, oob_is_err=False,
                            compute_op=ALU.add).then_inc(added, 16)

                gather(0, 0)
                gather(0, 1)
                add(0, 0)
                gather(1, 0)
                add(1, 1)
                gather(1, 1)
                add(2, 0)
                with pool.Fori(1, E // 2 - 1) as step:
                    e = step * 2
                    gather(step + 1, 0)
                    add(e + 1, 1)
                    gather(step + 1, 1)
                    add(e + 2, 0)
                add(E - 1, 1)
                pool.wait_ge(added, 16 * STILES * E)

            @block.scalar
            def _(act):
                act.preload_act_table_set("natural_log_exp_and_others")

                def weights_hi(n, b):
                    act.wait_ge(w_here, n * 32 + 32)
                    need(act, rows_done, (n - 1) * STILES)
                    act.activation(w1h[b][:], w1[:], ACT.Copy).then_inc(w_hi, 1)
                    act.activation(w2h[b][:], w2[:], ACT.Copy).then_inc(w_hi, 1)

                def tokens_hi(n):
                    for a in range(2):
                        for c in range(CT):
                            act.wait_ge(turned_done, n * 4 + a * 2 + c + 1)
                            if a == 0 and c == 0:
                                need(act, inner_done, n * (2 * ITILES))
                            act.activation(gth[:, a, c, :], turned[c][:, 0:HALF], ACT.Copy).then_inc(gt_hi, 1)

                def relu_hi(n, a):
                    for t in range(ITILES):
                        act.wait_ge(inner_done, n * (2 * ITILES) + a * ITILES + t + 1)
                        if t == 0:
                            need(act, rows_done, n * STILES + a * HT2)
                        act.activation(hh[:, t, :], inner[t % 4][:, 0:HALF], ACT.Relu).then_inc(inner_hi, 1)

                def expert(n, b, prepare):
                    relu_hi(n, 0)
                    if prepare:
                        weights_hi(n + 1, 1 - b)
                    relu_hi(n, 1)
                    if prepare:
                        tokens_hi(n + 1)

                weights_hi(0, 0)
                tokens_hi(0)
                expert(0, 0, True)
                expert(1, 1, True)
                with act.Fori(1, E // 2 - 1) as step:
                    e = step * 2
                    expert(e, 0, True)
                    expert(e + 1, 1, True)
                expert(E - 2, 0, True)
                expert(E - 1, 1, False)

            @block.vector
            def _(dve):
                def weights_lo(n, b):
                    dve.wait_ge(w_hi, n * 2 + 2)
                    dve.tensor_tensor(w1l[b][:], w1[:], w1h[b][:].bitcast(F32), ALU.subtract).then_inc(w_lo, 1)
                    dve.tensor_tensor(w2l[b][:], w2[:], w2h[b][:].bitcast(F32), ALU.subtract).then_inc(w_lo, 1)

                def tokens_lo(n):
                    for a in range(2):
                        for c in range(CT):
                            dve.wait_ge(gt_hi, n * 4 + a * 2 + c + 1)
                            dve.tensor_tensor(gtl[:, a, c, :], turned[c][:, 0:HALF], gth[:, a, c, :].bitcast(F32),
                                              ALU.subtract).then_inc(gt_lo, 1)

                def relu_lo(n, a):
                    for t in range(ITILES):
                        dve.wait_ge(inner_hi, n * (2 * ITILES) + a * ITILES + t + 1)
                        dve.scalar_tensor_tensor(out=hl[:, t, :], in0=inner[t % 4][:, 0:HALF], scalar=0.0,
                                                 in1=hh[:, t, :].bitcast(F32), op0=ALU.max,
                                                 op1=ALU.subtract).then_inc(inner_lo, 1)

                def take_rows(n, b, a):
                    for s in range(a * HT2, a * HT2 + HT2):
                        dve.wait_ge(rows_done, n * STILES + s + 1)
                        need(dve, added, n * (16 * STILES) - 16 * STILES + 16 * STILES)
                        dve.tensor_scalar(y[:S, s, :], rows[s % 2][:S, 0:D], lists_sb[b][:S, s, 1:2], None,
                                          ALU.mult).then_inc(y_made, 1)

                def expert(n, b, prepare):
                    relu_lo(n, 0)
                    take_rows(n, b, 0)
                    if prepare:
                        weights_lo(n + 1, 1 - b)
                    relu_lo(n, 1)
                    if prepare:
                        tokens_lo(n + 1)
                    take_rows(n, b, 1)

                weights_lo(0, 0)
                tokens_lo(0)
                expert(0, 0, True)
                expert(1, 1, True)
                with dve.Fori(1, E // 2 - 1) as step:
                    e = step * 2
                    expert(e, 0, True)
                    expert(e + 1, 1, True)
                expert(E - 2, 0, True)
                expert(E - 1, 1, False)

            @block.tensor
            def _(pe):
                def turn(n, b):
                    for a in range(2):
                        for c in range(CT):
                            if a == 0 and c == 0:
                                pe.wait_ge(gathered[b], n * (8 * STILES) + (16 - 8 * b) * STILES)
                            need(pe, gt_lo, n * 4 + a * 2 + c - 1)
                            for s in range(HT2):
                                last = pe.transpose(turned[c][:, s * S:s * S + S],
                                                    got[b][:S, a * HT2 + s, c * P:c * P + P], ident2[:S, :S])
                            last.then_inc(turned_done, 1)

                def first(n, b, a):
                    if a == 0:
                        pe.wait_ge(w_lo, n * 2 + 2)
                    pe.wait_ge(gt_lo, n * 4 + a * 2 + 2)
                    for t in range(ITILES):
                        need(pe, inner_lo, n * (2 * ITILES) + a * ITILES + t - 3)
                        k = 0
                        for c in range(CT):
                            for w_, g_ in ((w1h, gth), (w1h, gtl), (w1l, gth)):
                                last = pe.matmul(inner[t % 4][:, 0:HALF], w_[b][:, c, t * P:t * P + P], g_[:, a, c, :],
                                                 start=(k == 0), stop=(k == 3 * CT - 1))
                                k += 1
                        last.then_inc(inner_done, 1)

                def second(n, b, a):
                    for s in range(a * HT2, a * HT2 + HT2):
                        need(pe, y_made, n * STILES + s - 1)
                        if s == a * HT2:
                            pe.wait_ge(inner_lo, n * (2 * ITILES) + (a + 1) * ITILES)
                        at = (s - a * HT2) * S
                        k = 0
                        for t in range(ITILES):
                            for h_, w_ in ((hh, w2h), (hl, w2h), (hh, w2l)):
                                last = pe.matmul(rows[s % 2][:S, 0:D], h_[:, t, at:at + S], w_[b][:, t, :],
                                                 start=(k == 0), stop=(k == 3 * ITILES - 1))
                                k += 1
                        last.then_inc(rows_done, 1)

                pe.wait_ge(id_made, 2)
                turn(0, 0)

                def expert(n, b, prepare):
                    first(n, b, 0)
                    second(n, b, 0)
                    first(n, b, 1)
                    if prepare:
                        turn(n + 1, 1 - b)
                    second(n, b, 1)

                expert(0, 0, True)
                expert(1, 1, True)
                with pe.Fori(1, E // 2 - 1) as step:
                    e = step * 2
                    expert(e, 0, True)
                    expert(e + 1, 1, True)
                expert(E - 2, 0, True)
                expert(E - 1, 1, False)


def kernel(x, L0_tok_W, L0_tok_b, L0_tok_gamma, L0_tok_beta, L0_attn_w_qkv, L0_attn_w_proj, L0_attn_b_proj,
           L0_ffn_W_router, L0_ffn_b_router, L0_ffn_experts_inter, L0_ffn_experts_out):
    import numpy as np
    import concourse.bacc as bacc
    from concourse.bass_utils import run_bass_kernel_spmd

    D = L0_tok_W.shape[1]
    mels = x.shape[1]
    taps = L0_tok_W.shape[0] // mels
    w_qkv = np.asarray(L0_attn_w_qkv)
    w_proj = np.asarray(L0_attn_w_proj)
    heads, hs = 16, D // 16
    wp_t = np.zeros((heads, 2 * hs, D), w_proj.dtype)
    wp_t[:, :hs, :] = w_proj.T.reshape(heads, hs, D)
    given = {
        "x": np.asarray(x),
        "tok_w": np.asarray(L0_tok_W).reshape(mels, taps, D),
        "tok_b": np.asarray(L0_tok_b).reshape(1, D),
        "gamma": np.asarray(L0_tok_gamma),
        "beta": np.asarray(L0_tok_beta),
        "wqk_t": np.ascontiguousarray(w_qkv[:2 * D].T),
        "wv_t": np.ascontiguousarray(w_qkv[2 * D:].T),
        "wp_t": wp_t.reshape(heads * 2 * hs, D),
        "b_proj": np.asarray(L0_attn_b_proj).reshape(1, D),
        "wr_t": np.ascontiguousarray(np.asarray(L0_ffn_W_router).T),
        "b_router": np.asarray(L0_ffn_b_router),
        "w_in": np.asarray(L0_ffn_experts_inter),
        "w_out": np.asarray(L0_ffn_experts_out),
    }
    batches, _, frames = given["x"].shape
    tokens = (frames - taps) // (taps // 2) + 1
    experts = given["w_in"].shape[0]
    nc = bacc.Bacc("TRN2", target_bir_lowering=False, num_devices=1)
    arrays = {f"in_{k}": np.ascontiguousarray(a) for k, a in given.items()}
    args = [nc.dram_tensor(k, a.shape, mybir.dt.from_np(a.dtype), kind="ExternalInput").ap() for k, a in arrays.items()]
    out = nc.dram_tensor("out", (batches * tokens, D), F32, kind="ExternalOutput").ap()
    tokens_dram = nc.dram_tensor("tokens", (batches * tokens, D), F32, kind="Internal").ap()
    table_dram = nc.dram_tensor("table", (experts * 8 * 117, 2), F32, kind="Internal").ap()
    audio_tower(nc, *args, out, tokens_dram, table_dram)
    r = run_bass_kernel_spmd(nc, [arrays], core_ids=[0])
    return r.results[0]["out"].reshape(batches, tokens, D)
```

```python
from contextlib import ExitStack

import concourse.bass as bass
from concourse import mybir

ALU = mybir.AluOpType
ACT = mybir.ActivationFunctionType
AX = mybir.AxisListType
F32 = mybir.dt.float32
F32R = mybir.dt.float32r
BF16 = mybir.dt.bfloat16
I32 = mybir.dt.int32
U32 = mybir.dt.uint32

P = 128
EPS = 1e-5
DEN_EPS = 1e-9
LN_MAX = 2.0 ** 60


def words(ap):
    return ap.bitcast(F32)


def need(eng, sem, value):
    if isinstance(value, int) and value <= 0:
        return
    eng.wait_ge(sem, value)


def wait_apart(eng, sem, value, passed):
    if isinstance(value, int):
        return need(eng, sem, value)
    eng.wait_ge(sem, value)
    eng.sem_inc(passed, 1)


def audio_tower(nc, x, tok_w, tok_b, gamma, beta, wqk_t, wv_t, wp_t, b_proj, wr_t, b_router, w_in, w_out,
                out, tokens_dram, table_dram):
    B, MELS, FRAMES = x.shape
    D = tok_w.shape[2]
    TAPS = tok_w.shape[1]
    HOP = TAPS // 2
    N = (FRAMES - TAPS) // HOP + 1
    PAIRS = B // 2
    NP = 2 * N
    T = 124
    TILES = NP // T
    TOKENS = B * N
    CT = D // P
    HEADS, HS = 16, D // 16
    HT = P // HS
    K0 = P
    K1 = N - K0
    E, INNER = w_in.shape[0], w_in.shape[2]
    CAP = -(-(TOKENS * 5) // (E * 4))
    S = 117
    STILES = 8
    SLOTS = S * STILES
    ITILES = INNER // P
    HALF = SLOTS // 2
    BIG = float(1 << 20)
    SCALE = HS ** -0.5
    STACK = MELS + MELS // 2
    BATCH_COLS = N * HOP
    MID = BATCH_COLS + BATCH_COLS + HOP
    MID_HALF = HOP * T // 2
    XCOLS = MID + 2 * MID_HALF
    assert TAPS == 2 * HOP and TILES == 3 and N - T == T // 2
    UNITS = 12
    LOOP_FROM, LOOP_TO = 4, (PAIRS - 3) // 2 * 2
    assert TILES * T == NP and SLOTS >= CAP and HALF <= 512 and CAP * E * 4 >= TOKENS * 5

    out_pairs = out.rearrange("(p k t) d -> p t k d", k=TILES, t=T)
    tokens_pairs = tokens_dram.rearrange("(p k t) d -> p t k d", k=TILES, t=T)
    table_experts = table_dram.rearrange("(e s t) w -> e t s w", e=E, s=STILES)
    w_in_v = w_in.rearrange("e (c p) i -> e p c i", p=P)
    w_out_v = w_out.rearrange("e (t p) d -> e p t d", p=P)

    with ExitStack() as ctx:
        sems = {}

        def sem(name):
            sems[name] = ctx.enter_context(nc.semaphore(name))
            return sems[name]

        big = ctx.enter_context(nc.sbuf_tensor("big", [P, HT * 2 * CT * NP], F32R))
        RING = 4
        probs_all = ctx.enter_context(nc.sbuf_tensor("probs_all", [P, RING, 4 * N], F32))
        xraw = ctx.enter_context(nc.sbuf_tensor("xraw", [P, max(XCOLS, ITILES * D)], F32))
        w1h0, w1l0, w2h0 = (big[:, k * CT * INNER:(k + 1) * CT * INNER] for k in range(3))
        w1 = probs_all[:].rearrange("p r q -> p (r q)")[:, 0:CT * INNER].rearrange("p (c n) -> p c n", c=CT)
        w2 = xraw[:, 0:ITILES * D].rearrange("p (t d) -> p t d", t=ITILES)
        w1h0 = w1h0.rearrange("p (c n) -> p c n", c=CT)
        w1l0 = w1l0.rearrange("p (c n) -> p c n", c=CT)
        w2h0 = w2h0.rearrange("p (t d) -> p t d", t=ITILES)
        assert CT * INNER == ITILES * D and CT * INNER <= RING * 4 * N and 3 * CT * INNER <= HT * 2 * CT * NP
        w_here = sem("w_here")
        w_hi = sem("w_hi")
        w_lo = sem("w_lo")

        with ExitStack() as mem:
            def sb(name, shape, dt=F32):
                return mem.enter_context(nc.sbuf_tensor(name, shape, dt))

            def bank(name):
                return mem.enter_context(nc.psum_tensor(name, [P, 512], F32))

            score = mem.enter_context(nc.psum_tensor("score", [P, 4, 512], F32))
            heads_out = [bank(f"heads_out{i}") for i in range(2)]
            work = [bank(f"work{i}") for i in range(2)]

            ASIDE = NP + 12

            ident = sb("ident", [P, P])
            pick = sb("pick", [P, 4, P])
            before_f = sb("before_f", [P, T])
            before = sb("before", [P, T], BF16)
            ones_b = sb("ones_b", [P, T], BF16)
            expert_id = sb("expert_id", [P, E])
            token_id = sb("token_id", [P, TILES])
            mel_wa = sb("mel_wa", [P, TAPS, D], F32R)
            mel_wb = sb("mel_wb", [P, TAPS, D], F32R)
            bias_raw = sb("bias_raw", [1, 2, D])
            qk_wh = sb("qk_wh", [P, CT, 2 * D], F32R)
            qk_wl = sb("qk_wl", [P, CT, 2 * D], F32R)
            v_wh = sb("v_wh", [P, CT, D], F32R)
            v_wl = sb("v_wl", [P, CT, D], F32R)
            p_wh = sb("p_wh", [P, 4, D], F32R)
            p_wl = sb("p_wl", [P, 4, D], F32R)
            p_bias = sb("p_bias", [P, D], F32R)
            one_rows = sb("one_rows", [P, T], F32R)
            wr = sb("wr", [P, CT, E])
            br = sb("br", [P, E])
            gam = sb("gam", [P, D])
            bet = sb("bet", [P, D])

            xa = sb("xa", [P, XCOLS], F32R)
            xb = sb("xb", [P, XCOLS], F32R)
            h0 = sb("h0", [P, TILES, D])
            h0_next = sb("h0_next", [P, TILES, D])
            h0_kept = sb("h0_kept", [P, TILES, D])
            xn = sb("xn", [P, TILES, D])
            stats = sb("stats", [P, TILES, 6])
            mv = sb("mv", [P, TILES, 2])
            ve = sb("ve", [P, TILES])
            lnv = sb("lnv", [P, TILES])
            ra = sb("ra", [P, TILES])
            rb = sb("rb", [P, TILES])
            rc = sb("rc", [P, TILES])
            rstd = sb("rstd", [P, TILES])
            KPAD = N + K0 + P
            xth = sb("xth", [P, CT, KPAD], F32R)
            xtl = sb("xtl", [P, CT, KPAD], F32R)
            q_hl = sb("q_hl", [P, 2, CT, NP], F32R)
            q_diag = big[:].rearrange("p (h s c q) -> p h s c q", h=HT, s=2, c=CT)
            kh = sb("kh", [P, CT, KPAD], F32R)
            kl = sb("kl", [P, CT, KPAD], F32R)
            v = [sb(f"v{i}", [P, 2, 2, HEADS, 2 * HS]) for i in range(2)]
            probs = [probs_all[:, i, :] for i in range(RING)]
            stage = probs_all[:].rearrange("p r q -> p (r q)")[:, 0:TAPS * D]
            flat = big[:]
            mel_wl = flat[:, 0:TAPS * D].rearrange("p (f d) -> p f d", f=TAPS)
            one_line = flat[0:1, TAPS * D:TAPS * D + XCOLS]
            bias_at = TAPS * D + XCOLS
            bias_hl = flat[0:1, bias_at:bias_at + 2 * D].rearrange("p (s d) -> p s d", s=2)
            p_bias_hl = flat[0:1, bias_at + 2 * D:bias_at + 4 * D].rearrange("p (s d) -> p s d", s=2)
            u = sb("u", [P, 4, NP])
            DEN_CUT = 6
            den = sb("den", [HEADS * DEN_CUT, NP // DEN_CUT])
            den_eps = sb("den_eps", [HEADS * DEN_CUT, NP // DEN_CUT])
            den_inv = sb("den_inv", [HEADS * DEN_CUT, NP // DEN_CUT])
            rden = sb("rden", [P, NP])
            ah = sb("ah", [P, 4, NP], F32R)
            al = sb("al", [P, 4, NP], F32R)
            h1 = sb("h1", [P, TILES, D])
            xn2 = sb("xn2", [P, TILES, D])
            stats2 = sb("stats2", [P, TILES, 6])
            mv2 = sb("mv2", [P, TILES, 2])
            ve2 = sb("ve2", [P, TILES])
            lnv2 = sb("lnv2", [P, TILES])
            ra2 = sb("ra2", [P, TILES])
            rb2 = sb("rb2", [P, TILES])
            rc2 = sb("rc2", [P, TILES])
            rstd2 = sb("rstd2", [P, TILES])
            x2t = sb("x2t", [P, CT, NP])
            lg = sb("lg", [P, TILES, E])
            top = sb("top", [P, TILES, 8])
            top_at = sb("top_at", [P, TILES, 8], U32)
            topd = sb("topd", [P, TILES, 8])
            tope = sb("tope", [P, TILES, 8])
            tsum = sb("tsum", [P, TILES])
            trec = sb("trec", [P, TILES])
            at_f = sb("at_f", [P, TILES, 2])
            valid = sb("valid", [P, 2, TILES])
            hot = sb("hot", [P, 2, TILES, E])
            hot_b = sb("hot_b", [P, TILES, E], BF16)
            seen = [sb(f"seen{i}", [P, E]) for i in range(TILES + 1)]
            seen_b = sb("seen_b", [P, E], BF16)
            rank = sb("rank", [P, TILES, E])
            mine = sb("mine", [P, 2, TILES, E])
            place = sb("place", [P, 2, TILES])
            over = sb("over", [P, 2, TILES])
            place2 = sb("place2", [P, 2, TILES])
            place_i = sb("place_i", [P, 2, TILES], U32)
            entry = sb("entry", [P, 2, TILES, 2])
            blank = sb("blank", [96, 2 * E * SLOTS // 96], I32)

            patch_w_loaded = sem("patch_w_loaded")
            w_loaded = sem("w_loaded")
            w_stage_free = sem("w_stage_free")
            dve_setup = sem("dve_setup")
            pool_setup = sem("pool_setup")
            mel_moved = sem("mel_moved")
            setup_moved = sem("setup_moved")
            x_loaded = sem("x_loaded")
            xh_made = sem("xh_made")
            xl_made = sem("xl_made")
            x_stacked = sem("x_stacked")
            tok_done = sem("tok_done")
            ln_var = sem("ln_var")
            ln_guess = sem("ln_guess")
            xhat_made = sem("xhat_made")
            h0_made = sem("h0_made")
            xn_made = sem("xn_made")
            xt_done = sem("xt_done")
            xth_made = sem("xth_made")
            xtl_made = sem("xtl_made")
            qk_done = sem("qk_done")
            v_done = sem("v_done")
            qk_hi = sem("qk_hi")
            qk_lo = sem("qk_lo")
            v_made = sem("v_made")
            q_spread = [sem(f"q_spread{c}") for c in range(CT)]
            scores_done = sem("scores_done")
            exp_done = sem("exp_done")
            clamp_done = sem("clamp_done")
            ln_done = sem("ln_done")
            max_done = sem("max_done")
            square_done = sem("square_done")
            causal_done = sem("causal_done")
            pv_done = sem("pv_done")
            u_made = sem("u_made")
            den_moved = sem("den_moved")
            inv_made = sem("inv_made")
            rden_moved = sem("rden_moved")
            spread_done = sem("spread_done")
            attn_made = sem("attn_made")
            ah_made = sem("ah_made")
            al_made = sem("al_made")
            proj_done = sem("proj_done")
            proj_taken = sem("proj_taken")
            h1_made = sem("h1_made")
            ln2_var = sem("ln2_var")
            ln2_guess = sem("ln2_guess")
            xn2_made = sem("xn2_made")
            h1_stored = sem("h1_stored")
            tokens_stored = sem("tokens_stored")
            x2t_done = sem("x2t_done")
            x2t_made = sem("x2t_made")
            logits_done = sem("logits_done")
            top_ready = sem("top_ready")
            top_exp = sem("top_exp")
            hot_made = sem("hot_made")
            rank_done = sem("rank_done")
            rank_read = sem("rank_read")
            place_made = sem("place_made")
            listed = sem("listed")
            own = sem("own")
            front_own = sem("front_own")
            divide_own, residual_own, norm2_own, top_own, weights_own, places_own = (
                sem(f"{part}_own") for part in ("divide", "residual", "norm2", "top", "weights", "places"))
            table_blank = sem("table_blank")
            pool_passed = sem("pool_passed")
            dve_passed = sem("dve_passed")
            pe_passed = sem("pe_passed")
            sp_passed = sem("sp_passed")
            rest_split = sem("rest_split")
            q_cleared = sem("q_cleared")
            raw_made = sem("raw_made")
            h0_scaled = sem("h0_scaled")
            h0_next_moved = sem("h0_next_moved")
            h0_kept_moved = sem("h0_kept_moved")

            def here(n):
                return not isinstance(n, int) or 0 <= n < PAIRS

            def upto(value, most):
                return min(value, most) if isinstance(value, int) else value

            def behind(i, w, lag):
                return (i, w - lag) if w >= lag else (i - 1, w - lag + UNITS)

            def do(steps, i, parity, w, half):
                for slot, step in steps:
                    if int(2 * slot) % (2 * UNITS) == 2 * w + half:
                        behind_by = int(2 * slot) // (2 * UNITS)
                        if here(i - behind_by):
                            step(i - behind_by, (parity - behind_by) % 2)

            def walk(eng, body):
                for i in range(-2, LOOP_FROM):
                    body(i, i % 2)
                with eng.Fori(LOOP_FROM // 2, LOOP_TO // 2) as half:
                    body(half * 2, 0)
                    body(half * 2 + 1, 1)
                for i in range(LOOP_TO, PAIRS + 3):
                    body(i, i % 2)

            def keys(b, kt):
                return b * N + kt * K0

            def unit(w):
                return w // 6, w // 3 % 2, w % 3

            def patches(t, k, f):
                rows = STACK + 1 if f == 0 else STACK
                at = MID + f - HOP if k == 1 and f >= HOP else HOP * T * k + f
                return t[:rows, at:at + HOP * (T - 1) + 1:HOP]

            def frames(n):
                if isinstance(n, int):
                    src = x[2 * n], x[2 * n + 1]
                else:
                    src = [x[bass.ds(2 * n + b, 1)].rearrange("b m t -> (b m) t") for b in range(2)]
                return [(xraw[:MELS, 0:BATCH_COLS], src[0][:, 0:BATCH_COLS]),
                        (xraw[:MELS, BATCH_COLS:MID], src[1][:, 0:BATCH_COLS + HOP]),
                        (xraw[:MELS, MID:MID + MID_HALF], src[0][:, HOP * (T + 1):HOP * (T + 1) + MID_HALF]),
                        (xraw[:MELS, MID + MID_HALF:XCOLS], src[1][:, HOP:HOP + MID_HALF])]

            block = mem.enter_context(nc.Block())

            @block.sync
            def _(sp):
                sp.dma_start(stage[:MELS, :], tok_w.rearrange("m f d -> m (f d)")).then_inc(patch_w_loaded, 16)
                sp.dma_start(bias_raw[:, 0, :], tok_b).then_inc(patch_w_loaded, 16)
                sp.dma_start(bias_raw[:, 1, :], b_proj).then_inc(patch_w_loaded, 16)
                for cols, src in frames(0):
                    sp.dma_start(cols, src).then_inc(x_loaded, 16)
                sp.wait_ge(own, 3)
                sp.dma_start(words(xa[STACK:STACK + 1, :]), words(one_line)).then_inc(mel_moved, 16)
                sp.dma_start(words(xb[STACK:STACK + 1, :]), words(one_line)).then_inc(mel_moved, 16)
                sp.dma_start(wr[:], wr_t.rearrange("(c p) e -> p c e", p=P)).then_inc(w_loaded, 16)
                sp.dma_start(br[:], b_router.partition_broadcast(P)).then_inc(w_loaded, 16)
                sp.dma_start(gam[:], gamma.partition_broadcast(P)).then_inc(w_loaded, 16)
                sp.dma_start(bet[:], beta.partition_broadcast(P)).then_inc(w_loaded, 16)
                sp.wait_ge(dve_setup, 4)
                sp.dma_start(words(mel_wa[MELS:STACK, :, :]), words(mel_wl[0:STACK - MELS, :, :])).then_inc(mel_moved, 16)
                sp.dma_start(words(mel_wb[MELS:STACK, :, :]), words(mel_wl[STACK - MELS:MELS, :, :])).then_inc(mel_moved, 16)
                sp.dma_start(words(mel_wa[STACK:STACK + 1, 0, :]), words(bias_hl[:, 0])).then_inc(mel_moved, 16)
                sp.dma_start(words(mel_wb[STACK:STACK + 1, 0, :]), words(bias_hl[:, 1])).then_inc(mel_moved, 16)

                def later_setup():
                    sp.dma_start(words(p_bias[0:1, :]), words(p_bias_hl[:, 0])).then_inc(setup_moved, 16)
                    sp.dma_start(words(p_bias[1:2, :]), words(p_bias_hl[:, 1])).then_inc(setup_moved, 16)
                    sp.dma_start(words(one_rows[0:1, :]), words(one_line[:, 0:T])).then_inc(setup_moved, 16)
                    sp.dma_start(words(one_rows[1:2, :]), words(one_line[:, 0:T])).then_inc(setup_moved, 16)
                    sp.wait_ge(w_stage_free, 1)
                    sp.dma_start(stage[:, 0:CT * D].rearrange("p (c n) -> p c n", c=CT),
                                 wv_t.rearrange("(c p) n -> p c n", p=P)).then_inc(w_loaded, 16)
                    sp.dma_start(stage[:, CT * D:CT * D + 4 * D].rearrange("p (c n) -> p c n", c=4),
                                 wp_t.rearrange("(c p) n -> p c n", p=P)).then_inc(w_loaded, 16)
                    sp.wait_ge(pool_setup, 9)
                    sp.dma_start(table_dram.rearrange("(p n) w -> p (n w)", p=96).bitcast(I32),
                                 blank[:]).then_inc(table_blank, 16)

                def stack(n):
                    h = STACK - MELS
                    sp.wait_ge(xh_made, n)
                    sp.dma_start(words(xa[MELS:STACK, :]), words(xa[0:h, :])).then_inc(x_stacked, 16)
                    sp.dma_start(words(xb[MELS:STACK, :]), words(xa[h:MELS, :])).then_inc(x_stacked, 16)

                def load_x(n2, parts):
                    sp.wait_ge(xl_made, n2)
                    for cols, src in parts:
                        sp.dma_start(cols, src).then_inc(x_loaded, 16)

                def count(value):
                    return value if isinstance(value, int) else sp.snap(value)

                def spread_q(n, ct):
                    wait_apart(sp, qk_lo, n * 4 + 2 * ct + 1, sp_passed)
                    need(sp, scores_done, n * UNITS + 6 * ct - 6)
                    for h in range(HT):
                        sp.dma_start(words(q_diag[HS * h:HS * h + HS, h, :, ct]),
                                     words(q_hl[HS * h:HS * h + HS, :, ct])).then_inc(q_spread[ct], 16)

                def move_den(n):
                    wait_apart(sp, u_made, n * 4 + 4, sp_passed)
                    need(sp, inv_made, n)
                    for g in range(4):
                        h = 4 * g * DEN_CUT
                        sp.dma_start(den[h:h + 4 * DEN_CUT, :], u[HS:P:2 * HS, g, :]).then_inc(den_moved, 16)

                def move_rden(n):
                    wait_apart(sp, inv_made, n + 1, sp_passed)
                    need(sp, spread_done, 4 * n)
                    sp.dma_start(rden[0:HEADS, :], den_inv[:]).then_inc(rden_moved, 16)

                def keep_h0(i):
                    if here(i):
                        if not isinstance(i, int) or i:
                            wait_apart(sp, h1_made, i, sp_passed)
                        sp.wait_ge(h0_next_moved, i * 16 + 16)
                        sp.dma_start(h0_kept[:T], h0_next[:T]).then_inc(h0_kept_moved, 16)
                    if here(i + 1):
                        if here(i):
                            wait_apart(sp, h0_kept_moved, i * 16 + 16, sp_passed)
                        sp.wait_ge(h0_made, i + 2)
                        sp.dma_start(h0_next[:T], h0[:T]).then_inc(h0_next_moved, 16)

                def store_h1(n, at):
                    sp.wait_ge(h1_made, n + 1)
                    sp.dma_start(at, h1[:T]).then_inc(h1_stored, 16)

                def store_tokens(n, at):
                    sp.wait_ge(xn2_made, n + 1)
                    sp.dma_start(at, xn2[:T]).then_inc(tokens_stored, 16)

                def rows_at(a, n):
                    return a[n] if isinstance(n, int) else a[bass.ds(n, 1)].rearrange("p t k d -> (p t) k d")

                def body(i, parity):
                    if here(i - 2):
                        store_tokens(count(i - 2), rows_at(tokens_pairs, i - 2))
                    if here(i - 1):
                        move_den(i - 1)
                    if here(i):
                        spread_q(i, 1)
                    if here(i - 1):
                        move_rden(i - 1)
                    if here(i + 2):
                        stack(count(2 * i + 6))
                    if isinstance(i, int) and i == -2:
                        sp.dma_start(stage[:, 0:CT * 2 * D].rearrange("p (c n) -> p c n", c=CT),
                                     wqk_t.rearrange("(c p) n -> p c n", p=P)).then_inc(w_loaded, 16)
                    if here(i + 3):
                        load_x(count(2 * i + 6), frames(i + 3))
                    if isinstance(i, int) and i == -2:
                        later_setup()
                    if here(i + 1):
                        spread_q(i + 1, 0)
                    keep_h0(i)
                    if isinstance(i, int) and i == PAIRS:
                        sp.wait_ge(pv_done, UNITS * PAIRS)
                        sp.dma_start(w1, w_in_v[0]).then_inc(w_here, 16)
                        sp.wait_ge(xl_made, 2 * PAIRS)
                        sp.dma_start(w2, w_out_v[0]).then_inc(w_here, 16)
                    if here(i - 1):
                        store_h1(count(i - 1), rows_at(out_pairs, i - 1))

                walk(sp, body)
                sp.wait_ge(h1_stored, 16 * PAIRS)
                sp.wait_ge(tokens_stored, 16 * PAIRS)

            @block.gpsimd
            def _(pool):
                setup = [0]

                def made(ins, wait=False):
                    setup[0] += 1
                    ins.then_inc(pool_setup, 1)
                    if wait:
                        pool.wait_ge(pool_setup, setup[0])

                made(pool.memset(ident[:], 0.0))
                made(pool.memset(pick[:], 0.0))
                made(pool.memset(before_f[:], 1.0))
                made(pool.memset(blank[:], 1 << 20), True)
                made(pool.affine_select(out=ident[:], in_=ident[:], compare_op=ALU.not_equal, fill=1.0, base=0,
                                        pattern=[[-1, P]], channel_multiplier=1))
                made(pool.affine_select(out=pick[:].rearrange("p g (j d) -> p g j d", j=4),
                                        in_=pick[:].rearrange("p g (j d) -> p g j d", j=4),
                                        compare_op=ALU.not_equal, fill=1.0, base=0,
                                        pattern=[[4, 4], [1, 4], [0, 2 * HS]], channel_multiplier=-1))
                made(pool.affine_select(out=before_f[:], in_=before_f[:], compare_op=ALU.is_gt, fill=0.0, base=0,
                                        pattern=[[1, T]], channel_multiplier=-1))
                made(pool.iota(expert_id[:], pattern=[[1, E]], base=0, channel_multiplier=0,
                               allow_small_or_imprecise_dtypes=True))
                made(pool.iota(token_id[:], pattern=[[T, TILES]], base=0, channel_multiplier=1,
                               allow_small_or_imprecise_dtypes=True))
                for t in v:
                    made(pool.memset(t[:], 1.0))

                def x_lo(n, half):
                    pool.wait_ge(xh_made, 2 * n + half + 1)
                    need(pool, tok_done, 2 * n)
                    cols = slice(half * (XCOLS // 2), (half + 1) * (XCOLS // 2))
                    pool.tensor_tensor(xb[:MELS, cols], xraw[:MELS, cols], xa[:MELS, cols].bitcast(F32),
                                       ALU.subtract).then_inc(xl_made, 1)

                def affine(n, beta_too):
                    if beta_too:
                        b = bet[:T].rearrange("p (a d) -> p a d", a=1).broadcast_to([T, TILES, D])
                        pool.wait_ge(h0_scaled, n + 1)
                        pool.tensor_tensor(h0[:T], h0[:T], b, ALU.add).then_inc(h0_made, 1)
                        return
                    pool.wait_ge(xhat_made, n + 1)
                    need(pool, h0_next_moved, 16 * n)
                    g = gam[:T].rearrange("p (a d) -> p a d", a=1).broadcast_to([T, TILES, D])
                    pool.tensor_tensor(h0[:T], xn[:T], g, ALU.mult).then_inc(h0_scaled, 1)

                def causal(n, w):
                    ct, b, part = unit(w)
                    buf = probs[w % RING]
                    wait_apart(pool, square_done, n * UNITS + w + 1, pool_passed)
                    if part < 2:
                        a = buf.rearrange("p (h q) -> p h q", h=4)[:, :, 0:K0]
                        pattern = [[0, 4], [1, K0]]
                    else:
                        a = buf[0:K1, 0:HT * K1].rearrange("p (h q) -> p h q", h=HT)
                        pattern = [[0, HT], [1, K1]]
                    pool.affine_select(out=a, in_=a, compare_op=ALU.is_ge, fill=0.0, base=0, pattern=pattern,
                                       channel_multiplier=-1).then_inc(causal_done, 1)

                def attn_lo(n, groups):
                    for g in groups:
                        pool.wait_ge(ah_made, n * 4 + g + 1)
                        if g == 0:
                            need(pool, proj_done, 2 * n)
                        pool.tensor_tensor(al[:, g, :], u[:, g, :], ah[:, g, :].bitcast(F32), ALU.subtract).then_inc(al_made, 1)

                def lists(n, k):
                    wait_apart(pool, place_made, n + 1, pool_passed)
                    for c in range(2):
                        pool.indirect_dma_start(
                            out=table_dram[:, :],
                            out_offset=bass.IndirectOffsetOnAxis(ap=place_i[:T, c, k:k + 1], axis=0),
                            in_=entry[:T, c, k, :], in_offset=None,
                            bounds_check=E * SLOTS - 1, oob_is_err=False).then_inc(listed, 16)

                steps = [
                    (-18.0, lambda n, parity: x_lo(n, 0)),
                    (-17.5, lambda n, parity: x_lo(n, 1)),
                    (-8.5, lambda n, parity: affine(n, False)),
                    (-7.5, lambda n, parity: affine(n, True)),
                    (19.0, lambda n, parity: attn_lo(n, (0,))),
                    (19.0, lambda n, parity: attn_lo(n, (1,))),
                    (19.0, lambda n, parity: attn_lo(n, (2,))),
                    (20.0, lambda n, parity: attn_lo(n, (3,))),
                    (38.0, lambda n, parity: lists(n, 0)),
                    (39.0, lambda n, parity: lists(n, 1)),
                    (40.0, lambda n, parity: lists(n, 2)),
                ]

                def body(i, parity):
                    if isinstance(i, int) and i == -1:
                        pool.wait_ge(mel_moved, 96)
                        pool.wait_ge(setup_moved, 64)
                        pool.memset(words(big[:]), 0.0).then_inc(q_cleared, 1)
                    if isinstance(i, int) and i == 3:
                        pool.wait_ge(table_blank, 16)
                    for w in range(UNITS):
                        do(steps, i, parity, w, 0)
                        n, u_ = behind(i, w, 2)
                        if here(n):
                            causal(n, u_)
                        do(steps, i, parity, w, 1)

                walk(pool, body)
                pool.wait_ge(listed, 16 * 2 * TILES * PAIRS)

            @block.scalar
            def _(act):
                act.preload_act_table_set("natural_log_exp_and_others")
                act.wait_ge(pool_setup, 11)

                def x_hi(n, half):
                    if half == 0:
                        act.wait_ge(x_loaded, n * 64 + 64)
                        need(act, tok_done, 2 * n)
                    cols = slice(half * (XCOLS // 2), (half + 1) * (XCOLS // 2))
                    act.activation(xa[:MELS, cols], xraw[:MELS, cols], ACT.Copy).then_inc(xh_made, 1)

                def take_tok(n, j):
                    act.wait_ge(tok_done, n * 2 + j + 1)
                    if j == 0:
                        need(act, xt_done, 2 * n)
                    cols = TILES - 2 if j else 2
                    act.activation(xn[:T, 2 * j:2 * j + cols, :].rearrange("p k d -> p (k d)"),
                                   work[j][:T, 0:cols * D], ACT.Copy).then_inc(raw_made, 1)

                def guess(n, second):
                    act.wait_ge(ln_var, n * 2 + second + 1)
                    act.activation(lnv[:T], ve[:T], ACT.Ln).then_inc(ln_guess, 1)
                    act.wait_ge(ln_guess, n * 4 + 2 * second + 1)
                    act.activation(ra[:T], lnv[:T], ACT.Exp, scale=-0.5).then_inc(ln_guess, 1)

                def guess2(n):
                    act.wait_ge(ln2_var, n + 1)
                    act.activation(lnv2[:T], ve2[:T], ACT.Ln).then_inc(ln2_guess, 1)
                    act.wait_ge(ln2_guess, n * 2 + 1)
                    act.activation(ra2[:T], lnv2[:T], ACT.Exp, scale=-0.5).then_inc(ln2_guess, 1)

                def xt_hi(n):
                    for c in range(CT):
                        act.wait_ge(xt_done, n * 2 + c + 1)
                        if c == 0:
                            need(act, qk_done, 4 * n)
                        act.activation(xth[:, c, 0:NP], work[c][:, 0:NP], ACT.Copy).then_inc(xth_made, 1)

                def q_hi(n, ct):
                    act.wait_ge(qk_done, n * 4 + 2 * ct + 1)
                    need(act, q_spread[ct], 16 * HT * n)
                    act.activation(q_hl[:, 0, ct, :], work[0][:, 0:NP], ACT.Copy).then_inc(qk_hi, 1)

                def k_hi(n, ct):
                    act.wait_ge(qk_done, n * 4 + 2 * ct + 2)
                    need(act, scores_done, UNITS * n + 6 * ct - 6)
                    act.activation(kh[:, ct, 0:NP], work[1][:, 0:NP], ACT.Copy).then_inc(qk_hi, 1)

                def take_v(n, parity, b):
                    act.wait_ge(v_done, n * 2 + b + 1)
                    if b == 0:
                        need(act, pv_done, UNITS * (n - 1))
                    for kt, rows in ((0, K0), (1, K1)):
                        act.activation(v[parity][:rows, b, kt, :, 0:HS],
                                       work[b][:rows, kt * D:kt * D + D].rearrange("p (h d) -> p h d", h=HEADS),
                                       ACT.Copy).then_inc(v_made, 1)

                def whole(w):
                    return probs[w % RING] if unit(w)[2] < 2 else probs[w % RING][0:K1, 0:HT * K1]

                def expo(n, w):
                    s = 2 * (w % 2)
                    act.wait_ge(scores_done, n * UNITS + w + 1)
                    need(act, pv_done, n * UNITS + w + 1 - RING)
                    if unit(w)[2] < 2:
                        src, dst = score[:, s:s + 2, 0:2 * N], whole(w).rearrange("p (a q) -> p a q", a=2)
                    else:
                        src, dst = score[0:K1, s, 0:HT * K1], whole(w)
                    act.activation(dst, src, ACT.Exp, scale=SCALE).then_inc(exp_done, 1)

                def loga(n, w):
                    act.wait_ge(clamp_done, n * UNITS + w + 1)
                    act.activation(whole(w), whole(w), ACT.Ln, bias=1.0).then_inc(ln_done, 1)

                def square(n, w):
                    act.wait_ge(max_done, n * UNITS + w + 1)
                    act.activation(whole(w), whole(w), ACT.Square).then_inc(square_done, 1)

                def take_u(n, ct):
                    act.wait_ge(pv_done, n * UNITS + 6 * ct + 6)
                    if ct == 0:
                        need(act, al_made, 4 * n)
                    for j in range(2):
                        act.activation(u[:, 2 * ct + j, :], heads_out[j][:, 0:NP], ACT.Copy).then_inc(u_made, 1)

                def attn_hi(n, groups):
                    for g in groups:
                        act.wait_ge(attn_made, n * 4 + g + 1)
                        if g == 0:
                            need(act, proj_done, 2 * n)
                        act.activation(ah[:, g, :], u[:, g, :], ACT.Copy).then_inc(ah_made, 1)

                def x2t_copy(n):
                    for c in range(CT):
                        act.wait_ge(x2t_done, n * 2 + c + 1)
                        if c == 0:
                            need(act, logits_done, n)
                        act.activation(x2t[:, c, :], work[c][:, 0:NP], ACT.Copy).then_inc(x2t_made, 1)

                def top_exps(n):
                    act.wait_ge(top_ready, n + 1)
                    act.activation(tope[:T], topd[:T], ACT.Exp).then_inc(top_exp, 1)

                steps = [
                    (-20.5, lambda n, parity: x_hi(n, 0)),
                    (-18.5, lambda n, parity: x_hi(n, 1)),
                    (-10.5, lambda n, parity: take_tok(n, 0)),
                    (24.0, lambda n, parity: guess2(n)),
                    (-10.0, lambda n, parity: take_tok(n, 1)),
                    (-9.5, lambda n, parity: guess(n, 0)),
                    (-6.5, lambda n, parity: guess(n, 1)),
                    (-3.5, lambda n, parity: xt_hi(n)),
                    (-2.0, lambda n, parity: q_hi(n, 0)),
                    (-2.0, lambda n, parity: k_hi(n, 0)),
                    (-0.5, lambda n, parity: take_v(n, parity, 0)),
                    (0.5, lambda n, parity: take_v(n, parity, 1)),
                    (2.5, lambda n, parity: q_hi(n, 1)),
                    (2.5, lambda n, parity: k_hi(n, 1)),
                    (9.0, lambda n, parity: take_u(n, 0)),
                    (15.0, lambda n, parity: take_u(n, 1)),
                    (18.5, lambda n, parity: attn_hi(n, (0,))),
                    (18.5, lambda n, parity: attn_hi(n, (1,))),
                    (19.5, lambda n, parity: attn_hi(n, (2,))),
                    (19.5, lambda n, parity: attn_hi(n, (3,))),
                    (28.0, lambda n, parity: x2t_copy(n)),
                    (30.5, lambda n, parity: top_exps(n)),
                ]

                def body(i, parity):
                    if isinstance(i, int) and i == PAIRS + 1:
                        act.wait_ge(w_here, 32)
                        act.wait_ge(scores_done, UNITS * PAIRS)
                        act.activation(w1h0, w1, ACT.Copy).then_inc(w_hi, 1)
                        act.activation(w2h0, w2, ACT.Copy).then_inc(w_hi, 1)
                    for w in range(UNITS):
                        do(steps, i, parity, w, 0)
                        n, u_ = behind(i, w, 1)
                        if here(n):
                            loga(n, u_)
                        if here(i):
                            expo(i, w)
                        n, u_ = behind(i, w, 2)
                        if here(n):
                            square(n, u_)
                        do(steps, i, parity, w, 1)

                walk(act, body)

            @block.vector
            def _(dve):
                wst = stage[:MELS, :].rearrange("p (f d) -> p f d", f=TAPS)
                links = [0]

                def link(ins):
                    links[0] += 1
                    ins.then_inc(own, 1)
                    dve.wait_ge(own, links[0])

                link(dve.memset(p_bias[:].bitcast(F32), 0.0))
                link(dve.memset(one_rows[:].bitcast(F32), 0.0))
                link(dve.memset(one_line.bitcast(F32), 1.0))
                dve.wait_ge(patch_w_loaded, 16 * 3)
                link(dve.tensor_copy(mel_wa[:MELS], wst))
                link(dve.tensor_copy(bias_hl[:, 0, :], bias_raw[:, 0, :]))
                link(dve.tensor_copy(p_bias_hl[:, 0, :], bias_raw[:, 1, :]))
                dve.tensor_tensor(mel_wl[:MELS], wst, mel_wa[:MELS].bitcast(F32), ALU.subtract).then_inc(dve_setup, 1)
                dve.tensor_copy(mel_wb[:MELS], wst).then_inc(dve_setup, 1)
                dve.tensor_tensor(bias_hl[:, 1, :], bias_raw[:, 0, :], bias_hl[:, 0, :].bitcast(F32),
                                  ALU.subtract).then_inc(dve_setup, 1)
                dve.tensor_tensor(p_bias_hl[:, 1, :], bias_raw[:, 1, :], p_bias_hl[:, 0, :].bitcast(F32),
                                  ALU.subtract).then_inc(dve_setup, 1)
                for t in (xth, xtl, kh, kl):
                    dve.memset(t[:, :, NP:KPAD].bitcast(F32), 0.0).then_inc(dve_setup, 1)
                dve.memset(ones_b[:], 1.0).then_inc(dve_setup, 1)
                dve.memset(rden[:], 0.0).then_inc(dve_setup, 1)
                dve.memset(seen[0][:], 0.0).then_inc(dve_setup, 1)
                dve.memset(seen_b[:], 0.0).then_inc(dve_setup, 1)
                dve.wait_ge(pool_setup, 9)
                dve.tensor_copy(before[:], before_f[:]).then_inc(dve_setup, 1)
                SETUP = 13
                dve.wait_ge(dve_setup, SETUP)

                def split_rest():
                    sv = stage[:, 0:CT * 2 * D].rearrange("p (c n) -> p c n", c=CT)
                    dve.wait_ge(w_loaded, 16 * 5)
                    link(dve.tensor_copy(qk_wh[:], sv))
                    dve.tensor_tensor(qk_wl[:], sv, qk_wh[:].bitcast(F32), ALU.subtract).then_inc(w_stage_free, 1)
                    dve.wait_ge(w_loaded, 16 * 7)
                    sv2 = stage[:, 0:CT * D].rearrange("p (c n) -> p c n", c=CT)
                    sv3 = stage[:, CT * D:CT * D + 4 * D].rearrange("p (c n) -> p c n", c=4)
                    link(dve.tensor_copy(v_wh[:], sv2))
                    link(dve.tensor_copy(p_wh[:], sv3))
                    dve.tensor_tensor(v_wl[:], sv2, v_wh[:].bitcast(F32), ALU.subtract).then_inc(rest_split, 1)
                    dve.tensor_tensor(p_wl[:], sv3, p_wh[:].bitcast(F32), ALU.subtract).then_inc(rest_split, 1)

                def chain(signal, per, n, done):
                    count = [done]

                    def step(ins, apart=False):
                        count[0] += 1
                        ins.then_inc(signal, 1)
                        if apart:
                            wait_apart(dve, signal, n * per + count[0], dve_passed)
                        else:
                            dve.wait_ge(signal, n * per + count[0])
                    return step, count

                def mean_var(src, st, m, v_, signal, step):
                    for k in range(TILES):
                        last = dve.bn_stats(st[:T, k, :], src[:T, k, :])
                    step(last, True)
                    for k in range(TILES):
                        last = dve.bn_aggr(m[:T, k, :], st[:T, k, :])
                    step(last)
                    dve.tensor_scalar(v_[:T], m[:T, :, 1], EPS, None, ALU.add).then_inc(signal, 1)

                def newton(v_, a, b, c, r, step):
                    step(dve.tensor_tensor(b[:T], a[:T], a[:T], ALU.mult))
                    step(dve.scalar_tensor_tensor(out=c[:T], in0=b[:T], scalar=-0.5, in1=v_[:T],
                                                  op0=ALU.mult, op1=ALU.mult))
                    step(dve.scalar_tensor_tensor(out=r[:T], in0=c[:T], scalar=1.5, in1=a[:T],
                                                  op0=ALU.add, op1=ALU.mult))

                def normalise(dst, src, m, r):
                    for k in range(TILES):
                        last = dve.tensor_scalar(dst[:T, k, :], src[:T, k, :], m[:T, k, 0:1], r[:T, k:k + 1],
                                                 ALU.subtract, ALU.mult)
                    return last

                FRONT = 10

                def front_a(n):
                    step, _ = chain(front_own, FRONT, n, 0)
                    dve.wait_ge(raw_made, n * 2 + 2)
                    need(dve, xn_made, n)
                    mean_var(xn, stats, mv, ve, ln_var, step)

                def front_b(n):
                    step, _ = chain(front_own, FRONT, n, 2)
                    dve.wait_ge(ln_guess, n * 4 + 2)
                    newton(ve, ra, rb, rc, rstd, step)
                    normalise(xn, xn, mv, rstd).then_inc(xhat_made, 1)

                def front_c(n):
                    step, _ = chain(front_own, FRONT, n, 5)
                    dve.wait_ge(h0_made, n + 1)
                    mean_var(h0, stats, mv, ve, ln_var, step)

                def front_d(n):
                    step, c = chain(front_own, FRONT, n, 7)
                    dve.wait_ge(ln_guess, n * 4 + 4)
                    newton(ve, ra, rb, rc, rstd, step)
                    normalise(xn, h0, mv, rstd).then_inc(xn_made, 1)
                    assert c[0] == FRONT

                def xt_lo(n):
                    for c in range(CT):
                        dve.wait_ge(xth_made, n * 2 + c + 1)
                        dve.tensor_tensor(xtl[:, c, 0:NP], work[c][:, 0:NP], xth[:, c, 0:NP].bitcast(F32),
                                          ALU.subtract).then_inc(xtl_made, 1)

                def q_lo(n, ct):
                    dve.wait_ge(qk_hi, n * 4 + 2 * ct + 1)
                    dve.tensor_tensor(q_hl[:, 1, ct, :], work[0][:, 0:NP], q_hl[:, 0, ct, :].bitcast(F32),
                                      ALU.subtract).then_inc(qk_lo, 1)

                def k_lo(n, ct):
                    dve.wait_ge(qk_hi, n * 4 + 2 * ct + 2)
                    dve.tensor_tensor(kl[:, ct, 0:NP], work[1][:, 0:NP], kh[:, ct, 0:NP].bitcast(F32),
                                      ALU.subtract).then_inc(qk_lo, 1)

                def whole(w):
                    return probs[w % RING] if unit(w)[2] < 2 else probs[w % RING][0:K1, 0:HT * K1]

                def clamp(n, w):
                    dve.wait_ge(exp_done, n * UNITS + w + 1)
                    dve.tensor_scalar(whole(w), whole(w), LN_MAX, None, ALU.min).then_inc(clamp_done, 1)

                def soft(n, w):
                    s = 2 * (w % 2)
                    dve.wait_ge(ln_done, n * UNITS + w + 1)
                    if unit(w)[2] < 2:
                        x_, a = score[:, s:s + 2, 0:2 * N], whole(w).rearrange("p (a q) -> p a q", a=2)
                    else:
                        x_, a = score[0:K1, s, 0:HT * K1], whole(w)
                    dve.scalar_tensor_tensor(out=a, in0=x_, scalar=SCALE, in1=a, op0=ALU.mult,
                                             op1=ALU.max).then_inc(max_done, 1)

                def divide(n):
                    step, _ = chain(divide_own, 1, n, 0)
                    dve.wait_ge(den_moved, n * 64 + 64)
                    need(dve, rden_moved, 16 * n)
                    step(dve.tensor_scalar(den_eps[:], den[:], DEN_EPS, None, ALU.add))
                    dve.reciprocal(den_inv[:], den_eps[:]).then_inc(inv_made, 1)

                def scale_heads(n, groups):
                    for g in groups:
                        dve.wait_ge(spread_done, n * 4 + g + 1)
                        dve.tensor_tensor(u[:, g, :], u[:, g, :], work[g % 2][:, 0:NP], ALU.mult).then_inc(attn_made, 1)

                def residual(n):
                    step, _ = chain(residual_own, 2, n, 0)
                    need(dve, h1_stored, 16 * n)
                    need(dve, xn2_made, n)
                    dve.wait_ge(h0_kept_moved, n * 16 + 16)
                    dve.wait_ge(proj_done, n * 2 + 1)
                    dve.tensor_tensor(h1[:T, 0:2, :], work[0][:T, :].rearrange("p (k d) -> p k d", k=2),
                                      h0_kept[:T, 0:2, :], ALU.add).then_inc(proj_taken, 1)
                    dve.wait_ge(proj_done, n * 2 + 2)
                    dve.tensor_tensor(h1[:T, 2, :], work[1][:T, 0:D], h0_kept[:T, 2, :], ALU.add).then_inc(h1_made, 1)
                    dve.wait_ge(h1_made, n + 1)
                    mean_var(h1, stats2, mv2, ve2, ln2_var, step)

                def norm2(n):
                    step, c = chain(norm2_own, 3, n, 0)
                    dve.wait_ge(ln2_guess, n * 2 + 2)
                    need(dve, x2t_done, 2 * n)
                    need(dve, tokens_stored, 16 * n)
                    newton(ve2, ra2, rb2, rc2, rstd2, step)
                    normalise(xn2, h1, mv2, rstd2).then_inc(xn2_made, 1)

                def top_two(n):
                    step, _ = chain(top_own, 3, n, 0)
                    dve.wait_ge(logits_done, n + 1)
                    step(dve.tensor_tensor(lg[:T], work[1][:T, ASIDE:ASIDE + TILES * E].rearrange("p (k e) -> p k e", k=TILES),
                                           br[:T].rearrange("p (a e) -> p a e", a=1).broadcast_to([T, TILES, E]), ALU.add), True)
                    for k in range(TILES):
                        last = dve.max(top[:T, k, :], lg[:T, k, :])
                    step(last)
                    need(dve, top_exp, n)
                    dve.tensor_tensor(topd[:T], top[:T], top[:T, :, 0:1].broadcast_to([T, TILES, 8]),
                                      ALU.subtract).then_inc(top_ready, 1)
                    for k in range(TILES):
                        last = dve.max_index(top_at[:T, k, :], top[:T, k, :], lg[:T, k, :])
                    step(last)

                def weights(n):
                    step, c = chain(weights_own, 6, n, 0)
                    dve.wait_ge(top_exp, n + 1)
                    step(dve.tensor_reduce(tsum[:T], tope[:T], AX.X, ALU.add))
                    step(dve.reciprocal(trec[:T], tsum[:T]))
                    need(dve, listed, n * (16 * 2 * TILES))
                    for j in range(2):
                        last = dve.tensor_tensor(entry[:T, j, :, 1], tope[:T, :, j], trec[:T], ALU.mult)
                    step(last)
                    for j in range(2):
                        last = dve.tensor_scalar(valid[:T, j, :], entry[:T, j, :, 1], 0.0, None, ALU.is_gt)
                    dve.tensor_copy(at_f[:T], top_at[:T, :, 0:2])
                    step(dve.tensor_copy(entry[:T, :, :, 0].bitcast(I32),
                                         token_id[:T].rearrange("p (a k) -> p a k", a=1).broadcast_to([T, 2, TILES])))
                    dve.tensor_scalar(token_id[:T], token_id[:T], float(NP), None, ALU.add)
                    for j in range(2):
                        last = dve.tensor_tensor(hot[:T, j],
                                                 expert_id[:T].rearrange("p (a e) -> p a e", a=1).broadcast_to([T, TILES, E]),
                                                 at_f[:T, :, j:j + 1].broadcast_to([T, TILES, E]), ALU.is_equal)
                    step(last)
                    for j in range(2):
                        last = dve.tensor_tensor(hot[:T, j], hot[:T, j],
                                                 valid[:T, j, :].rearrange("p (k a) -> p k a", a=1).broadcast_to([T, TILES, E]),
                                                 ALU.mult)
                    step(last)
                    dve.tensor_tensor(hot_b[:T], hot[:T, 0], hot[:T, 1], ALU.add).then_inc(hot_made, 1)

                def read_ranks(n):
                    dve.wait_ge(rank_done, n + 1)
                    dve.tensor_copy(rank[:T], work[1][:T, ASIDE:ASIDE + TILES * E].rearrange("p (k e) -> p k e",
                                                                              k=TILES)).then_inc(rank_read, 1)

                def places(n):
                    step, c = chain(places_own, TILES + 5, n, 0)
                    for k in range(TILES):
                        step(dve.tensor_tensor(seen[k + 1][:T], seen[k][:T], hot_b[:T, k, :], ALU.add))
                    dve.wait_ge(rank_read, n + 1)
                    dve.tensor_copy(seen[0][:T], seen[TILES][:T])
                    dve.tensor_copy(seen_b[:T], seen[TILES][:T])
                    for j in range(2):
                        last = dve.tensor_tensor(mine[:T, j], hot[:T, j], rank[:T], ALU.mult)
                    step(last)
                    step(dve.tensor_reduce(place[:T], mine[:T], AX.X, ALU.add))
                    step(dve.tensor_scalar(over[:T], place[:T], float(CAP), BIG, ALU.is_ge, ALU.mult))
                    step(dve.tensor_tensor(place2[:T], place[:T], over[:T], ALU.add))
                    dve.tensor_scalar(over[:T], valid[:T], -BIG, BIG, ALU.mult, ALU.add)
                    for j in range(2):
                        last = dve.scalar_tensor_tensor(out=place[:T, j], in0=at_f[:T, :, j], scalar=float(SLOTS),
                                                        in1=place2[:T, j], op0=ALU.mult, op1=ALU.add)
                    step(last)
                    dve.tensor_tensor(place_i[:T], place[:T], over[:T], ALU.add).then_inc(place_made, 1)
                    assert c[0] == TILES + 5

                steps = [
                    (25.5, lambda n, parity: norm2(n)),
                    (-10.5, lambda n, parity: front_a(n)),
                    (-9.5, lambda n, parity: front_b(n)),
                    (-6.5, lambda n, parity: front_c(n)),
                    (18.5, lambda n, parity: scale_heads(n, (0,))),
                    (18.5, lambda n, parity: scale_heads(n, (1,))),
                    (19.5, lambda n, parity: scale_heads(n, (2,))),
                    (19.5, lambda n, parity: scale_heads(n, (3,))),
                    (-5.0, lambda n, parity: front_d(n)),
                    (-3.5, lambda n, parity: xt_lo(n)),
                    (-2.0, lambda n, parity: q_lo(n, 0)),
                    (-2.0, lambda n, parity: k_lo(n, 0)),
                    (2.5, lambda n, parity: q_lo(n, 1)),
                    (3.0, lambda n, parity: k_lo(n, 1)),
                    (15.5, lambda n, parity: divide(n)),
                    (22.5, lambda n, parity: residual(n)),
                    (29.5, lambda n, parity: top_two(n)),
                    (33.0, lambda n, parity: weights(n)),
                    (34.5, lambda n, parity: read_ranks(n)),
                    (36.5, lambda n, parity: places(n)),
                ]

                def body(i, parity):
                    if isinstance(i, int) and i == PAIRS + 1:
                        dve.wait_ge(w_hi, 1)
                        dve.tensor_tensor(w1l0, w1, words(w1h0), ALU.subtract).then_inc(w_lo, 1)
                    for w in range(UNITS):
                        do(steps, i, parity, w, 0)
                        n, u_ = behind(i, w, 1)
                        if here(n):
                            soft(n, u_)
                        if here(i):
                            clamp(i, w)
                        do(steps, i, parity, w, 1)

                split_rest()
                walk(dve, body)

            @block.tensor
            def _(pe):
                def products(o, terms):
                    for t, (lhs, rhs) in enumerate(terms):
                        last = pe.matmul(o, lhs, rhs, start=(t == 0), stop=(t == len(terms) - 1))
                    return last

                def tok_tiles(n, tiles):
                    if 0 in tiles:
                        pe.wait_ge(x_stacked, n * 32 + 32)
                        pe.wait_ge(xl_made, 2 * n + 2)
                        need(pe, v_made, 4 * n - 2)
                    if 2 in tiles:
                        need(pe, v_made, 4 * n)
                    for k in tiles:
                        o = work[k // 2][:T, (k % 2) * D:(k % 2) * D + D]
                        last = products(o, [(patches(a, k, f), m[:STACK + (1 if f == 0 else 0), f, :])
                                            for f in range(TAPS) for a, m in ((xa, mel_wa), (xb, mel_wb))])
                        if k:
                            last.then_inc(tok_done, 1)

                def turn(src, c, signal):
                    for k in range(TILES):
                        last = pe.transpose(work[c][:, k * T:k * T + T], src[:T, k, c * P:c * P + P], ident[:T, :T])
                    last.then_inc(signal, 1)

                def turn_x(n):
                    pe.wait_ge(xn_made, n + 1)
                    need(pe, attn_made, 4 * (n - 1))
                    need(pe, qk_lo, 4 * n)
                    turn(xn, 0, xt_done)
                    turn(xn, 1, xt_done)

                def turn_x2(n):
                    pe.wait_ge(xn2_made, n + 1)
                    pe.wait_ge(qk_lo, upto(4 * n + 12, 4 * PAIRS))
                    turn(xn2, 0, x2t_done)
                    turn(xn2, 1, x2t_done)

                def spread_rden(n, groups):
                    for g in groups:
                        if g == 0:
                            pe.wait_ge(rden_moved, 16 * n + 16)
                            pe.wait_ge(qk_lo, upto(4 * n + 8, 4 * PAIRS))
                            need(pe, x2t_made, 2 * n)
                        if g >= 2:
                            pe.wait_ge(attn_made, n * 4 + g - 1)
                        if g == 1:
                            need(pe, top_ready, n)
                        pe.matmul(work[g % 2][:, 0:NP], pick[:, g, :], rden[:], start=True,
                                  stop=True).then_inc(spread_done, 1)

                def project(n, tiles):
                    if 0 in tiles:
                        pe.wait_ge(al_made, n * 4 + 4)
                        pe.wait_ge(qk_lo, upto(4 * n + 10, 4 * PAIRS))
                    for k in tiles:
                        o = work[k // 2][:T, (k % 2) * D:(k % 2) * D + D]
                        sl = slice(k * T, k * T + T)
                        last = products(o, [(one_rows[:, :], p_bias[:])] +
                                        [(a[:, g, sl], wt[:, g, :]) for g in range(4)
                                         for a, wt in ((ah, p_wh), (al, p_wh), (ah, p_wl))])
                        if k:
                            last.then_inc(proj_done, 1)

                def logits(n):
                    pe.wait_ge(x2t_made, n * 2 + 2)
                    for k in range(TILES):
                        last = products(work[1][:T, ASIDE + k * E:ASIDE + k * E + E],
                                        [(x2t[:, c, k * T:k * T + T], wr[:, c, :]) for c in range(CT)])
                    last.then_inc(logits_done, 1)

                def ranks(n):
                    pe.wait_ge(hot_made, n + 1)
                    pe.wait_ge(qk_lo, upto(4 * n + 14, 4 * PAIRS))
                    for k in range(TILES):
                        last = products(work[1][:T, ASIDE + k * E:ASIDE + k * E + E],
                                        [(before[:T, :], hot_b[:T, k, :])] +
                                        [(ones_b[:T, :], hot_b[:T, j, :]) for j in range(k)] +
                                        [(ones_b[:T, :], seen_b[:T, :])])
                    last.then_inc(rank_done, 1)

                def qk(n, ct, parts):
                    for s in parts:
                        if s == 0:
                            pe.wait_ge(xtl_made, n * 2 + 2)
                        if ct:
                            pe.wait_ge(raw_made, upto(2 * n + 3 + s, 2 * PAIRS))
                        col = (2 * s + ct) * P
                        products(work[s][:, 0:NP],
                                 [(wt[:, c, col:col + P], xt[:, c, 0:NP])
                                  for c in range(CT) for wt, xt in ((qk_wh, xth), (qk_wh, xtl), (qk_wl, xth))]
                                 ).then_inc(qk_done, 1)

                def values(n, b):
                    pe.wait_ge(qk_lo, n * 4 + b + 1)
                    if b == 0:
                        need(pe, proj_taken, n - 1)
                    else:
                        need(pe, h1_made, n - 1)
                        need(pe, rank_read, n - 2)
                    for kt in range(2):
                        a = keys(b, kt)
                        last = products(work[b][:, kt * D:kt * D + D],
                                        [(xt[:, c, a:a + P], wt[:, c, :])
                                         for c in range(CT) for xt, wt in ((xth, v_wh), (xtl, v_wh), (xth, v_wl))])
                    last.then_inc(v_done, 1)

                def scores(n, w):
                    ct, b, part = unit(w)
                    s = 2 * (w % 2)
                    need(pe, max_done, n * UNITS + w - 1)
                    if w % 6 == 0:
                        pe.wait_ge(qk_lo, n * 4 + 2 * ct + 2)
                        pe.wait_ge(q_spread[ct], n * (16 * HT) + 16 * HT)
                    a = keys(b, part // 2)
                    for j in range(2 if part < 2 else 1):
                        h = part * 4 + 2 * j
                        if part < 2:
                            rhs = [q_diag[:, h:h + 2, x_, ct, b * N:b * N + N] for x_ in range(2)]
                            o = score[:, s + j, 0:2 * N].rearrange("p (h q) -> p h q", h=2)
                        else:
                            rhs = [q_diag[:, :, x_, ct, b * N + K0:b * N + N] for x_ in range(2)]
                            o = score[:, s, 0:HT * K1].rearrange("p (h q) -> p h q", h=HT)
                        last = products(o, [(kh[:, ct, a:a + P], rhs[0]), (kh[:, ct, a:a + P], rhs[1]),
                                            (kl[:, ct, a:a + P], rhs[0])])
                    last.then_inc(scores_done, 1)

                def weigh(n, w, values_at):
                    ct, b, part = unit(w)
                    buf = probs[w % RING]
                    if w == 0:
                        pe.wait_ge(v_made, n * 4 + 4)
                        need(pe, u_made, 4 * n)
                    if w == 6:
                        pe.wait_ge(u_made, n * 4 + 2)
                    wait_apart(pe, causal_done, n * UNITS + w + 1, pe_passed)
                    if part < 2:
                        for j in range(4):
                            last = pe.matmul(heads_out[part][32 * j:32 * j + 32, b * N:b * N + N],
                                             values_at[:, b, 0, HT * ct + 4 * part + j, :], buf[:, j * N:j * N + N],
                                             start=True, stop=False, skip_group_check=True)
                    else:
                        for g in range(2):
                            for j in range(4):
                                h = 4 * g + j
                                last = pe.matmul(heads_out[g][32 * j:32 * j + 32, b * N + K0:b * N + N],
                                                 values_at[0:K1, b, 1, HT * ct + h, :], buf[0:K1, h * K1:h * K1 + K1],
                                                 start=False, stop=True, skip_group_check=True)
                    last.then_inc(pv_done, 1)

                pe.wait_ge(mel_moved, 96)

                def project_and_rank(n, parity):
                    if here(n - 1):
                        ranks(n - 1)
                    project(n, (2,))

                pe.wait_ge(pool_setup, 11)
                steps = [
                    (-4.5, lambda n, parity: turn_x(n)),
                    (-3.0, lambda n, parity: qk(n, 0, (0,))),
                    (-3.0, lambda n, parity: qk(n, 0, (1,))),
                    (21.5, lambda n, parity: project(n, (0,))),
                    (21.5, lambda n, parity: project(n, (1,))),
                    (21.5, project_and_rank),
                    (-1.5, lambda n, parity: values(n, 0)),
                    (-0.5, lambda n, parity: values(n, 1)),
                    (-11.5, lambda n, parity: tok_tiles(n, (0,))),
                    (-11.5, lambda n, parity: tok_tiles(n, (1,))),
                    (-11.5, lambda n, parity: tok_tiles(n, (2,))),
                    (1.5, lambda n, parity: qk(n, 1, (0,))),
                    (1.5, lambda n, parity: qk(n, 1, (1,))),
                    (27.5, lambda n, parity: turn_x2(n)),
                    (27.5, lambda n, parity: logits(n)),
                    (17.5, lambda n, parity: spread_rden(n, (0, 1))),
                    (18.5, lambda n, parity: spread_rden(n, (2, 3))),
                ]

                def body(i, parity):
                    for w in range(UNITS):
                        do(steps, i, parity, w, 0)
                        if isinstance(i, int) and (i, w) == (-1, 8):
                            pe.wait_ge(rest_split, 2)
                            pe.wait_ge(q_cleared, 1)
                            pe.wait_ge(setup_moved, 64)
                        if isinstance(i, int) and (i, w) == (PAIRS + 1, 11):
                            ranks(PAIRS - 1)
                        n, u_ = behind(i, w, 3)
                        if here(n):
                            weigh(n, u_, v[parity if w >= 3 else 1 - parity])
                        n, u_ = behind(i + 1, w, UNITS - 1)
                        if here(n):
                            scores(n, u_)
                        do(steps, i, parity, w, 1)

                walk(pe, body)

        with ExitStack() as mem:
            def sb(name, shape, dt=F32):
                return mem.enter_context(nc.sbuf_tensor(name, shape, dt))

            def bank(name):
                return mem.enter_context(nc.psum_tensor(name, [P, 512], F32))

            turned = [bank(f"turned{i}") for i in range(2)]
            inner = [bank(f"inner{i}") for i in range(4)]
            rows = [bank(f"rows{i}") for i in range(2)]

            ident2 = sb("ident2", [P, P])
            lists_sb = [sb(f"lists{i}", [P, STILES, 2]) for i in range(2)]
            got = [sb(f"got{i}", [P, STILES, D]) for i in range(2)]
            w1h = [w1h0, sb("w1h1", [P, CT, INNER], F32R)[:]]
            w1l = [w1l0, sb("w1l1", [P, CT, INNER], F32R)[:]]
            w2h = [w2h0, sb("w2h1", [P, ITILES, D], F32R)[:]]
            w2l = [sb(f"w2l{i}", [P, ITILES, D], F32R)[:] for i in range(2)]
            gth = sb("gth", [P, 2, CT, HALF], F32R)
            gtl = sb("gtl", [P, 2, CT, HALF], F32R)
            hh = [sb(f"hh{a}", [P, ITILES, HALF], F32R) for a in range(2)]
            hl = [sb(f"hl{a}", [P, ITILES, HALF], F32R) for a in range(2)]
            y = sb("y", [P, STILES, D])
            ROUND = ITILES // 2

            lists_loaded = [sem("lists_loaded0"), sem("lists_loaded1")]
            gathered = [[sem(f"gathered{b}{a}") for a in range(2)] for b in range(2)]
            id_made = sem("id_made")
            got_clear = sem("got_clear")
            turned_done = sem("turned_done")
            gt_hi = sem("gt_hi")
            gt_lo = sem("gt_lo")
            inner_done = sem("inner_done")
            inner_hi = sem("inner_hi")
            inner_lo = sem("inner_lo")
            rows_done = sem("rows_done")
            y_made = sem("y_made")
            added = sem("added")
            pool_passed = sem("pool_passed_too")
            HT2 = STILES // 2

            block = mem.enter_context(nc.Block())

            @block.sync
            def _(sp):
                def load(n, m, lists_at, w1_at, w2_at):
                    if m["added"] is not None:
                        sp.wait_ge(added, m["added"])
                    sp.dma_start(lists_sb[n % 2][:S], lists_at).then_inc(lists_loaded[n % 2], 16)
                    if m["lo"] is not None:
                        sp.wait_ge(w_lo, m["lo"])
                    if w1_at is not None:
                        sp.dma_start(w1, w1_at).then_inc(w_here, 16)
                        sp.dma_start(w2, w2_at).then_inc(w_here, 16)

                load(0, dict(added=None, lo=None), table_experts[0], None, None)
                load(1, dict(added=None, lo=2), table_experts[1], w_in_v[1], w_out_v[1])
                with sp.Fori(0, E // 2 - 1) as step:
                    e = step * 2
                    at = [(dict(added=sp.snap(e * (16 * STILES) + 16 * STILES * (b + 1)), lo=sp.snap(e * 2 + 2 * (b + 2))),
                           table_experts[bass.ds(e + (2 + b), 1)].rearrange("e t s w -> (e t) s w"),
                           w_in_v[bass.ds(e + (2 + b), 1)].rearrange("e p c i -> (e p) c i"),
                           w_out_v[bass.ds(e + (2 + b), 1)].rearrange("e p t d -> (e p) t d")) for b in range(2)]
                    for b in range(2):
                        load(b, *at[b])

            @block.gpsimd
            def _(pool):
                pool.memset(ident2[:], 0.0).then_inc(id_made, 1)
                pool.wait_ge(id_made, 1)
                pool.affine_select(out=ident2[:], in_=ident2[:], compare_op=ALU.not_equal, fill=1.0, base=0,
                                   pattern=[[-1, P]], channel_multiplier=1).then_inc(id_made, 1)
                for b in range(2):
                    pool.memset(got[b][:], 0.0).then_inc(got_clear, 1)
                pool.wait_ge(got_clear, 2)

                def gather(m, b):
                    pool.wait_ge(lists_loaded[b], m * 16 + 16)
                    wait_apart(pool, turned_done, m * 8 + (4 * b - 4), pool_passed)
                    for s in range(STILES):
                        pool.indirect_dma_start(
                            out=got[b][:S, s, :], out_offset=None, in_=tokens_dram[:, :],
                            in_offset=bass.IndirectOffsetOnAxis(ap=lists_sb[b][:S, s, 0:1].bitcast(U32), axis=0),
                            bounds_check=TOKENS - 1, oob_is_err=False).then_inc(gathered[b][s // HT2], 16)

                def add(n, b):
                    need(pool, added, n * (16 * STILES))
                    for s in range(STILES):
                        wait_apart(pool, y_made, n * STILES + s + 1, pool_passed)
                        pool.indirect_dma_start(
                            out=out[:, :],
                            out_offset=bass.IndirectOffsetOnAxis(ap=lists_sb[b][:S, s, 0:1].bitcast(U32), axis=0),
                            in_=y[:S, s, :], in_offset=None, bounds_check=TOKENS - 1, oob_is_err=False,
                            compute_op=ALU.add).then_inc(added, 16)

                gather(0, 0)
                gather(0, 1)
                add(0, 0)
                gather(1, 0)
                add(1, 1)
                gather(1, 1)
                add(2, 0)
                with pool.Fori(1, E // 2 - 1) as step:
                    e = step * 2
                    gather(step + 1, 0)
                    add(e + 1, 1)
                    gather(step + 1, 1)
                    add(e + 2, 0)
                add(E - 1, 1)
                pool.wait_ge(added, 16 * STILES * E)

            @block.scalar
            def _(act):
                act.preload_act_table_set("natural_log_exp_and_others")

                def weights_hi(n, b):
                    act.wait_ge(w_here, n * 32 + 32)
                    need(act, rows_done, (n - 1) * STILES)
                    act.activation(w1h[b], w1, ACT.Copy).then_inc(w_hi, 1)
                    act.activation(w2h[b], w2, ACT.Copy).then_inc(w_hi, 1)

                def tokens_hi(n, a):
                    for c in range(CT):
                        act.wait_ge(turned_done, n * 4 + a * 2 + c + 1)
                        if a == 0 and c == 0:
                            need(act, inner_done, n * (2 * ITILES))
                        act.activation(gth[:, a, c, :], turned[c][:, 0:HALF], ACT.Copy).then_inc(gt_hi, 1)

                def relu_hi(n, a):
                    for t in range(ITILES):
                        act.wait_ge(inner_done, n * (2 * ITILES) + a * ITILES + t + 1)
                        if t == 0:
                            need(act, rows_done, n * STILES + (a - 1) * HT2)
                        act.activation(hh[a][:, t, :], inner[t % 4][:, 0:HALF], ACT.Relu).then_inc(inner_hi, 1)

                def expert(n, b, prepare):
                    relu_hi(n, 0)
                    relu_hi(n, 1)
                    if prepare:
                        tokens_hi(n + 1, 0)
                        weights_hi(n + 1, 1 - b)
                        tokens_hi(n + 1, 1)

                tokens_hi(0, 0)
                tokens_hi(0, 1)
                expert(0, 0, True)
                expert(1, 1, True)
                with act.Fori(1, E // 2 - 1) as step:
                    e = step * 2
                    expert(e, 0, True)
                    expert(e + 1, 1, True)
                expert(E - 2, 0, True)
                expert(E - 1, 1, False)

            @block.vector
            def _(dve):
                def weights_lo(n, b, second):
                    dve.wait_ge(w_hi, n * 2 + 1 + second)
                    if second:
                        dve.tensor_tensor(w2l[b], w2, words(w2h[b]), ALU.subtract).then_inc(w_lo, 1)
                    else:
                        dve.tensor_tensor(w1l[b], w1, words(w1h[b]), ALU.subtract).then_inc(w_lo, 1)

                def tokens_lo(n, a):
                    for c in range(CT):
                        dve.wait_ge(gt_hi, n * 4 + a * 2 + c + 1)
                        dve.tensor_tensor(gtl[:, a, c, :], turned[c][:, 0:HALF], gth[:, a, c, :].bitcast(F32),
                                          ALU.subtract).then_inc(gt_lo, 1)

                def relu_lo(n, a):
                    for t in range(ITILES):
                        dve.wait_ge(inner_hi, n * (2 * ITILES) + a * ITILES + t + 1)
                        dve.scalar_tensor_tensor(out=hl[a][:, t, :], in0=inner[t % 4][:, 0:HALF], scalar=0.0,
                                                 in1=words(hh[a][:, t, :]), op0=ALU.max,
                                                 op1=ALU.subtract).then_inc(inner_lo, 1)

                def take_rows(n, b, first, last):
                    for s in range(first, last):
                        dve.wait_ge(rows_done, n * STILES + s + 1)
                        need(dve, added, n * (16 * STILES) - 16 * STILES + 16 * STILES)
                        dve.tensor_scalar(y[:S, s, :], rows[s % 2][:S, 0:D], lists_sb[b][:S, s, 1:2], None,
                                          ALU.mult).then_inc(y_made, 1)

                def expert(n, b, prepare):
                    relu_lo(n, 0)
                    relu_lo(n, 1)
                    if prepare:
                        tokens_lo(n + 1, 0)
                    take_rows(n, b, 0, 2)
                    if prepare:
                        weights_lo(n + 1, 1 - b, 0)
                    take_rows(n, b, 2, 3)
                    if prepare:
                        weights_lo(n + 1, 1 - b, 1)
                        tokens_lo(n + 1, 1)
                    take_rows(n, b, 3, STILES)

                dve.tensor_tensor(w2l[0], w2, words(w2h[0]), ALU.subtract).then_inc(w_lo, 1)
                tokens_lo(0, 0)
                tokens_lo(0, 1)
                expert(0, 0, True)
                expert(1, 1, True)
                with dve.Fori(1, E // 2 - 1) as step:
                    e = step * 2
                    expert(e, 0, True)
                    expert(e + 1, 1, True)
                expert(E - 2, 0, True)
                expert(E - 1, 1, False)

            @block.tensor
            def _(pe):
                def turn(n, b, a):
                    for c in range(CT):
                        if c == 0:
                            pe.wait_ge(gathered[b][a], n * (4 * STILES) + (8 - 4 * b) * STILES)
                        need(pe, gt_lo, n * 4 + a * 2 + c - 1)
                        for s in range(HT2):
                            last = pe.transpose(turned[c][:, s * S:s * S + S],
                                                got[b][:S, a * HT2 + s, c * P:c * P + P], ident2[:S, :S])
                        last.then_inc(turned_done, 1)

                def first(n, b, a):
                    if a == 0:
                        pe.wait_ge(w_lo, n * 2 + 2)
                    pe.wait_ge(gt_lo, n * 4 + a * 2 + 2)
                    for t in range(ITILES):
                        need(pe, inner_lo, n * (2 * ITILES) + a * ITILES + t - 3)
                        k = 0
                        for c in range(CT):
                            for w_, g_ in ((w1h, gth), (w1h, gtl), (w1l, gth)):
                                last = pe.matmul(inner[t % 4][:, 0:HALF], w_[b][:, c, t * P:t * P + P], g_[:, a, c, :],
                                                 start=(k == 0), stop=(k == 3 * CT - 1))
                                k += 1
                        last.then_inc(inner_done, 1)

                def second(n, b, a):
                    for s in range(a * HT2, a * HT2 + HT2):
                        need(pe, y_made, n * STILES + s - 1)
                        if s == a * HT2:
                            pe.wait_ge(inner_lo, n * (2 * ITILES) + (a + 1) * ITILES)
                        at = (s - a * HT2) * S
                        k = 0
                        for t in range(ITILES):
                            for h_, w_ in ((hh[a], w2h), (hl[a], w2h), (hh[a], w2l)):
                                last = pe.matmul(rows[s % 2][:S, 0:D], h_[:, t, at:at + S], w_[b][:, t, :],
                                                 start=(k == 0), stop=(k == 3 * ITILES - 1))
                                k += 1
                        last.then_inc(rows_done, 1)

                pe.wait_ge(id_made, 2)
                turn(0, 0, 0)
                turn(0, 0, 1)

                def expert(n, b, prepare):
                    first(n, b, 0)
                    first(n, b, 1)
                    if prepare:
                        turn(n + 1, 1 - b, 0)
                    second(n, b, 0)
                    if prepare:
                        turn(n + 1, 1 - b, 1)
                    second(n, b, 1)

                expert(0, 0, True)
                expert(1, 1, True)
                with pe.Fori(1, E // 2 - 1) as step:
                    e = step * 2
                    expert(e, 0, True)
                    expert(e + 1, 1, True)
                expert(E - 2, 0, True)
                expert(E - 1, 1, False)


def kernel(x, L0_tok_W, L0_tok_b, L0_tok_gamma, L0_tok_beta, L0_attn_w_qkv, L0_attn_w_proj, L0_attn_b_proj,
           L0_ffn_W_router, L0_ffn_b_router, L0_ffn_experts_inter, L0_ffn_experts_out):
    import numpy as np
    import concourse.bacc as bacc
    from concourse.bass_utils import run_bass_kernel_spmd

    D = L0_tok_W.shape[1]
    mels = x.shape[1]
    taps = L0_tok_W.shape[0] // mels
    w_qkv = np.asarray(L0_attn_w_qkv)
    w_proj = np.asarray(L0_attn_w_proj)
    heads, hs = 16, D // 16
    wp_t = np.zeros((heads, 2 * hs, D), w_proj.dtype)
    wp_t[:, :hs, :] = w_proj.T.reshape(heads, hs, D)
    given = {
        "x": np.asarray(x),
        "tok_w": np.asarray(L0_tok_W).reshape(mels, taps, D),
        "tok_b": np.asarray(L0_tok_b).reshape(1, D),
        "gamma": np.asarray(L0_tok_gamma),
        "beta": np.asarray(L0_tok_beta),
        "wqk_t": np.ascontiguousarray(w_qkv[:2 * D].T),
        "wv_t": np.ascontiguousarray(w_qkv[2 * D:].T),
        "wp_t": wp_t.reshape(heads * 2 * hs, D),
        "b_proj": np.asarray(L0_attn_b_proj).reshape(1, D),
        "wr_t": np.ascontiguousarray(np.asarray(L0_ffn_W_router).T),
        "b_router": np.asarray(L0_ffn_b_router),
        "w_in": np.asarray(L0_ffn_experts_inter),
        "w_out": np.asarray(L0_ffn_experts_out),
    }
    batches, _, frames = given["x"].shape
    tokens = (frames - taps) // (taps // 2) + 1
    experts = given["w_in"].shape[0]
    nc = bacc.Bacc("TRN2", target_bir_lowering=False, num_devices=1)
    arrays = {f"in_{k}": np.ascontiguousarray(a) for k, a in given.items()}
    args = [nc.dram_tensor(k, a.shape, mybir.dt.from_np(a.dtype), kind="ExternalInput").ap() for k, a in arrays.items()]
    out = nc.dram_tensor("out", (batches * tokens, D), F32, kind="ExternalOutput").ap()
    tokens_dram = nc.dram_tensor("tokens", (batches * tokens, D), F32, kind="Internal").ap()
    table_dram = nc.dram_tensor("table", (experts * 8 * 117, 2), F32, kind="Internal").ap()
    audio_tower(nc, *args, out, tokens_dram, table_dram)
    r = run_bass_kernel_spmd(nc, [arrays], core_ids=[0])
    return r.results[0]["out"].reshape(batches, tokens, D)
```
